# Optimizing a Trainium2 kernel written in Bass

```python
import numpy as np
import jax
import jax.numpy as jnp

def _softmax(x, axis=-1):
    return jax.nn.softmax(x, axis=axis)

def _gelu(x):
    return jax.nn.gelu(x, approximate=True)

def _silu(x):
    return jax.nn.silu(x)

def _sigmoid(x):
    return jax.nn.sigmoid(x)

def _layernorm(x, axis=-1, eps=1e-05):
    m = jnp.mean(x, axis=axis, keepdims=True)
    v = jnp.var(x, axis=axis, keepdims=True)
    return (x - m) / jnp.sqrt(v + eps)

def _scatter_add(tgt, idx, src, axis=0):
    return tgt.at[idx].add(src)

def _segment_sum(src, seg, n):
    return jax.ops.segment_sum(src, seg, n)
kernel_name = 'mk_prb_d2_jaxref_r4_662963'

def setup_inputs(seed: int=0):
    np.random.seed(seed)
    _w = jnp.asarray

    def _L0_attn_setup():
        import jax, jax.numpy as jnp
        import numpy as np
        B, S, D = (2, 512, 256)
        H, DH = (16, 64)
        DQL, DKVL = (128, 128)
        DR = 64
        TOPK = 64
        LN_EPS = 1e-05
        ROPE_BASE = 10000.0

        def _rope_tables(seq_len, dim):
            inv_freq = 1.0 / ROPE_BASE ** (np.arange(0, dim, 2, dtype=np.float32) / dim)
            t = np.arange(seq_len, dtype=np.float32)
            freqs = np.outer(t, inv_freq)
            cos = np.concatenate([np.cos(freqs), np.cos(freqs)], -1)[:, ::2]
            sin = np.concatenate([np.sin(freqs), np.sin(freqs)], -1)[:, ::2]
            return (jnp.asarray(cos), jnp.asarray(sin))

        def _apply_rope_subspace(x, d_rope):
            s = x.shape[-2]
            cos, sin = _rope_tables(s, d_rope)
            xr, xp = (x[..., :d_rope], x[..., d_rope:])
            e, o = (xr[..., 0::2], xr[..., 1::2])
            rot = jnp.stack([e * cos - o * sin, e * sin + o * cos], axis=-1).reshape(xr.shape)
            return jnp.concatenate([rot, xp], axis=-1)

        def _reference_tuple_inner(x, w_down_q, w_down_kv, w_up_q, w_up_k, w_up_v, w_out, ln_scale, ln_bias):
            b, s, d = x.shape
            residual = x
            mu = jnp.mean(x, axis=-1, keepdims=True)
            var = jnp.mean((x - mu) ** 2, axis=-1, keepdims=True)
            h = (x - mu) * jax.lax.rsqrt(var + LN_EPS) * ln_scale + ln_bias
            c_q = h @ w_down_q.T
            c_kv = h @ w_down_kv.T
            q = (c_q @ w_up_q.T).reshape(b, s, H, DH).transpose(0, 2, 1, 3)
            k = (c_kv @ w_up_k.T).reshape(b, s, H, DH).transpose(0, 2, 1, 3)
            v = (c_kv @ w_up_v.T).reshape(b, s, H, DH).transpose(0, 2, 1, 3)
            q = _apply_rope_subspace(q, DR)
            k = _apply_rope_subspace(k, DR)
            scale = 1.0 / np.sqrt(DH).astype(np.float32)
            scores = jnp.einsum('bhqd,bhkd->bhqk', q, k) * scale
            _, indices = jax.lax.top_k(scores, min(TOPK, s))
            attn = jax.nn.softmax(scores, axis=-1)
            out = jnp.einsum('bhqk,bhkd->bhqd', attn, v)
            out = out.transpose(0, 2, 1, 3).reshape(b, s, H * DH)
            out = out @ w_out.T + residual
            return (out, indices.astype(jnp.int64))
        key = jax.random.key(seed)
        ks = jax.random.split(key, 7)
        init = lambda k, shape: jax.random.normal(k, shape, jnp.float32) * 0.02
        return {'x': jax.random.normal(ks[0], (B, S, D), jnp.float32), 'w_down_q': init(ks[1], (DQL, D)), 'w_down_kv': init(ks[2], (DKVL, D)), 'w_up_q': init(ks[3], (H * DH, DQL)), 'w_up_k': init(ks[4], (H * DH, DKVL)), 'w_up_v': init(ks[5], (H * DH, DKVL)), 'w_out': init(ks[6], (D, H * DH)), 'ln_scale': jnp.ones((D,), jnp.float32), 'ln_bias': jnp.zeros((D,), jnp.float32)}
    _L0_attn_in = _L0_attn_setup()

    def _L0_ffn_setup():
        import jax, jax.numpy as jnp
        import numpy as np

        def _binarize(w):
            alpha = jax.lax.stop_gradient(jnp.mean(jnp.abs(w), axis=1, keepdims=True))
            bw = alpha * jnp.sign(w)
            return w + jax.lax.stop_gradient(bw - w)
        key = jax.random.key(seed)
        k1, k2, k3, k4, k5 = jax.random.split(key, 5)
        D, H = (256, 1024)
        x = jax.random.normal(k1, (64, 196, D), dtype=jnp.float32)
        w1 = jax.random.normal(k2, (H, D), dtype=jnp.float32) * 0.02
        b1 = jax.random.normal(k3, (H,), dtype=jnp.float32) * 0.02
        w2 = jax.random.normal(k4, (D, H), dtype=jnp.float32) * 0.02
        b2 = jax.random.normal(k5, (D,), dtype=jnp.float32) * 0.02
        return {'x': x, 'w1': w1, 'b1': b1, 'w2': w2, 'b2': b2}
    _L0_ffn_in = _L0_ffn_setup()

    def _L1_attn_setup():
        import jax, jax.numpy as jnp
        import numpy as np
        NUM_HEADS = 16
        HIDDEN = 256
        HEAD_DIM = HIDDEN // NUM_HEADS
        B, L = (2, 512)
        key = jax.random.key(seed)
        ks = jax.random.split(key, 5)
        scale = 1.0 / np.sqrt(HIDDEN)
        return {'x': jax.random.normal(ks[0], (B, L, HIDDEN), dtype=jnp.float32), 'Wq': jax.random.normal(ks[1], (HIDDEN, HIDDEN), dtype=jnp.float32) * scale, 'Wk': jax.random.normal(ks[2], (HIDDEN, HIDDEN), dtype=jnp.float32) * scale, 'Wv': jax.random.normal(ks[3], (HIDDEN, HIDDEN), dtype=jnp.float32) * scale, 'Wo': jax.random.normal(ks[4], (HIDDEN, HIDDEN), dtype=jnp.float32) * scale}
    _L1_attn_in = _L1_attn_setup()

    def _L1_ffn_setup():
        import jax, jax.numpy as jnp
        import numpy as np
        D = 256
        FF = 4 * D
        E = 8
        TOP_K = 2
        B, S = (4, 1024)
        key = jax.random.key(seed)
        ks = jax.random.split(key, 8)
        x = jax.random.normal(ks[0], (B, S, D), dtype=jnp.float32)
        Wg = jax.random.normal(ks[1], (D, E), dtype=jnp.float32) * 0.02
        bg = jnp.zeros((E,), dtype=jnp.float32)
        W1 = jax.random.normal(ks[2], (E, D, FF), dtype=jnp.float32) * 0.02
        b1 = jnp.zeros((E, FF), dtype=jnp.float32)
        W2 = jax.random.normal(ks[3], (E, FF, D), dtype=jnp.float32) * 0.02
        b2 = jnp.zeros((E, D), dtype=jnp.float32)
        return {'x': x, 'Wg': Wg, 'bg': bg, 'W1': W1, 'b1': b1, 'W2': W2, 'b2': b2}
    _L1_ffn_in = _L1_ffn_setup()
    _d = {'L0_attn_x': _L0_attn_in['x'], 'L0_attn_w_down_q': _L0_attn_in['w_down_q'], 'L0_attn_w_down_kv': _L0_attn_in['w_down_kv'], 'L0_attn_w_up_q': _L0_attn_in['w_up_q'], 'L0_attn_w_up_k': _L0_attn_in['w_up_k'], 'L0_attn_w_up_v': _L0_attn_in['w_up_v'], 'L0_attn_w_out': _L0_attn_in['w_out'], 'L0_attn_ln_scale': _L0_attn_in['ln_scale'], 'L0_attn_ln_bias': _L0_attn_in['ln_bias'], 'L0_ffn_w1': _L0_ffn_in['w1'], 'L0_ffn_b1': _L0_ffn_in['b1'], 'L0_ffn_w2': _L0_ffn_in['w2'], 'L0_ffn_b2': _L0_ffn_in['b2'], 'L1_attn_Wq': _L1_attn_in['Wq'], 'L1_attn_Wk': _L1_attn_in['Wk'], 'L1_attn_Wv': _L1_attn_in['Wv'], 'L1_attn_Wo': _L1_attn_in['Wo'], 'L1_ffn_Wg': _L1_ffn_in['Wg'], 'L1_ffn_bg': _L1_ffn_in['bg'], 'L1_ffn_W1': _L1_ffn_in['W1'], 'L1_ffn_b1': _L1_ffn_in['b1'], 'L1_ffn_W2': _L1_ffn_in['W2'], 'L1_ffn_b2': _L1_ffn_in['b2']}
    _x0 = _d['L0_attn_x']
    _d['L0_attn_x'] = jax.random.normal(jax.random.fold_in(jax.random.key(seed), 1), (8, 512, 256), dtype=_x0.dtype)
    del _x0
    return _d

def reference(L0_attn_x, L0_attn_w_down_q, L0_attn_w_down_kv, L0_attn_w_up_q, L0_attn_w_up_k, L0_attn_w_up_v, L0_attn_w_out, L0_attn_ln_scale, L0_attn_ln_bias, L0_ffn_w1, L0_ffn_b1, L0_ffn_w2, L0_ffn_b2, L1_attn_Wq, L1_attn_Wk, L1_attn_Wv, L1_attn_Wo, L1_ffn_Wg, L1_ffn_bg, L1_ffn_W1, L1_ffn_b1, L1_ffn_W2, L1_ffn_b2):

    def _L0_attn_ref(x, w_down_q, w_down_kv, w_up_q, w_up_k, w_up_v, w_out, ln_scale, ln_bias):
        import jax, jax.numpy as jnp
        import numpy as np
        B, S, D = (2, 512, 256)
        H, DH = (16, 64)
        DQL, DKVL = (128, 128)
        DR = 64
        TOPK = 64
        LN_EPS = 1e-05
        ROPE_BASE = 10000.0

        def _rope_tables(seq_len, dim):
            inv_freq = 1.0 / ROPE_BASE ** (np.arange(0, dim, 2, dtype=np.float32) / dim)
            t = np.arange(seq_len, dtype=np.float32)
            freqs = np.outer(t, inv_freq)
            cos = np.concatenate([np.cos(freqs), np.cos(freqs)], -1)[:, ::2]
            sin = np.concatenate([np.sin(freqs), np.sin(freqs)], -1)[:, ::2]
            return (jnp.asarray(cos), jnp.asarray(sin))

        def _apply_rope_subspace(x, d_rope):
            s = x.shape[-2]
            cos, sin = _rope_tables(s, d_rope)
            xr, xp = (x[..., :d_rope], x[..., d_rope:])
            e, o = (xr[..., 0::2], xr[..., 1::2])
            rot = jnp.stack([e * cos - o * sin, e * sin + o * cos], axis=-1).reshape(xr.shape)
            return jnp.concatenate([rot, xp], axis=-1)

        def _reference_tuple_inner(x, w_down_q, w_down_kv, w_up_q, w_up_k, w_up_v, w_out, ln_scale, ln_bias):
            b, s, d = x.shape
            residual = x
            mu = jnp.mean(x, axis=-1, keepdims=True)
            var = jnp.mean((x - mu) ** 2, axis=-1, keepdims=True)
            h = (x - mu) * jax.lax.rsqrt(var + LN_EPS) * ln_scale + ln_bias
            c_q = h @ w_down_q.T
            c_kv = h @ w_down_kv.T
            q = (c_q @ w_up_q.T).reshape(b, s, H, DH).transpose(0, 2, 1, 3)
            k = (c_kv @ w_up_k.T).reshape(b, s, H, DH).transpose(0, 2, 1, 3)
            v = (c_kv @ w_up_v.T).reshape(b, s, H, DH).transpose(0, 2, 1, 3)
            q = _apply_rope_subspace(q, DR)
            k = _apply_rope_subspace(k, DR)
            scale = 1.0 / np.sqrt(DH).astype(np.float32)
            scores = jnp.einsum('bhqd,bhkd->bhqk', q, k) * scale
            _, indices = jax.lax.top_k(scores, min(TOPK, s))
            attn = jax.nn.softmax(scores, axis=-1)
            out = jnp.einsum('bhqk,bhkd->bhqd', attn, v)
            out = out.transpose(0, 2, 1, 3).reshape(b, s, H * DH)
            out = out @ w_out.T + residual
            return (out, indices.astype(jnp.int64))
        return _reference_tuple_inner(x, w_down_q, w_down_kv, w_up_q, w_up_k, w_up_v, w_out, ln_scale, ln_bias)[0]

    def _L0_ffn_ref(x, w1, b1, w2, b2):
        import jax, jax.numpy as jnp
        import numpy as np

        def _binarize(w):
            alpha = jax.lax.stop_gradient(jnp.mean(jnp.abs(w), axis=1, keepdims=True))
            bw = alpha * jnp.sign(w)
            return w + jax.lax.stop_gradient(bw - w)
        bw1 = _binarize(w1)
        h = jnp.einsum('bsd,hd->bsh', x, bw1) + b1
        h = jax.nn.gelu(h, approximate=False)
        bw2 = _binarize(w2)
        out = jnp.einsum('bsh,dh->bsd', h, bw2) + b2
        return out

    def _L1_attn_ref(x, Wq, Wk, Wv, Wo):
        import jax, jax.numpy as jnp
        import numpy as np
        NUM_HEADS = 16
        HIDDEN = 256
        HEAD_DIM = HIDDEN // NUM_HEADS
        B, L = (2, 512)
        b, l, _ = x.shape
        q = (x @ Wq.T).reshape(b, l, NUM_HEADS, HEAD_DIM)
        k = (x @ Wk.T).reshape(b, l, NUM_HEADS, HEAD_DIM)
        v = (x @ Wv.T).reshape(b, l, NUM_HEADS, HEAD_DIM)
        q = jax.nn.elu(q) + 1.0
        k = jax.nn.elu(k) + 1.0
        kv = jnp.einsum('blhd,blhe->blhde', k, v)
        kv_cumsum = jnp.cumsum(kv, axis=1)
        k_cumsum = jnp.cumsum(k, axis=1)
        out = jnp.einsum('blhd,blhde->blhe', q, kv_cumsum)
        normalizer = jnp.clip(jnp.einsum('blhd,blhd->blh', q, k_cumsum), 1e-06, None)
        out = out / normalizer[..., None]
        out = out.reshape(b, l, HIDDEN)
        return out @ Wo.T

    def _L1_ffn_ref(x, Wg, bg, W1, b1, W2, b2):
        import jax, jax.numpy as jnp
        import numpy as np
        D = 256
        FF = 4 * D
        E = 8
        TOP_K = 2
        B, S = (4, 1024)
        b, s, d = x.shape
        xt = x.reshape(b * s, d)
        gate = jax.nn.softmax(xt @ Wg + bg, axis=-1)
        _, idx = jax.lax.top_k(gate, TOP_K)
        sel = jax.nn.one_hot(idx, E, dtype=jnp.float32).sum(axis=1) > 0
        sel = sel.astype(x.dtype)
        out = jnp.zeros_like(xt)
        for e in range(E):
            h = jax.nn.relu(xt @ W1[e] + b1[e])
            y = h @ W2[e] + b2[e]
            out = out + sel[:, e:e + 1] * y
        return out.reshape(b, s, d)
    x = L0_attn_x
    xn = _layernorm(x, axis=-1)
    x = x + _L0_attn_ref(xn, L0_attn_w_down_q, L0_attn_w_down_kv, L0_attn_w_up_q, L0_attn_w_up_k, L0_attn_w_up_v, L0_attn_w_out, L0_attn_ln_scale, L0_attn_ln_bias) + _L0_ffn_ref(xn, L0_ffn_w1, L0_ffn_b1, L0_ffn_w2, L0_ffn_b2)
    xn = _layernorm(x, axis=-1)
    x = x + _L1_attn_ref(xn, L1_attn_Wq, L1_attn_Wk, L1_attn_Wv, L1_attn_Wo) + _L1_ffn_ref(xn, L1_ffn_Wg, L1_ffn_bg, L1_ffn_W1, L1_ffn_b1, L1_ffn_W2, L1_ffn_b2)
    return x

_drawn_inputs = setup_inputs


def setup_inputs(seed=0):
    import zlib

    import numpy as np

    out = dict(_drawn_inputs(seed))
    spreads = {'L0_attn_ln_scale': (1.0, 0.6),
     'L0_attn_ln_bias': (0.0, 0.8),
     'L1_ffn_bg': (0.0, 0.8),
     'L1_ffn_b1': (0.0, 0.8),
     'L1_ffn_b2': (0.0, 2.0)}
    factors = {'L0_attn_w_down_q': 8.0,
     'L0_attn_w_down_kv': 8.0,
     'L0_attn_w_up_q': 8.0,
     'L0_attn_w_up_k': 8.0,
     'L0_attn_w_up_v': 8.0,
     'L0_attn_w_out': 8.0,
     'L0_ffn_b1': 64.0,
     'L0_ffn_b2': 31.264,
     'L1_attn_Wq': 200.0,
     'L1_attn_Wk': 114.746,
     'L0_ffn_w1': 8.0,
     'L0_ffn_w2': 8.0,
     'L1_attn_Wv': 3.616,
     'L1_attn_Wo': 3.277,
     'L1_ffn_Wg': 8.0,
     'L1_ffn_W1': 8.0,
     'L1_ffn_W2': 8.0}
    for name, (base, spread) in spreads.items():
        noise = np.random.default_rng([zlib.crc32(name.encode()), seed]).standard_normal(out[name].shape)
        drawn = base * np.exp(spread * noise) if base else spread * noise
        out[name] = jnp.asarray(drawn.astype(out[name].dtype))
    for name, factor in factors.items():
        out[name] = (out[name] * factor).astype(out[name].dtype)
    return out
```

```python
from contextlib import ExitStack

import numpy as np

import concourse.bass as bass
from concourse import mybir

F32 = mybir.dt.float32
F32R = mybir.dt.float32r
ALU = mybir.AluOpType
ACT = mybir.ActivationFunctionType
AX = mybir.AxisListType

P = 128
B, S, D = 8, 512, 256
T = B * S
NT = S // P
KC = D // P
H0, DH = 16, 64
NP = H0 // 2
FF = 1024
MC = FF // P
H1, DE = 16, 16
NE = 8
TT = T // P
TILE = 512
TILES = 2 * T // TILE + NE
MAX_TRIPS = T // TILE
ZERO_W = 2048
EPS = 1e-5
SCALE = 1.0 / 8.0
WORKERS = 4
PE, DVE, ACTE, POOL = range(WORKERS)


class Stage:

    def __init__(self, nc, ctx, name):
        self.nc, self.ctx, self.name = nc, ctx, name
        self.cleared = []
        self.arrived = self.lasting("arrived")
        self.go = [self.lasting(f"go{i}") for i in range(WORKERS)]

    def sb(self, name, shape, dt=F32):
        return self.ctx.enter_context(self.nc.sbuf_tensor(f"{self.name}_{name}", shape, dt))

    def bank(self, name, shape=(P, 512)):
        return self.ctx.enter_context(self.nc.psum_tensor(f"{self.name}_{name}", list(shape), F32))

    def lasting(self, name):
        return self.ctx.enter_context(self.nc.semaphore(f"{self.name}_{name}"))

    def sem(self, name):
        s = self.lasting(name)
        self.cleared.append(s)
        return s

    def meet(self, eng, worker):
        eng.sem_inc(self.arrived, 1)
        eng.wait_ge(self.go[worker], 1)
        eng.sem_clear(self.go[worker])

    def lead(self, eng):
        eng.wait_ge(self.arrived, WORKERS)
        for s in self.cleared:
            eng.sem_clear(s)
        eng.sem_clear(self.arrived)
        for go in self.go:
            eng.sem_inc(go, 1)


def product(nc, out, l_hi, l_lo, r_hi, r_lo, start, stop, **kw):
    nc.tensor.matmul(out, l_lo, r_hi, start=start, stop=False, **kw)
    nc.tensor.matmul(out, l_hi, r_lo, start=False, stop=False, **kw)
    return nc.tensor.matmul(out, l_hi, r_hi, start=False, stop=stop, **kw)


def layer_norm(nc, dve, x, out, stats, mean_var, var_eps, std, rstd, shift, ready, done, root_done):
    sem, n = done
    tiles = x.shape[1]
    for t in range(tiles):
        nc.vector.bn_stats(stats[:, t, :], x[:, t, :]).then_inc(sem, 1)
    dve.wait_ge(sem, n + tiles)
    for t in range(tiles):
        nc.vector.bn_aggr(mean_var[:, t, :], stats[:, t, :]).then_inc(sem, 1)
    dve.wait_ge(sem, n + 2 * tiles)
    nc.vector.tensor_scalar(var_eps, mean_var[:, :, 1], EPS, None, ALU.add).then_inc(sem, 1)
    dve.wait_ge(*root_done)
    nc.vector.reciprocal(rstd, std).then_inc(sem, 1)
    dve.wait_ge(sem, n + 2 * tiles + 2)
    nc.vector.scalar_tensor_tensor(out=shift, in0=mean_var[:, :, 0], scalar=-1.0, in1=rstd,
                                   op0=ALU.mult, op1=ALU.mult).then_inc(sem, 1)
    dve.wait_ge(sem, n + 2 * tiles + 3)
    for t in range(tiles):
        nc.vector.tensor_scalar(out[:, t, :], x[:, t, :], rstd[:, t:t + 1], shift[:, t:t + 1],
                                ALU.mult, ALU.add).then_inc(sem, 1)
    return n + 3 * tiles + 3


LN_VAR = 2 * NT + 1
LN_ALL = 3 * NT + 3


def tokens(ap, b):
    return ap[bass.ds(b * S, S), :].rearrange("(t p) d -> p t d", p=P)


def stage_f(nc, x, w1_rows, w1_t, w2_t, b1, b2, ident_d, part, rows, results):
    with ExitStack() as ctx:
        st = Stage(nc, ctx, "f")
        sb, bank, sem = st.sb, st.bank, st.sem
        ident = sb("ident", [P, P])
        ones = sb("ones", [P, P])
        zero = sb("zero", [P, ZERO_W])
        b1_c = sb("b1_c", [P, MC])
        b2_row = sb("b2_row", [P, D])
        alpha1 = sb("alpha1", [P, MC])
        alpha2 = sb("alpha2", [P, 2, D])
        sign1 = sb("sign1", [P, KC, FF], F32R)
        sign2 = sb("sign2", [P, MC, D], F32R)
        w1r = sb("w1r", [P, MC, D])
        w1s = sb("w1s", [P, KC, FF])
        w2s = sb("w2s", [P, MC, D])
        w2abs = sb("w2abs", [P, MC, D])

        x_t = sb("x_t", [P, NT, D])
        xn = sb("xn", [P, NT, D])
        base = sb("base", [P, NT, D])
        y = sb("y", [P, NT, D])
        out = sb("out", [P, NT, D])
        stats = sb("stats", [P, NT, 6])
        mean_var = sb("mean_var", [P, NT, 2])
        small = sb("small", [P, 4, NT])
        xT_hi = sb("xT_hi", [P, KC, S], F32R)
        xT_lo = sb("xT_lo", [P, KC, S], F32R)
        g = sb("g", [P, MC, S])
        g_hi = sb("g_hi", [P, MC, S], F32R)
        g_lo = sb("g_lo", [P, MC, S], F32R)

        pX = [bank(f"pX{c}") for c in range(KC)]
        pU = [bank(f"pU{i}") for i in range(3)]
        pY = [bank(f"pY{i}", (P, 2, D)) for i in range(2)]

        loaded = st.lasting("loaded")
        ones_set = st.lasting("ones_set")
        zero_set = st.lasting("zero_set")
        zeroed = st.lasting("zeroed")
        signs_done = st.lasting("signs_done")
        alpha1_done = st.lasting("alpha1_done")
        sums_done = st.lasting("sums_done")
        alpha2_done = st.lasting("alpha2_done")

        x_in = sem("x_in")
        ln_step = sem("ln_step")
        root = sem("root")
        xT_done = sem("xT_done")
        xT_hi_done = sem("xT_hi_done")
        xT_lo_done = sem("xT_lo_done")
        up_done = sem("up_done")
        gelu_done = sem("gelu_done")
        g_lo_done = sem("g_lo_done")
        down_done = sem("down_done")
        base_done = sem("base_done")
        y_done = sem("y_done")
        out_done = sem("out_done")
        stored = sem("stored")

        with nc.Block() as block:
            @block.sync
            def _(sp):
                sp.dma_start(ident[:], ident_d).then_inc(loaded, 16)
                sp.dma_start(w1r[:], w1_rows.rearrange("(m p) d -> p m d", p=P)).then_inc(loaded, 16)
                sp.dma_start(w1s[:], w1_t.rearrange("(c p) f -> p c f", p=P)).then_inc(loaded, 16)
                sp.dma_start(w2s[:], w2_t.rearrange("(m p) d -> p m d", p=P)).then_inc(loaded, 16)
                sp.dma_start(b1_c[:], b1).then_inc(loaded, 16)
                sp.dma_start(b2_row[:], b2).then_inc(loaded, 16)
                with sp.Fori(0, B) as b:
                    sp.dma_start(x_t[:], tokens(x, b)).then_inc(x_in, 16)
                    sp.wait_ge(out_done, 2)
                    sp.dma_start(tokens(part, b), out[:]).then_inc(stored, 16)
                    sp.wait_ge(stored, 16)
                    st.lead(sp)

            @block.gpsimd
            def _(pool):
                nc.gpsimd.memset(ones[:], 1.0).then_inc(ones_set, 1)
                nc.gpsimd.memset(zero[:], 0.0).then_inc(zero_set, 1)
                pool.wait_ge(zero_set, 1)
                width = TILES * TILE * D // P
                for buf in (rows, results):
                    flat = buf.rearrange("(p r) d -> p (r d)", p=P)
                    for i in range(width // ZERO_W):
                        pool.dma_start(flat[:, i * ZERO_W:(i + 1) * ZERO_W], zero[:]).then_inc(zeroed, 16)
                pool.wait_ge(loaded, 96)
                with pool.Fori(0, B) as b:
                    pool.wait_ge(ln_step, LN_ALL)
                    nc.gpsimd.tensor_tensor(base[:], x_t[:], xn[:], ALU.add).then_inc(base_done, 1)
                    pool.wait_ge(base_done, 1)
                    for t in range(NT):
                        nc.gpsimd.tensor_tensor(base[:, t, :], base[:, t, :], b2_row[:],
                                                ALU.add).then_inc(base_done, 1)
                    pool.wait_ge(base_done, 1 + NT)
                    st.meet(pool, POOL)
                pool.wait_ge(zeroed, 16 * 2 * (width // ZERO_W))

            @block.scalar
            def _(act):
                act.wait_ge(loaded, 96)
                nc.scalar.activation(sign1[:], w1s[:], ACT.Sign).then_inc(signs_done, 1)
                nc.scalar.activation(sign2[:], w2s[:], ACT.Sign).then_inc(signs_done, 1)
                nc.scalar.activation(w2abs[:], w2s[:], ACT.Abs).then_inc(signs_done, 1)
                act.wait_ge(alpha1_done, 3)
                with act.Fori(0, B) as b:
                    act.wait_ge(ln_step, LN_VAR)
                    nc.scalar.activation(small[:, 1, :], small[:, 0, :], ACT.Sqrt).then_inc(root, 1)
                    for c in range(KC):
                        act.wait_ge(xT_done, c + 1)
                        nc.scalar.copy(xT_hi[:, c, :], pX[c][:]).then_inc(xT_hi_done, 1)
                    for m in range(MC):
                        act.wait_ge(up_done, m + 1)
                        for dst in (g, g_hi):
                            nc.scalar.activation(dst[:, m, :], pU[m % 3][:], ACT.Gelu, bias=b1_c[:, m:m + 1],
                                                 scale=alpha1[:, m:m + 1]).then_inc(gelu_done, 1)
                    act.wait_ge(gelu_done, 2 * MC)
                    st.meet(act, ACTE)

            @block.vector
            def _(dve):
                dve.wait_ge(loaded, 96)
                nc.vector.tensor_reduce(alpha1[:], w1r[:], AX.X, ALU.add,
                                        apply_absolute_value=True).then_inc(alpha1_done, 1)
                dve.wait_ge(alpha1_done, 1)
                nc.vector.tensor_scalar(alpha1[:], alpha1[:], 1.0 / D, None, ALU.mult).then_inc(alpha1_done, 2)
                dve.wait_ge(sums_done, 1)
                for i in range(2):
                    nc.vector.tensor_scalar(alpha2[:, i, :], pY[0][:, 0, :], 1.0 / FF, None,
                                            ALU.mult).then_inc(alpha2_done, 1)
                dve.wait_ge(alpha2_done, 2)
                with dve.Fori(0, B) as b:
                    dve.wait_ge(x_in, 16)
                    layer_norm(nc, dve, x_t, xn, stats, mean_var, small[:, 0, :], small[:, 1, :],
                               small[:, 2, :], small[:, 3, :], None, (ln_step, 0), (root, 1))
                    for c in range(KC):
                        dve.wait_ge(xT_hi_done, c + 1)
                        nc.vector.tensor_tensor(xT_lo[:, c, :], pX[c][:], xT_hi[:, c, :],
                                                ALU.subtract).then_inc(xT_lo_done, 1)
                    for m in range(MC):
                        dve.wait_ge(gelu_done, 2 * m + 2)
                        nc.vector.tensor_tensor(g_lo[:, m, :], g[:, m, :], g_hi[:, m, :],
                                                ALU.subtract).then_inc(g_lo_done, 1)
                    for i in range(2):
                        dve.wait_ge(down_done, i + 1)
                        nc.vector.tensor_tensor(y[:, 2 * i:2 * i + 2, :], pY[i][:], alpha2[:],
                                                ALU.mult).then_inc(y_done, 1)
                    dve.wait_ge(base_done, 1 + NT)
                    for i in range(2):
                        dve.wait_ge(y_done, i + 1)
                        nc.vector.tensor_tensor(out[:, 2 * i:2 * i + 2, :], y[:, 2 * i:2 * i + 2, :],
                                                base[:, 2 * i:2 * i + 2, :], ALU.add).then_inc(out_done, 1)
                    dve.wait_ge(out_done, 2)
                    st.meet(dve, DVE)

            @block.tensor
            def _(pe):
                pe.wait_ge(ones_set, 1)
                pe.wait_ge(signs_done, 3)
                for m in range(MC):
                    last = nc.tensor.matmul(pY[0][:, 0, :], ones[:], w2abs[:, m, :],
                                            start=(m == 0), stop=(m == MC - 1))
                last.then_inc(sums_done, 1)
                pe.wait_ge(alpha2_done, 2)
                with pe.Fori(0, B) as b:
                    pe.wait_ge(ln_step, LN_ALL)
                    for c in range(KC):
                        for t in range(NT):
                            last = nc.tensor.transpose(pX[c][:, t * P:(t + 1) * P],
                                                       xn[:, t, c * P:(c + 1) * P], ident[:])
                        last.then_inc(xT_done, 1)
                    pe.wait_ge(xT_lo_done, KC)
                    for m in range(MC):
                        if m >= 3:
                            pe.wait_ge(gelu_done, 2 * (m - 2))
                        for c in range(KC):
                            w = sign1[:, c, m * P:(m + 1) * P]
                            nc.tensor.matmul(pU[m % 3][:], w, xT_lo[:, c, :], start=(c == 0), stop=False)
                            last = nc.tensor.matmul(pU[m % 3][:], w, xT_hi[:, c, :], start=False,
                                                    stop=(c == KC - 1))
                        last.then_inc(up_done, 1)
                    for t in range(NT):
                        for m in range(MC):
                            if t == 0:
                                pe.wait_ge(g_lo_done, m + 1)
                            for part_ in (g_lo, g_hi):
                                last = nc.tensor.matmul(pY[t // 2][:, t % 2, :], part_[:, m, t * P:(t + 1) * P],
                                                        sign2[:, m, :], start=(m == 0 and part_ is g_lo),
                                                        stop=(m == MC - 1 and part_ is g_hi))
                        if t % 2:
                            last.then_inc(down_done, 1)
                    pe.wait_ge(down_done, 2)
                    st.meet(pe, PE)


WQK = 192 * NP


def stage_a(nc, x, wd_t, wq_t, wk_t, wv_t, wo_t, ln_sb, rope_c, rope_s, own_d, ident_d, part, x1):
    with ExitStack() as ctx:
        st = Stage(nc, ctx, "a")
        sb, bank, sem = st.sb, st.bank, st.sem
        ident = sb("ident", [P, P])
        ones = sb("ones", [P, P], F32R)
        ln = sb("ln", [P, 2, KC])
        cos = sb("cos", [P, S])
        sin = sb("sin", [P, S])
        names = {"d": (wd_t, KC * 2 * P), "q": (wq_t, WQK), "k": (wk_t, WQK), "v": (wv_t, H0 * DH),
                 "o": (wo_t, NP * D)}
        w_hi = {n: sb(f"w{n}_hi", [P, f], F32R) for n, (_, f) in names.items()}
        w_lo = {n: sb(f"w{n}_lo", [P, f], F32R) for n, (_, f) in names.items()}
        v_hi = sb("v_hi", [P, NT, NP, 3, DH], F32R)
        v_lo = sb("v_lo", [P, NT, NP, 3, DH], F32R)
        own = sb("own", [P, 2])
        q_hi = sb("q_hi", [P, 2, 2, S], F32R)
        q_lo = sb("q_lo", [P, 2, 2, S], F32R)

        loaded = st.lasting("loaded")
        w_split = st.lasting("w_split")
        w_lo_done = st.lasting("w_lo_done")
        fills = st.lasting("fills")
        x_in = sem("x_in")
        ln_step = sem("ln_step")
        root = sem("root")
        hT_done = sem("hT_done")
        hT_f_done = sem("hT_f_done")
        hT_split = sem("hT_split")
        c_done = sem("c_done")
        c_hi_done = sem("c_hi_done")
        c_lo_done = sem("c_lo_done")
        v_done = sem("v_done")
        v_hi_done = sem("v_hi_done")
        v_lo_done = sem("v_lo_done")
        pj_done = sem("pj_done")
        rot_mul = sem("rot_mul")
        rot_add = sem("rot_add")
        qk_hi_done = sem("qk_hi_done")
        qk_lo_done = sem("qk_lo_done")
        s_done = sem("s_done")
        max_done = sem("max_done")
        diag_done = sem("diag_done")
        st_done = sem("st_done")
        exp_done = sem("exp_done")
        p_lo_done = sem("p_lo_done")
        pv_done = sem("pv_done")
        inv_done = sem("inv_done")
        norm_done = sem("norm_done")
        att_split = sem("att_split")
        o_done = sem("o_done")
        part_in = sem("part_in")
        out_done = sem("out_done")
        stored = sem("stored")

        with ExitStack() as ctx2:
            raw = {n: ctx2.enter_context(nc.sbuf_tensor(f"a_raw_{n}", [P, f], F32)) for n, (_, f) in names.items()}
            with nc.Block() as block:
                @block.sync
                def _(sp):
                    for n, (src, _) in names.items():
                        sp.dma_start(raw[n][:], src).then_inc(loaded, 16)
                    for dst, src in ((ident, ident_d), (cos, rope_c), (sin, rope_s), (own, own_d)):
                        sp.dma_start(dst[:], src).then_inc(loaded, 16)
                    sp.dma_start(ln[:], ln_sb).then_inc(loaded, 16)

                @block.scalar
                def _(act):
                    act.wait_ge(loaded, 16 * (len(names) + 5))
                    for n in names:
                        nc.scalar.copy(w_hi[n][:], raw[n][:]).then_inc(w_split, 1)

                @block.vector
                def _(dve):
                    for i, n in enumerate(names):
                        dve.wait_ge(w_split, i + 1)
                        nc.vector.tensor_tensor(w_lo[n][:], raw[n][:], w_hi[n][:],
                                                ALU.subtract).then_inc(w_lo_done, 1)
                    dve.wait_ge(w_lo_done, len(names))

                @block.gpsimd
                def _(pool):
                    nc.gpsimd.memset(ones[:].bitcast(F32), 1.0).then_inc(fills, 1)
                    nc.gpsimd.memset(v_hi[:, :, :, 1, :].bitcast(F32), 1.0).then_inc(fills, 1)
                    nc.gpsimd.memset(v_lo[:, :, :, 1, :].bitcast(F32), 0.0).then_inc(fills, 1)
                    pool.wait_ge(fills, 3)

        x_t = sb("x_t", [P, NT, D])
        h0 = sb("h0", [P, NT, D])
        stats = sb("stats", [P, NT, 6])
        mean_var = sb("mean_var", [P, NT, 2])
        small = sb("small", [P, 4, NT])
        c_hi = sb("c_hi", [P, 2, S], F32R)
        c_lo = sb("c_lo", [P, 2, S], F32R)
        rot = sb("rot", [P, 3, S])
        k_hi = sb("k_hi", [P, 2, S], F32R)
        k_lo = sb("k_lo", [P, 2, S], F32R)
        row_max = sb("row_max", [P, H0, NT])
        diag = sb("diag", [P, 2, NT, P], F32R)
        pr = sb("pr", [P, 1, S])
        pr_hi = sb("pr_hi", [P, 3, S], F32R)
        pr_lo = sb("pr_lo", [P, 3, S], F32R)
        hT, hT_hi, hT_lo = rot[:, 0:KC, :], pr_hi[:, 0:KC, :], pr_lo[:, 0:KC, :]
        inv = sb("inv", [P, S])
        att = sb("att", [P, S])
        att_hi = sb("att_hi", [P, NP, S], F32R)
        att_lo = sb("att_lo", [P, NP, S], F32R)

        pG = [bank(f"pG{i}") for i in range(2)]
        pM = [bank(f"pM{i}") for i in range(2)]
        pT = [bank(f"pT{i}") for i in range(2)]
        pA = [bank(f"pA{i}") for i in range(2)]

        J = H0 * NT
        PR = 3

        def head_cols(w, p, swapped):
            return w[:, 192 * p + 64 * swapped:192 * p + 64 * swapped + P]

        def v_cols(v, t, h):
            return v[:, t, h // 2, :, :].rearrange("p b d -> p (b d)")[:, 64 * (h % 2):64 * (h % 2) + P]

        with nc.Block() as block:
            @block.sync
            def _(sp):
                with sp.Fori(0, B) as b:
                    sp.dma_start(x_t[:], tokens(x, b)).then_inc(x_in, 16)
                    sp.wait_ge(ln_step, 2 * LN_ALL)
                    sp.dma_start(x_t[:], tokens(part, b)).then_inc(part_in, 16)
                    sp.wait_ge(out_done, 2)
                    sp.dma_start(tokens(x1, b), h0[:]).then_inc(stored, 16)
                    sp.wait_ge(stored, 16)
                    st.lead(sp)

            @block.tensor
            def _(pe):
                def project(p, i):
                    n = 4 * p + i
                    if n >= 2:
                        pe.wait_ge(rot_mul, n - 1)
                    w, c = ("q", 0) if i < 2 else ("k", 1)
                    product(nc, pG[i % 2][:], head_cols(w_hi[w], p, i % 2), head_cols(w_lo[w], p, i % 2),
                            c_hi[:, c, :], c_lo[:, c, :], True, True).then_inc(pj_done, 1)

                def scores(h, t):
                    p, n = h // 2, NT * h + t
                    if t == 0:
                        pe.wait_ge(qk_hi_done, 3 * p + 3)
                    if n >= 2:
                        pe.wait_ge(max_done, n - 1)
                    nc.tensor.matmul(pM[n % 2][:], q_hi[:, p % 2, h % 2, t * P:(t + 1) * P], k_hi[:, p % 2, :],
                                     start=True, stop=True).then_inc(s_done, 1)

                def shifted(j):
                    h, t = j // NT, j % NT
                    p = h // 2
                    ks = slice(t * P, (t + 1) * P)
                    if t == 0:
                        pe.wait_ge(qk_lo_done, 3 * p + 3)
                    if j >= 2:
                        pe.wait_ge(exp_done, 2 * (j - 1))
                    product(nc, pT[j % 2][:], k_hi[:, p % 2, ks], k_lo[:, p % 2, ks],
                            q_hi[:, p % 2, h % 2, :], q_lo[:, p % 2, h % 2, :], True, False)
                    if t == 0:
                        pe.wait_ge(diag_done, NT * h + NT)
                    nc.tensor.matmul(pT[j % 2][:], ones[:], diag[:, h % 2, :, :], start=False,
                                     stop=True).then_inc(st_done, 1)

                def weigh(j):
                    h, t = j // NT, j % NT
                    if t == 0 and h >= 2:
                        pe.wait_ge(norm_done, h - 1)
                    pe.wait_ge(p_lo_done, j + 1)
                    product(nc, pA[h % 2][:], v_cols(v_hi, t, h), v_cols(v_lo, t, h), pr_hi[:, j % PR, :],
                            pr_lo[:, j % PR, :], t == 0, t == NT - 1).then_inc(pv_done, 1)

                with pe.Fori(0, B) as b:
                    pe.wait_ge(ln_step, 2 * LN_ALL)
                    for c in range(KC):
                        for t in range(NT):
                            last = nc.tensor.transpose(pT[c][:, t * P:(t + 1) * P],
                                                       h0[:, t, c * P:(c + 1) * P], ident[:])
                        last.then_inc(hT_done, 1)
                    pe.wait_ge(hT_split, 2 * KC)
                    for i in range(2):
                        for c in range(KC):
                            cols = slice((2 * c + i) * P, (2 * c + i + 1) * P)
                            last = product(nc, pG[i][:], w_hi["d"][:, cols], w_lo["d"][:, cols],
                                           hT_hi[:, c, :], hT_lo[:, c, :], c == 0, c == KC - 1)
                        last.then_inc(c_done, 1)
                    pe.wait_ge(c_lo_done, 2)
                    for i in range(2 * NT):
                        t, half = i // 2, i % 2
                        if i >= 2:
                            pe.wait_ge(v_lo_done, i - 1)
                        cols = slice(half * 512, half * 512 + 512)
                        ts = slice(t * P, (t + 1) * P)
                        product(nc, pG[half][:], c_hi[:, 1, ts], c_lo[:, 1, ts], w_hi["v"][:, cols],
                                w_lo["v"][:, cols], True, True).then_inc(v_done, 1)
                    pe.wait_ge(v_lo_done, 2 * NT)
                    for i in range(4):
                        project(0, i)
                    for t in range(NT):
                        scores(0, t)
                    for j in range(J + 2):
                        h, t = j // NT, j % NT
                        if j < J:
                            shifted(j)
                            if h % 2 == 0 and t < 2 and h // 2 + 1 < NP:
                                project(h // 2 + 1, 2 * t)
                                project(h // 2 + 1, 2 * t + 1)
                            if h + 1 < H0:
                                if t == 0:
                                    scores(h + 1, 0)
                                    scores(h + 1, 1)
                                elif t < 3:
                                    scores(h + 1, t + 1)
                        if j >= 2:
                            weigh(j - 2)
                    pe.wait_ge(att_split, 2 * NP)
                    for t in range(NT):
                        ts = slice(t * P, (t + 1) * P)
                        for p in range(NP):
                            cols = slice(p * D, (p + 1) * D)
                            last = product(nc, pG[t // 2][:, (t % 2) * D:(t % 2 + 1) * D], att_hi[:, p, ts],
                                           att_lo[:, p, ts], w_hi["o"][:, cols], w_lo["o"][:, cols],
                                           p == 0, p == NP - 1)
                        if t % 2:
                            last.then_inc(o_done, 1)
                    pe.wait_ge(o_done, 2)
                    st.meet(pe, PE)

            @block.vector
            def _(dve):
                def rotate(p, i):
                    n = 4 * p + i
                    dve.wait_ge(pj_done, n + 1)
                    if n >= 2:
                        dve.wait_ge(rot_add, n // 2)
                    nc.vector.tensor_tensor(rot[:, i % 2, :], pG[i % 2][:], (cos, sin)[i % 2][:],
                                            ALU.mult).then_inc(rot_mul, 1)

                def q_low(p):
                    for i in range(2):
                        dve.wait_ge(qk_hi_done, 3 * p + i + 1)
                        nc.vector.scalar_tensor_tensor(out=q_lo[:, p % 2, i, :], in0=rot[:, 2, :],
                                                       scalar=own[:, i:i + 1], in1=q_hi[:, p % 2, i, :],
                                                       op0=ALU.mult, op1=ALU.subtract).then_inc(qk_lo_done, 1)

                def k_low(p):
                    dve.wait_ge(qk_hi_done, 3 * p + 3)
                    nc.vector.tensor_tensor(k_lo[:, p % 2, :], rot[:, 2, :], k_hi[:, p % 2, :],
                                            ALU.subtract).then_inc(qk_lo_done, 1)

                def maximum(h, t):
                    n = NT * h + t
                    dve.wait_ge(s_done, n + 1)
                    nc.vector.reduce_max(row_max[:, h, t:t + 1], pM[n % 2][:], AX.X).then_inc(max_done, 1)
                    if t == 0 and h >= 2:
                        dve.wait_ge(st_done, NT * (h - 1))
                    dve.wait_ge(max_done, n + 1)
                    nc.vector.tensor_scalar(diag[:, h % 2, t, :], ident[:], row_max[:, h, t:t + 1], -1.0,
                                            ALU.mult, ALU.mult).then_inc(diag_done, 1)

                def normalise(h):
                    own, other = (slice(0, 64), slice(64, 128)) if h % 2 == 0 else (slice(64, 128), slice(0, 64))
                    dve.wait_ge(pv_done, NT * (h + 1))
                    nc.vector.reciprocal(inv[own, :], pA[h % 2][other, :]).then_inc(inv_done, 1)
                    if h >= 2:
                        dve.wait_ge(att_split, 2 * (h // 2))
                    dve.wait_ge(inv_done, h + 1)
                    nc.vector.tensor_tensor(att[own, :], pA[h % 2][own, :], inv[own, :],
                                            ALU.mult).then_inc(norm_done, 1)

                with dve.Fori(0, B) as b:
                    dve.wait_ge(x_in, 16)
                    layer_norm(nc, dve, x_t, x_t, stats, mean_var, small[:, 0, :], small[:, 1, :],
                               small[:, 2, :], small[:, 3, :], None, (ln_step, 0), (root, 1))
                    dve.wait_ge(ln_step, LN_ALL)
                    layer_norm(nc, dve, x_t, h0, stats, mean_var, small[:, 0, :], small[:, 1, :],
                               small[:, 2, :], small[:, 3, :], None, (ln_step, LN_ALL), (root, 2))
                    for i in range(2):
                        dve.wait_ge(c_hi_done, i + 1)
                        nc.vector.tensor_tensor(c_lo[:, i, :], pG[i][:], c_hi[:, i, :],
                                                ALU.subtract).then_inc(c_lo_done, 1)
                    for i in range(2 * NT):
                        t, half = i // 2, i % 2
                        ps = slice(half * NP // 2, (half + 1) * NP // 2)
                        dve.wait_ge(v_hi_done, i + 1)
                        nc.vector.tensor_tensor(v_lo[:, t, ps, 0:3:2, :],
                                                pG[half][:].rearrange("p (h o d) -> p h o d", o=2, d=DH),
                                                v_hi[:, t, ps, 0:3:2, :], ALU.subtract).then_inc(v_lo_done, 1)
                    for i in range(4):
                        rotate(0, i)
                    q_low(0)
                    k_low(0)
                    for t in range(NT):
                        maximum(0, t)
                    for j in range(J + 2):
                        h, t = j // NT, j % NT
                        if j < J:
                            if h % 2 == 0 and t < 2 and h // 2 + 1 < NP:
                                rotate(h // 2 + 1, 2 * t)
                                rotate(h // 2 + 1, 2 * t + 1)
                            if h + 1 < H0:
                                if t == 0:
                                    maximum(h + 1, 0)
                                    maximum(h + 1, 1)
                                elif t < 3:
                                    maximum(h + 1, t + 1)
                            if h % 2 == 0 and h // 2 + 1 < NP:
                                if t == 1:
                                    q_low(h // 2 + 1)
                                if t == 2:
                                    k_low(h // 2 + 1)
                        if j >= 5 and j % NT == 1:
                            normalise(h - 1)
                    dve.wait_ge(qk_lo_done, 3 * NP)
                    dve.wait_ge(part_in, 16)
                    for i in range(2):
                        dve.wait_ge(o_done, i + 1)
                        nc.vector.tensor_tensor(h0[:, 2 * i:2 * i + 2, :],
                                                pG[i][:].rearrange("p (t d) -> p t d", d=D),
                                                x_t[:, 2 * i:2 * i + 2, :], ALU.add).then_inc(out_done, 1)
                    dve.wait_ge(out_done, 2)
                    st.meet(dve, DVE)

            @block.scalar
            def _(act):
                def q_high(p):
                    for i in range(2):
                        act.wait_ge(rot_add, 2 * p + 1)
                        if p >= 2:
                            act.wait_ge(st_done, 2 * NT * (p - 1))
                        nc.scalar.activation(q_hi[:, p % 2, i, :], rot[:, 2, :], ACT.Copy,
                                             scale=own[:, i:i + 1]).then_inc(qk_hi_done, 1)

                def k_high(p):
                    act.wait_ge(rot_add, 2 * p + 2)
                    nc.scalar.copy(k_hi[:, p % 2, :], rot[:, 2, :]).then_inc(qk_hi_done, 1)

                with act.Fori(0, B) as b:
                    for i in range(2):
                        act.wait_ge(ln_step, i * LN_ALL + LN_VAR)
                        nc.scalar.activation(small[:, 1, :], small[:, 0, :], ACT.Sqrt).then_inc(root, 1)
                    for c in range(KC):
                        act.wait_ge(hT_done, c + 1)
                        nc.scalar.activation(hT[:, c, :], pT[c][:], ACT.Identity, bias=ln[:, 1, c:c + 1],
                                             scale=ln[:, 0, c:c + 1]).then_inc(hT_f_done, 1)
                    for i in range(2):
                        act.wait_ge(c_done, i + 1)
                        nc.scalar.copy(c_hi[:, i, :], pG[i][:]).then_inc(c_hi_done, 1)
                    for i in range(2 * NT):
                        t, half = i // 2, i % 2
                        act.wait_ge(v_done, i + 1)
                        nc.scalar.copy(v_hi[:, t, half * NP // 2:(half + 1) * NP // 2, 0:3:2, :],
                                       pG[half][:].rearrange("p (h o d) -> p h o d", o=2, d=DH)).then_inc(v_hi_done, 1)
                    q_high(0)
                    k_high(0)
                    for j in range(J):
                        h, t = j // NT, j % NT
                        act.wait_ge(st_done, j + 1)
                        if j >= 1:
                            act.wait_ge(p_lo_done, j)
                        nc.scalar.activation(pr[:, 0, :], pT[j % 2][:], ACT.Exp, scale=SCALE).then_inc(exp_done, 1)
                        if j >= PR:
                            act.wait_ge(pv_done, j - PR + 1)
                        nc.scalar.activation(pr_hi[:, j % PR, :], pT[j % 2][:], ACT.Exp,
                                             scale=SCALE).then_inc(exp_done, 1)
                        if h % 2 == 0 and h // 2 + 1 < NP:
                            if t == 1:
                                q_high(h // 2 + 1)
                            if t == 2:
                                k_high(h // 2 + 1)
                    act.wait_ge(exp_done, 2 * J)
                    st.meet(act, ACTE)

            @block.gpsimd
            def _(pool):
                def add(u):
                    pool.wait_ge(rot_mul, 2 * u + 2)
                    if u >= 1:
                        pool.wait_ge(qk_lo_done, 3 * (u // 2) + (2 if u % 2 else 0))
                    nc.gpsimd.tensor_tensor(rot[:, 2, :], rot[:, 0, :], rot[:, 1, :], ALU.add).then_inc(rot_add, 1)

                def split_att(p):
                    pool.wait_ge(norm_done, 2 * p + 2)
                    nc.gpsimd.tensor_copy(att_hi[:, p, :], att[:]).then_inc(att_split, 1)
                    pool.wait_ge(att_split, 2 * p + 1)
                    nc.gpsimd.tensor_tensor(att_lo[:, p, :], att[:], att_hi[:, p, :],
                                            ALU.subtract).then_inc(att_split, 1)

                with pool.Fori(0, B) as b:
                    for c in range(KC):
                        pool.wait_ge(hT_f_done, c + 1)
                        nc.gpsimd.tensor_copy(hT_hi[:, c, :], hT[:, c, :]).then_inc(hT_split, 1)
                        pool.wait_ge(hT_split, 2 * c + 1)
                        nc.gpsimd.tensor_tensor(hT_lo[:, c, :], hT[:, c, :], hT_hi[:, c, :],
                                                ALU.subtract).then_inc(hT_split, 1)
                    add(0)
                    add(1)
                    for j in range(J):
                        h, t = j // NT, j % NT
                        nxt = h // 2 + 1
                        more = h % 2 == 0 and nxt < NP
                        if more and t == 0:
                            add(2 * nxt)
                        pool.wait_ge(exp_done, 2 * j + 2)
                        if j >= PR:
                            pool.wait_ge(pv_done, j - PR + 1)
                        nc.gpsimd.tensor_tensor(pr_lo[:, j % PR, :], pr[:, 0, :], pr_hi[:, j % PR, :],
                                                ALU.subtract).then_inc(p_lo_done, 1)
                        if more and t == 1:
                            add(2 * nxt + 1)
                        if h % 2 == 0 and h >= 2 and t == 3:
                            split_att(h // 2 - 1)
                    split_att(NP - 1)
                    pool.wait_ge(att_split, 2 * NP)
                    st.meet(pool, POOL)


NC1 = KC
GW = 4 * (P + DE)


def stage_b(nc, wq_t, wk_t, wv_t, wo_t, wg, bg, own8_d, mask_d, before_d, ident_d, x1, xm_d, x2, sel_d):
    with ExitStack() as ctx:
        st = Stage(nc, ctx, "b")
        sb, bank, sem = st.sb, st.bank, st.sem
        ident = sb("ident", [P, P])
        own8 = sb("own8", [P, 8])
        mask = sb("mask", [P, P + P + 3 * P])
        before = sb("before", [P, NE, NE])
        bg_row = sb("bg_row", [P, NE])
        names = {"q": (wq_t, KC * D), "k": (wk_t, KC * D), "v": (wv_t, KC * D), "o": (wo_t, KC * D),
                 "g": (wg, KC * NE)}
        w_hi = {n: sb(f"w{n}_hi", [P, f], F32R) for n, (_, f) in names.items()}
        w_lo = {n: sb(f"w{n}_lo", [P, f], F32R) for n, (_, f) in names.items()}
        raw = {n: sb(f"raw_{n}", [P, f]) for n, (_, f) in names.items()}
        v_hi = sb("v_hi", [P, NT, 4, GW], F32R)
        v_lo = sb("v_lo", [P, NT, 4, GW], F32R)

        x_t = sb("x_t", [P, NT, D])
        xm = sb("xm", [P, NT, D])
        x_out = sb("x_out", [P, NT, D])
        stats = sb("stats", [P, NT, 6])
        mean_var = sb("mean_var", [P, NT, 2])
        small = sb("small", [P, 4, NT])
        xT_hi = sb("xT_hi", [P, KC, S], F32R)
        xT_lo = sb("xT_lo", [P, KC, S], F32R)
        neg = sb("neg", [P, 2, S])
        ex = sb("ex", [P, 2, S])
        feat = sb("feat", [P, 2 * NC1, S])
        q_hi = sb("q_hi", [P, NC1, S], F32R)
        q_lo = sb("q_lo", [P, NC1, S], F32R)
        kz_hi = sb("kz_hi", [P, 3, S], F32R)
        kz_lo = sb("kz_lo", [P, 3, S], F32R)
        RA = 4
        a_hi = sb("a_hi", [P, RA, S], F32R)
        a_lo = sb("a_lo", [P, RA, S], F32R)
        den = sb("den", [P, S])
        inv = sb("inv", [P, S])
        o = sb("o", [P, NC1, S])
        o_hi = sb("o_hi", [P, NC1, S], F32R)
        o_lo = sb("o_lo", [P, NC1, S], F32R)
        lg = sb("lg", [P, NT, NE])
        top = sb("top", [P, NT])
        tot = sb("tot", [P, NT])
        gate = sb("gate", [P, NT, NE])
        more = sb("more", [P, NT * NE, NE])
        same = sb("same", [P, NT * NE, NE])
        rank = sb("rank", [P, NT, NE])
        sel = sb("sel", [P, NT, NE])

        pG = [bank(f"pG{i}") for i in range(2)]
        pS = [bank(f"pS{i}") for i in range(4)]
        pO = [bank(f"pO{i}") for i in range(2)]

        loaded = st.lasting("loaded")
        w_split = st.lasting("w_split")
        w_lo_done = st.lasting("w_lo_done")
        zeros = st.lasting("zeros")
        fills = st.lasting("fills")
        x_in = sem("x_in")
        ln_step = sem("ln_step")
        root = sem("root")
        xm_out = sem("xm_out")
        xT_done = sem("xT_done")
        xT_hi_done = sem("xT_hi_done")
        xT_lo_done = sem("xT_lo_done")
        lg_done = sem("lg_done")
        gate_step = sem("gate_step")
        gate_exp = sem("gate_exp")
        v_done = sem("v_done")
        v_hi_done = sem("v_hi_done")
        v_lo_done = sem("v_lo_done")
        pj_done = sem("pj_done")
        neg_done = sem("neg_done")
        ex_done = sem("ex_done")
        feat_done = sem("feat_done")
        q_hi_done = sem("q_hi_done")
        q_lo_done = sem("q_lo_done")
        kz_hi_done = sem("kz_hi_done")
        kz_lo_done = sem("kz_lo_done")
        a_done = sem("a_done")
        a_hi_done = sem("a_hi_done")
        a_lo_done = sem("a_lo_done")
        mask_done = sem("mask_done")
        pv_done = sem("pv_done")
        den_done = sem("den_done")
        inv_done = sem("inv_done")
        o_done = sem("o_done")
        o_split = sem("o_split")
        y_done = sem("y_done")
        out_done = sem("out_done")
        stored = sem("stored")

        NJ = H1 * NT
        START = [0, P, 2 * P, 2 * P]
        def width(t):
            return S - START[t]

        with nc.Block() as block:
            @block.sync
            def _(sp):
                for n, (src, _) in names.items():
                    sp.dma_start(raw[n][:], src).then_inc(loaded, 16)
                for dst, src in ((ident, ident_d), (own8, own8_d), (mask, mask_d), (bg_row, bg)):
                    sp.dma_start(dst[:], src).then_inc(loaded, 16)
                sp.dma_start(before[:], before_d).then_inc(loaded, 16)
                with sp.Fori(0, B) as b:
                    sp.dma_start(x_t[:], tokens(x1, b)).then_inc(x_in, 16)
                    sp.wait_ge(ln_step, LN_ALL)
                    sp.dma_start(tokens(xm_d, b), xm[:]).then_inc(xm_out, 16)
                    sp.wait_ge(gate_step, 11)
                    sp.dma_start(tokens(sel_d, b), sel[:]).then_inc(xm_out, 16)
                    sp.wait_ge(out_done, 2)
                    sp.dma_start(tokens(x2, b), x_out[:]).then_inc(stored, 16)
                    sp.wait_ge(xm_out, 32)
                    sp.wait_ge(stored, 16)
                    st.lead(sp)

            @block.tensor
            def _(pe):
                def products(j):
                    h, t = j // NT, j % NT
                    c, w = h // 8, width(t)
                    ks, qs = slice(t * P, (t + 1) * P), slice(START[t], S)
                    if t == 0:
                        pe.wait_ge(q_lo_done, c + 1)
                        pe.wait_ge(kz_lo_done, h + 1)
                    if j >= 4:
                        pe.wait_ge(a_lo_done, j - 3)
                    product(nc, pS[j % 4][:, 0:w], kz_hi[:, h % 3, ks], kz_lo[:, h % 3, ks], q_hi[:, c, qs],
                            q_lo[:, c, qs], True, True).then_inc(a_done, 1)

                def weigh(j):
                    h, t = j // NT, j % NT
                    g, i, w = h // 4, h % 4, width(t)
                    if h % 4 == 0 and t == 0 and g >= 2:
                        pe.wait_ge(o_done, g - 1)
                    pe.wait_ge(mask_done, 2 * j + 2)
                    first, final = i == 0 and t == 0, i == 3 and t == NT - 1
                    cols = slice(i * P, (i + 1) * P)
                    product(nc, pO[g % 2][:, START[t]:S], v_hi[:, t, g, cols], v_lo[:, t, g, cols],
                            a_hi[:, j % RA, 0:w], a_lo[:, j % RA, 0:w], first, final).then_inc(pv_done, 1)

                pe.wait_ge(fills, NT)
                pe.wait_ge(w_lo_done, len(names))
                with pe.Fori(0, B) as b:
                    pe.wait_ge(ln_step, LN_ALL)
                    for c in range(KC):
                        for t in range(NT):
                            last = nc.tensor.transpose(pS[c][:, t * P:(t + 1) * P],
                                                       xm[:, t, c * P:(c + 1) * P], ident[:])
                        last.then_inc(xT_done, 1)
                    pe.wait_ge(xT_lo_done, KC)
                    for i in range(2 * NC1):
                        w = "q" if i < NC1 else "k"
                        if i >= 2:
                            pe.wait_ge(feat_done, i - 1)
                        for c in range(KC):
                            cols = slice(c * D + (i % NC1) * P, c * D + (i % NC1 + 1) * P)
                            last = product(nc, pG[i % 2][:], w_hi[w][:, cols], w_lo[w][:, cols],
                                           xT_hi[:, c, :], xT_lo[:, c, :], c == 0, c == KC - 1)
                        last.then_inc(pj_done, 1)
                    for t in range(NT):
                        ts = slice(t * P, (t + 1) * P)
                        for c in range(KC):
                            last = product(nc, pS[2][:, 8 * t:8 * t + 8], xT_hi[:, c, ts], xT_lo[:, c, ts],
                                           w_hi["g"][:, c * NE:(c + 1) * NE], w_lo["g"][:, c * NE:(c + 1) * NE],
                                           c == 0, c == KC - 1)
                    last.then_inc(lg_done, 1)
                    for t in range(NT):
                        ts = slice(t * P, (t + 1) * P)
                        pe.wait_ge(feat_done, 3 + t % 2)
                        if t >= 2:
                            pe.wait_ge(v_lo_done, t - 1)
                        for c in range(KC):
                            last = product(nc, pG[t % 2][:, 0:D], xT_hi[:, c, ts], xT_lo[:, c, ts],
                                           w_hi["v"][:, c * D:(c + 1) * D], w_lo["v"][:, c * D:(c + 1) * D],
                                           c == 0, c == KC - 1)
                        last.then_inc(v_done, 1)
                    pe.wait_ge(gate_step, 1)
                    pe.wait_ge(v_lo_done, NT)
                    for j in range(NJ + 3):
                        if j < NJ:
                            products(j)
                        if j >= 3:
                            weigh(j - 3)
                    for t in range(NT):
                        ts = slice(t * P, (t + 1) * P)
                        for c in range(NC1):
                            if t == 0:
                                pe.wait_ge(o_split, 2 * c + 2)
                            last = product(nc, pG[t // 2][:, (t % 2) * D:(t % 2 + 1) * D], o_hi[:, c, ts],
                                           o_lo[:, c, ts], w_hi["o"][:, c * D:(c + 1) * D],
                                           w_lo["o"][:, c * D:(c + 1) * D], c == 0, c == NC1 - 1)
                        if t % 2:
                            last.then_inc(y_done, 1)
                    pe.wait_ge(y_done, 2)
                    st.meet(pe, PE)

            @block.vector
            def _(dve):
                for i, n in enumerate(names):
                    dve.wait_ge(w_split, i + 1)
                    nc.vector.tensor_tensor(w_lo[n][:], raw[n][:], w_hi[n][:],
                                            ALU.subtract).then_inc(w_lo_done, 1)

                def features(i):
                    dve.wait_ge(pj_done, i + 1)
                    nc.vector.tensor_scalar(neg[:, i % 2, :], pG[i % 2][:], 0.0, None, ALU.min).then_inc(neg_done, 1)
                    dve.wait_ge(ex_done, i + 1)
                    nc.vector.scalar_tensor_tensor(out=feat[:, i, :], in0=pG[i % 2][:], scalar=0.0,
                                                   in1=ex[:, i % 2, :], op0=ALU.max,
                                                   op1=ALU.add).then_inc(feat_done, 1)

                def k_low(h):
                    dve.wait_ge(kz_hi_done, h + 1)
                    nc.vector.scalar_tensor_tensor(out=kz_lo[:, h % 3, :], in0=feat[:, NC1 + h // 8, :],
                                                   scalar=own8[:, h % 8:h % 8 + 1], in1=kz_hi[:, h % 3, :],
                                                   op0=ALU.mult, op1=ALU.subtract).then_inc(kz_lo_done, 1)

                def low(j):
                    w = width(j % NT)
                    dve.wait_ge(a_hi_done, j + 1)
                    nc.vector.tensor_tensor(a_lo[:, j % RA, 0:w], pS[j % 4][:, 0:w], a_hi[:, j % RA, 0:w],
                                            ALU.subtract).then_inc(a_lo_done, 1)

                def denominators(g):
                    rows = slice(64 * (g % 2), 64 * (g % 2) + 64)
                    dve.wait_ge(pv_done, 4 * NT * (g + 1))
                    nc.vector.tensor_scalar(den[rows, :], pO[g % 2][64:128, :], 1e-6, None,
                                            ALU.max).then_inc(den_done, 1)

                def quotients(c):
                    dve.wait_ge(den_done, 2 * c + 2)
                    nc.vector.reciprocal(inv[:], den[:]).then_inc(inv_done, 1)
                    dve.wait_ge(inv_done, c + 1)
                    for i in range(2):
                        rows = slice(64 * i, 64 * i + 64)
                        nc.vector.tensor_tensor(o[rows, c, :], pO[i][0:64, :], inv[rows, :],
                                                ALU.mult).then_inc(o_done, 1)

                def step(n, ins):
                    ins.then_inc(gate_step, 1)
                    dve.wait_ge(gate_step, n)

                def over(m, shape):
                    return m[:].unsqueeze(2).to_broadcast(shape)

                def choose():
                    by_e = [P, NT, NE]
                    step(2, nc.vector.tensor_reduce(top[:], lg[:], AX.X, ALU.max))
                    step(3, nc.vector.tensor_tensor(lg[:], lg[:], over(top, by_e), ALU.subtract))
                    dve.wait_ge(gate_exp, 1)
                    step(4, nc.vector.tensor_reduce(tot[:], gate[:], AX.X, ALU.add))
                    step(5, nc.vector.reciprocal(tot[:], tot[:]))
                    step(6, nc.vector.tensor_tensor(gate[:], gate[:], over(tot, by_e), ALU.mult))
                    for t in range(NT):
                        mine = gate[:, t, :].unsqueeze(2).to_broadcast([P, NE, NE])
                        others = gate[:, t, :].unsqueeze(1).to_broadcast([P, NE, NE])
                        es = slice(NE * t, NE * t + NE)
                        nc.vector.tensor_tensor(more[:, es, :], others, mine, ALU.is_gt)
                        last = nc.vector.tensor_tensor(same[:, es, :], others, mine, ALU.is_equal)
                    step(7, last)
                    for t in range(NT):
                        es = slice(NE * t, NE * t + NE)
                        last = nc.vector.tensor_tensor(same[:, es, :], same[:, es, :], before[:], ALU.mult)
                    step(8, last)
                    step(9, nc.vector.tensor_tensor(more[:], more[:], same[:], ALU.add))
                    step(10, nc.vector.tensor_reduce(rank[:].rearrange("p t e -> p (t e)"), more[:], AX.X, ALU.add))
                    step(11, nc.vector.tensor_scalar(sel[:], rank[:], 1.5, None, ALU.is_lt))

                with dve.Fori(0, B) as b:
                    dve.wait_ge(x_in, 16)
                    layer_norm(nc, dve, x_t, xm, stats, mean_var, small[:, 0, :], small[:, 1, :],
                               small[:, 2, :], small[:, 3, :], None, (ln_step, 0), (root, 1))
                    for c in range(KC):
                        dve.wait_ge(xT_hi_done, c + 1)
                        nc.vector.tensor_tensor(xT_lo[:, c, :], pS[c][:], xT_hi[:, c, :],
                                                ALU.subtract).then_inc(xT_lo_done, 1)
                    for i in range(2 * NC1):
                        features(i)
                    dve.wait_ge(lg_done, 1)
                    for t in range(NT):
                        last = nc.vector.tensor_tensor(lg[:, t, :], pS[2][:, 8 * t:8 * t + 8], bg_row[:], ALU.add)
                    step(1, last)
                    for t in range(NT):
                        dve.wait_ge(v_hi_done, t + 1)
                        blocks = lambda v: v[:, t, :, :].rearrange("p g (j c) -> p g j c", c=P + DE)[:, :, :, 0:DE]
                        nc.vector.tensor_tensor(blocks(v_lo), pG[t % 2][:, 0:D].rearrange("p (g j c) -> p g j c", j=4, c=DE),
                                                blocks(v_hi), ALU.subtract).then_inc(v_lo_done, 1)
                    k_low(0)
                    k_low(1)
                    for j in range(NJ + 4):
                        if j < NJ:
                            low(j)
                            if j % NT == 1 and j // NT + 2 < H1:
                                k_low(j // NT + 2)
                        if j == 2:
                            choose()
                        if j >= 4 * NT + 3 and (j - 3) % (4 * NT) == 0:
                            denominators((j - 3) // (4 * NT) - 1)
                        if j >= 8 * NT + 3 and (j - 3) % (8 * NT) == 0:
                            quotients((j - 3) // (8 * NT) - 1)
                    for i in range(2):
                        dve.wait_ge(y_done, i + 1)
                        nc.vector.tensor_tensor(x_out[:, 2 * i:2 * i + 2, :],
                                                pG[i][:].rearrange("p (t d) -> p t d", d=D),
                                                x_t[:, 2 * i:2 * i + 2, :], ALU.add).then_inc(out_done, 1)
                    dve.wait_ge(out_done, 2)
                    dve.wait_ge(kz_lo_done, H1)
                    st.meet(dve, DVE)

            @block.scalar
            def _(act):
                act.wait_ge(loaded, 16 * (len(names) + 5))
                for n in names:
                    nc.scalar.copy(w_hi[n][:], raw[n][:]).then_inc(w_split, 1)

                def k_high(h):
                    if h >= 3:
                        act.wait_ge(a_done, NT * (h - 2))
                    nc.scalar.activation(kz_hi[:, h % 3, :], feat[:, NC1 + h // 8, :], ACT.Copy,
                                         scale=own8[:, h % 8:h % 8 + 1]).then_inc(kz_hi_done, 1)

                with act.Fori(0, B) as b:
                    act.wait_ge(ln_step, LN_VAR)
                    nc.scalar.activation(small[:, 1, :], small[:, 0, :], ACT.Sqrt).then_inc(root, 1)
                    for c in range(KC):
                        act.wait_ge(xT_done, c + 1)
                        nc.scalar.copy(xT_hi[:, c, :], pS[c][:]).then_inc(xT_hi_done, 1)
                    for i in range(2 * NC1):
                        act.wait_ge(neg_done, i + 1)
                        nc.scalar.activation(ex[:, i % 2, :], neg[:, i % 2, :], ACT.Exp).then_inc(ex_done, 1)
                    act.wait_ge(feat_done, 2 * NC1)
                    for c in range(NC1):
                        nc.scalar.copy(q_hi[:, c, :], feat[:, c, :]).then_inc(q_hi_done, 1)
                    k_high(0)
                    k_high(1)
                    for t in range(NT):
                        act.wait_ge(v_done, t + 1)
                        nc.scalar.copy(v_hi[:, t, :, :].rearrange("p g (j c) -> p g j c", c=P + DE)[:, :, :, 0:DE],
                                       pG[t % 2][:, 0:D].rearrange("p (g j c) -> p g j c", j=4, c=DE)).then_inc(v_hi_done, 1)
                    for j in range(NJ):
                        h, t = j // NT, j % NT
                        w = width(t)
                        act.wait_ge(a_done, j + 1)
                        if j >= RA:
                            act.wait_ge(pv_done, j - RA + 1)
                        nc.scalar.copy(a_hi[:, j % RA, 0:w], pS[j % 4][:, 0:w]).then_inc(a_hi_done, 1)
                        if t == 1 and h + 2 < H1:
                            k_high(h + 2)
                        if j == 6:
                            act.wait_ge(gate_step, 3)
                            nc.scalar.activation(gate[:], lg[:], ACT.Exp).then_inc(gate_exp, 1)
                    act.wait_ge(a_hi_done, NJ)
                    act.wait_ge(kz_hi_done, H1)
                    st.meet(act, ACTE)

            @block.gpsimd
            def _(pool):
                for v in (v_hi, v_lo):
                    nc.gpsimd.memset(v[:].bitcast(F32), 0.0).then_inc(zeros, 1)
                pool.wait_ge(zeros, 2)
                for t in range(NT):
                    blocks = v_hi[:, t, :, :].rearrange("p g (j c) -> p g j c", c=P + DE)[:, :, :, 64:64 + DE]
                    nc.gpsimd.memset(blocks.bitcast(F32), 1.0).then_inc(fills, 1)
                pool.wait_ge(fills, NT)

                def split_o(c):
                    pool.wait_ge(o_done, 2 * c + 2)
                    nc.gpsimd.tensor_copy(o_hi[:, c, :], o[:, c, :]).then_inc(o_split, 1)
                    pool.wait_ge(o_split, 2 * c + 1)
                    nc.gpsimd.tensor_tensor(o_lo[:, c, :], o[:, c, :], o_hi[:, c, :],
                                            ALU.subtract).then_inc(o_split, 1)

                with pool.Fori(0, B) as b:
                    for c in range(NC1):
                        pool.wait_ge(q_hi_done, c + 1)
                        nc.gpsimd.tensor_tensor(q_lo[:, c, :], feat[:, c, :], q_hi[:, c, :],
                                                ALU.subtract).then_inc(q_lo_done, 1)
                    for j in range(NJ):
                        h, t = j // NT, j % NT
                        pool.wait_ge(a_lo_done, j + 1)
                        cut = slice(0, 2 * P) if t == 3 else slice(0, P)
                        m = mask[:, 0:2 * P] if t == 3 else mask[:, P:2 * P]
                        for a in (a_hi, a_lo):
                            nc.gpsimd.tensor_tensor(a[:, j % RA, cut], a[:, j % RA, cut], m, ALU.mult).then_inc(mask_done, 1)
                        if j == 8 * NT + 6:
                            split_o(0)
                    split_o(1)
                    pool.wait_ge(o_split, 2 * NC1)
                    pool.wait_ge(mask_done, 2 * NJ)
                    st.meet(pool, POOL)




def stage_c(nc, w1, w2, b1, b2, thresholds_d, lower_d, ident_d, xm_d, x2, sel_d, rows, results, out):
    I32 = mybir.dt.int32
    with ExitStack() as ctx:
        st = Stage(nc, ctx, "c")
        sb, bank, sem = st.sb, st.bank, st.sem
        ident = sb("ident", [P, P])
        slot_a = sb("slot_a", [P, TT], I32)
        slot_b = sb("slot_b", [P, TT], I32)
        trips = sb("trips", [P, NE], I32)
        first = sb("first", [P, NE], I32)
        all_rows = sb("all_rows", [P, TT, D])

        loaded = st.lasting("loaded")
        rows_in = st.lasting("rows_in")
        filled = st.lasting("filled")
        counted = st.lasting("counted")
        slot_step = st.lasting("slot_step")
        ones_set = st.lasting("ones_set")
        scattered = st.lasting("scattered")

        with ExitStack() as ctx2:
            def tmp(name, shape, dt=F32):
                return ctx2.enter_context(nc.sbuf_tensor(f"c_{name}", shape, dt))
            lower = tmp("lower", [P, P])
            ones = tmp("ones", [P, P])
            thresholds = tmp("thresholds", [P, NE, MAX_TRIPS - 1])
            sel = tmp("sel", [P, TT, NE])
            tot = tmp("tot", [P, TT, NE])
            upto = tmp("upto", [P, TT, NE])
            unit = tmp("unit", [P, TT])
            slot = tmp("slot", [P, TT, NE])
            pick = tmp("pick", [P, TT, NE])
            near = tmp("near", [P, 2, TT])
            above = tmp("above", [P, NE, MAX_TRIPS - 1])
            n_trips = tmp("n_trips", [P, NE])
            trips_upto = tmp("trips_upto", [P, NE])
            e_base = tmp("e_base", [P, NE])
            p_in = ctx2.enter_context(nc.psum_tensor("c_p_in", [P, TT, NE], F32))
            p_tot = ctx2.enter_context(nc.psum_tensor("c_p_tot", [P, TT, NE], F32))
            FAR = float(1 << 20)
            with nc.Block() as block:
                @block.sync
                def _(sp):
                    for dst, src in ((ident, ident_d), (lower, lower_d), (thresholds, thresholds_d),
                                     (sel, sel_d.rearrange("(t p) e -> p t e", p=P))):
                        sp.dma_start(dst[:], src).then_inc(loaded, 16)
                    sp.dma_start(all_rows[:], xm_d.rearrange("(t p) d -> p t d", p=P)).then_inc(rows_in, 16)

                @block.tensor
                def _(pe):
                    pe.wait_ge(loaded, 64)
                    pe.wait_ge(ones_set, 1)
                    nc.tensor.matmul(p_in[:], lower[:], sel[:], start=True, stop=True).then_inc(counted, 1)
                    nc.tensor.matmul(p_tot[:], ones[:], sel[:], start=True, stop=True).then_inc(counted, 1)

                @block.vector
                def _(dve):
                    def step(n, ins):
                        ins.then_inc(slot_step, 1)
                        dve.wait_ge(slot_step, n)
                    step(1, nc.vector.memset(unit[:], 1.0))
                    dve.wait_ge(counted, 2)
                    step(2, nc.vector.tensor_copy(tot[:], p_tot[:]))
                    for e in range(NE):
                        last = nc.vector.tensor_tensor_scan(out=upto[:, :, e], data0=unit[:], data1=tot[:, :, e],
                                                            initial=0.0, op0=ALU.mult, op1=ALU.add)
                    step(3, last)
                    step(4, nc.vector.tensor_tensor(
                        above[:], upto[:, TT - 1, :].unsqueeze(2).to_broadcast([P, NE, MAX_TRIPS - 1]),
                        thresholds[:], ALU.is_gt))
                    step(5, nc.vector.tensor_reduce(n_trips[:], above[:], AX.X, ALU.add))
                    step(6, nc.vector.tensor_scalar(n_trips[:], n_trips[:], 1.0, None, ALU.add))
                    step(7, nc.vector.tensor_tensor_scan(out=trips_upto[:], data0=unit[:, 0:NE], data1=n_trips[:],
                                                         initial=0.0, op0=ALU.mult, op1=ALU.add))
                    step(8, nc.vector.tensor_tensor(e_base[:], trips_upto[:], n_trips[:], ALU.subtract))
                    nc.vector.tensor_copy(trips[:], n_trips[:])
                    step(9, nc.vector.tensor_copy(first[:], e_base[:]))
                    step(10, nc.vector.tensor_scalar(e_base[:], e_base[:], float(TILE), None, ALU.mult))
                    step(11, nc.vector.tensor_tensor(slot[:], upto[:], tot[:], ALU.subtract))
                    step(12, nc.vector.tensor_tensor(slot[:], slot[:], p_in[:], ALU.add))
                    step(13, nc.vector.tensor_tensor(slot[:], slot[:], e_base[:].unsqueeze(1).to_broadcast([P, TT, NE]),
                                                     ALU.add))
                    step(14, nc.vector.scalar_tensor_tensor(out=pick[:], in0=slot[:], scalar=-FAR, in1=sel[:],
                                                            op0=ALU.add, op1=ALU.mult))
                    step(15, nc.vector.tensor_reduce(near[:, 0, :], pick[:], AX.X, ALU.min))
                    step(16, nc.vector.tensor_scalar(slot_a[:], near[:, 0, :], FAR, None, ALU.add))
                    step(17, nc.vector.tensor_tensor(pick[:], slot[:], sel[:], ALU.mult))
                    step(18, nc.vector.tensor_reduce(near[:, 1, :], pick[:], AX.X, ALU.max))
                    step(19, nc.vector.tensor_copy(slot_b[:], near[:, 1, :]))

                @block.gpsimd
                def _(pool):
                    nc.gpsimd.memset(ones[:], 1.0).then_inc(ones_set, 1)
                    pool.wait_ge(slot_step, 19)
                    pool.wait_ge(rows_in, 16)
                    for t in range(TT):
                        for s in (slot_a, slot_b):
                            pool.indirect_dma_start(out=rows, out_offset=bass.IndirectOffsetOnAxis(ap=s[:, t:t + 1], axis=0),
                                                    in_=all_rows[:, t, :], in_offset=None).then_inc(scattered, 16)
                    pool.wait_ge(scattered, 32 * TT)

        raw1 = sb("raw1", [P, KC, FF])
        raw2 = sb("raw2", [P, MC, D])
        w1_hi = sb("w1_hi", [P, KC, FF], F32R)
        w1_lo = sb("w1_lo", [P, KC, FF], F32R)
        w2_hi = sb("w2_hi", [P, MC, D], F32R)
        w2_lo = sb("w2_lo", [P, MC, D], F32R)
        raw_b1 = sb("raw_b1", [P, MC])
        raw_b2 = sb("raw_b2", [P, D])
        b1_c = sb("b1_c", [P, MC])
        b2_row = sb("b2_row", [P, D])
        x_t = sb("x_t", [P, NT, D])
        xT_hi = sb("xT_hi", [P, KC, S], F32R)
        xT_lo = sb("xT_lo", [P, KC, S], F32R)
        RH = 4
        h = sb("h", [P, RH, S])
        h_hi = sb("h_hi", [P, RH, S], F32R)
        h_lo = sb("h_lo", [P, RH, S], F32R)
        y = sb("y", [P, NT, D])
        pX = bank("pX")
        pU = [bank(f"pU{i}") for i in range(3)]
        pY = [bank(f"pY{i}", (P, D)) for i in range(NT)]

        raw_in = st.lasting("raw_in")
        w_hi_done = sem("w_hi_done")
        w_lo_done = sem("w_lo_done")
        x_in = sem("x_in")
        xT_done = sem("xT_done")
        xT_hi_done = sem("xT_hi_done")
        xT_lo_done = sem("xT_lo_done")
        up_done = sem("up_done")
        relu_done = sem("relu_done")
        h_lo_done = sem("h_lo_done")
        down_done = sem("down_done")
        y_done = sem("y_done")
        stored = sem("stored")

        def per_expert(eng, split, run):
            def one(e, more):
                split(e)
                n = eng.value_load(trips[0:1, bass.ds(e, 1)], min_val=1, max_val=MAX_TRIPS)
                run(e, n, more)
            with eng.Fori(0, NE - 1) as e:
                one(e, True)
            one(NE - 1, False)

        with nc.Block() as block:
            @block.sync
            def _(sp):
                def load(e):
                    sp.dma_start(raw1[:], w1[bass.ds(e, 1), :, :].rearrange("o (c p) f -> p (o c) f", p=P)).then_inc(raw_in, 16)
                    sp.dma_start(raw2[:], w2[bass.ds(e, 1), :, :].rearrange("o (m p) d -> p (o m) d", p=P)).then_inc(raw_in, 16)
                    sp.dma_start(raw_b1[:], b1[bass.ds(e, 1), :, :].rearrange("o p m -> p (o m)")).then_inc(raw_in, 16)
                    sp.dma_start(raw_b2[:], b2[bass.ds(e, 1), :, :].rearrange("o p d -> p (o d)")).then_inc(raw_in, 16)

                def run(e, n, more):
                    if more:
                        load(e + 1)
                    start = sp.value_load(first[0:1, bass.ds(e, 1)], min_val=0, max_val=TILES - 1)
                    with sp.Fori(0, n) as i:
                        at = nc.s_assert_le(start + i, TILES - 1) * TILE
                        sp.dma_start(x_t[:], rows[bass.ds(at, TILE), :].rearrange("(t p) d -> p t d", p=P)).then_inc(x_in, 16)
                        sp.wait_ge(y_done, NT)
                        sp.dma_start(results[bass.ds(at, TILE), :].rearrange("(t p) d -> p t d", p=P),
                                     y[:]).then_inc(stored, 16)
                        sp.wait_ge(stored, 16)
                        st.lead(sp)

                load(0)
                per_expert(sp, lambda e: st.lead(sp), run)

            @block.tensor
            def _(pe):
                def up(m):
                    if m >= 3:
                        pe.wait_ge(relu_done, 2 * (m - 2))
                    for c in range(KC):
                        cols = slice(m * P, (m + 1) * P)
                        last = product(nc, pU[m % 3][:], w1_hi[:, c, cols], w1_lo[:, c, cols], xT_hi[:, c, :],
                                       xT_lo[:, c, :], c == 0, c == KC - 1)
                    last.then_inc(up_done, 1)

                def down(m):
                    pe.wait_ge(h_lo_done, m + 1)
                    for t in range(NT):
                        ts = slice(t * P, (t + 1) * P)
                        last = product(nc, pY[t][:], h_hi[:, m % RH, ts], h_lo[:, m % RH, ts], w2_hi[:, m, :],
                                       w2_lo[:, m, :], m == 0, m == MC - 1)
                    last.then_inc(down_done, 1)

                def run(e, n, more):
                    with pe.Fori(0, n):
                        pe.wait_ge(x_in, 16)
                        for c in range(KC):
                            if c:
                                pe.wait_ge(xT_lo_done, 1)
                            for t in range(NT):
                                last = nc.tensor.transpose(pX[:, t * P:(t + 1) * P], x_t[:, t, c * P:(c + 1) * P], ident[:])
                            last.then_inc(xT_done, 1)
                        pe.wait_ge(xT_lo_done, KC)
                        for m in range(MC + 2):
                            if m < MC:
                                up(m)
                            if m >= 2:
                                down(m - 2)
                        pe.wait_ge(down_done, MC)
                        st.meet(pe, PE)

                per_expert(pe, lambda e: st.meet(pe, PE), run)

            @block.scalar
            def _(act):
                def split(e):
                    act.wait_ge(raw_in, 64)
                    act.sem_clear(raw_in)
                    nc.scalar.copy(w1_hi[:], raw1[:]).then_inc(w_hi_done, 1)
                    nc.scalar.copy(w2_hi[:], raw2[:]).then_inc(w_hi_done, 1)
                    nc.scalar.copy(b1_c[:], raw_b1[:]).then_inc(w_hi_done, 1)
                    nc.scalar.copy(b2_row[:], raw_b2[:]).then_inc(w_hi_done, 1)
                    act.wait_ge(w_hi_done, 4)
                    st.meet(act, ACTE)

                def run(e, n, more):
                    with act.Fori(0, n):
                        for c in range(KC):
                            act.wait_ge(xT_done, c + 1)
                            nc.scalar.copy(xT_hi[:, c, :], pX[:]).then_inc(xT_hi_done, 1)
                        for m in range(MC):
                            act.wait_ge(up_done, m + 1)
                            if m >= RH:
                                act.wait_ge(down_done, m - RH + 1)
                            for dst in (h, h_hi):
                                nc.scalar.activation(dst[:, m % RH, :], pU[m % 3][:], ACT.Relu,
                                                     bias=b1_c[:, m:m + 1]).then_inc(relu_done, 1)
                        act.wait_ge(relu_done, 2 * MC)
                        st.meet(act, ACTE)

                per_expert(act, split, run)

            @block.vector
            def _(dve):
                def split(e):
                    dve.wait_ge(w_hi_done, 1)
                    nc.vector.tensor_tensor(w1_lo[:], raw1[:], w1_hi[:], ALU.subtract).then_inc(w_lo_done, 1)
                    dve.wait_ge(w_hi_done, 2)
                    nc.vector.tensor_tensor(w2_lo[:], raw2[:], w2_hi[:], ALU.subtract).then_inc(w_lo_done, 1)
                    dve.wait_ge(w_lo_done, 2)
                    st.meet(dve, DVE)

                def run(e, n, more):
                    with dve.Fori(0, n):
                        for c in range(KC):
                            dve.wait_ge(xT_hi_done, c + 1)
                            nc.vector.tensor_tensor(xT_lo[:, c, :], pX[:], xT_hi[:, c, :],
                                                    ALU.subtract).then_inc(xT_lo_done, 1)
                        for m in range(MC):
                            dve.wait_ge(relu_done, 2 * m + 2)
                            nc.vector.tensor_tensor(h_lo[:, m % RH, :], h[:, m % RH, :], h_hi[:, m % RH, :],
                                                    ALU.subtract).then_inc(h_lo_done, 1)
                        dve.wait_ge(down_done, MC)
                        for t in range(NT):
                            nc.vector.tensor_tensor(y[:, t, :], pY[t][:], b2_row[:], ALU.add).then_inc(y_done, 1)
                        dve.wait_ge(y_done, NT)
                        st.meet(dve, DVE)

                per_expert(dve, split, run)

            @block.gpsimd
            def _(pool):
                def run(e, n, more):
                    with pool.Fori(0, n):
                        st.meet(pool, POOL)

                per_expert(pool, lambda e: st.meet(pool, POOL), run)

        with ExitStack() as ctx2:
            RG = 4
            ya = ctx2.enter_context(nc.sbuf_tensor("c_ya", [P, RG, D], F32))
            yb = ctx2.enter_context(nc.sbuf_tensor("c_yb", [P, RG, D], F32))
            x2_in = st.lasting("x2_in")
            ya_in = [st.lasting(f"ya_in{i}") for i in range(RG)]
            yb_in = [st.lasting(f"yb_in{i}") for i in range(RG)]
            added = st.lasting("added")
            out_stored = st.lasting("out_stored")
            with nc.Block() as block:
                @block.sync
                def _(sp):
                    sp.dma_start(all_rows[:], x2.rearrange("(t p) d -> p t d", p=P)).then_inc(x2_in, 16)
                    for i in range(TT // NT):
                        sp.wait_ge(added, 2 * NT * (i + 1))
                        sp.dma_start(tokens(out, i), all_rows[:, NT * i:NT * i + NT, :]).then_inc(out_stored, 16)
                    sp.wait_ge(out_stored, 16 * (TT // NT))

                @block.gpsimd
                def _(pool):
                    for t in range(TT):
                        if t >= RG:
                            pool.wait_ge(added, 2 * (t - RG + 1))
                        for dst, s, done in ((ya, slot_a, ya_in), (yb, slot_b, yb_in)):
                            pool.indirect_dma_start(out=dst[:, t % RG, :], out_offset=None, in_=results,
                                                    in_offset=bass.IndirectOffsetOnAxis(ap=s[:, t:t + 1], axis=0)
                                                    ).then_inc(done[t % RG], 16)

                @block.vector
                def _(dve):
                    dve.wait_ge(x2_in, 16)
                    for t in range(TT):
                        for k, (src, done) in enumerate(((ya, ya_in), (yb, yb_in))):
                            dve.wait_ge(done[t % RG], 16 * (t // RG + 1))
                            if k:
                                dve.wait_ge(added, 2 * t + 1)
                            nc.vector.tensor_tensor(all_rows[:, t, :], all_rows[:, t, :], src[:, t % RG, :],
                                                    ALU.add).then_inc(added, 1)


def rope_tables():
    inv_freq = 1.0 / 10000.0 ** (np.arange(0, DH, 2, dtype=np.float32) / DH)
    freqs = np.outer(np.arange(S, dtype=np.float32), inv_freq)[:, (2 * np.arange(32)) % 32].T
    c, s = np.cos(freqs), np.sin(freqs)
    return (np.ascontiguousarray(np.concatenate([c, c, c, c])).astype(np.float32),
            np.ascontiguousarray(np.concatenate([-s, -s, s, s])).astype(np.float32))


def lay_out(a):
    even, odd = np.arange(0, DH, 2), np.arange(1, DH, 2)
    of_pair = lambda f: np.concatenate([f, DH + f])
    rows = (2 * DH * np.arange(NP)[:, None] + np.concatenate([of_pair(even), of_pair(odd), of_pair(even)])[None]).ravel()
    by_chunk = lambda m: m.reshape(-1, P, m.shape[-1]).transpose(1, 0, 2).reshape(P, -1)
    down = np.stack([a["L0_attn_w_down_q"], a["L0_attn_w_down_kv"]])
    cos, sin = rope_tables()
    return {
        "x": a["L0_attn_x"].reshape(T, D),
        "w1_rows": a["L0_ffn_w1"],
        "w1_t": a["L0_ffn_w1"].T,
        "w2_t": a["L0_ffn_w2"].T,
        "b1": a["L0_ffn_b1"].reshape(MC, P).T,
        "b2": np.broadcast_to(a["L0_ffn_b2"], (P, D)),
        "ident_d": np.eye(P, dtype=np.float32),
        "wd_t": down.reshape(2, P, KC, P).transpose(3, 2, 0, 1).reshape(P, -1),
        "wq_t": a["L0_attn_w_up_q"][rows].T,
        "wk_t": a["L0_attn_w_up_k"][rows].T,
        "wv_t": a["L0_attn_w_up_v"].T,
        "wo_t": by_chunk(a["L0_attn_w_out"].T),
        "ln_sb": np.stack([a["L0_attn_ln_scale"].reshape(KC, P), a["L0_attn_ln_bias"].reshape(KC, P)]).transpose(2, 0, 1),
        "rope_c": cos,
        "rope_s": sin,
        "own_d": np.ascontiguousarray(np.tile(np.repeat(np.eye(2, dtype=np.float32), 32, axis=0), (2, 1))),
        "l1_wq": by_chunk(a["L1_attn_Wq"].T),
        "l1_wk": by_chunk(a["L1_attn_Wk"].T),
        "l1_wv": by_chunk(a["L1_attn_Wv"].T),
        "l1_wo": by_chunk(a["L1_attn_Wo"].T),
        "wg": by_chunk(a["L1_ffn_Wg"]),
        "bg": np.broadcast_to(a["L1_ffn_bg"], (P, NE)),
        "own8_d": np.repeat(np.eye(8, dtype=np.float32), DE, axis=0),
        "mask_d": np.concatenate([np.zeros((P, P)), np.triu(np.ones((P, P))), np.ones((P, 3 * P))], 1).astype(np.float32),
        "e_w1": a["L1_ffn_W1"],
        "e_w2": a["L1_ffn_W2"],
        "e_b1": a["L1_ffn_b1"].reshape(NE, MC, P).transpose(0, 2, 1),
        "e_b2": np.broadcast_to(a["L1_ffn_b2"][:, None, :], (NE, P, D)),
        "thresholds": np.broadcast_to(TILE * np.arange(1, MAX_TRIPS, dtype=np.float32), (P, NE, MAX_TRIPS - 1)),
        "lower_d": np.triu(np.ones((P, P), np.float32), 1),
        "before_d": np.broadcast_to(np.tril(np.ones((NE, NE)), -1).astype(np.float32), (P, NE, NE)),
    }


STAGES = (
    (stage_f, ("x", "w1_rows", "w1_t", "w2_t", "b1", "b2", "ident_d"), ("part", "rows", "results")),
    (stage_a, ("x", "wd_t", "wq_t", "wk_t", "wv_t", "wo_t", "ln_sb", "rope_c", "rope_s", "own_d", "ident_d"),
     ("part", "x1")),
    (stage_b, ("l1_wq", "l1_wk", "l1_wv", "l1_wo", "wg", "bg", "own8_d", "mask_d", "before_d", "ident_d"),
     ("x1", "xm", "x2", "sel")),
    (stage_c, ("e_w1", "e_w2", "e_b1", "e_b2", "thresholds", "lower_d", "ident_d"),
     ("xm", "x2", "sel", "rows", "results", "out")),
)
SCRATCH = {"part": (T, D), "x1": (T, D), "xm": (T, D), "x2": (T, D), "sel": (T, NE),
           "rows": (TILES * TILE, D), "results": (TILES * TILE, D)}


def program(nc, aps):
    for stage, inputs, between in STAGES:
        stage(nc, *(aps[n] for n in inputs + between))


def kernel(**inputs):
    import concourse.bacc as bacc
    from concourse.bass_utils import run_bass_kernel_spmd

    arrays = {n: np.ascontiguousarray(v) for n, v in lay_out({k: np.asarray(v) for k, v in inputs.items()}).items()}
    nc = bacc.Bacc("TRN2", target_bir_lowering=False, num_devices=1)
    aps = {n: nc.dram_tensor(f"in_{n}", a.shape, F32, kind="ExternalInput").ap() for n, a in arrays.items()}
    for n, shape in SCRATCH.items():
        aps[n] = nc.dram_tensor(f"mid_{n}", shape, F32, kind="Internal").ap()
    aps["out"] = nc.dram_tensor("out_x", (T, D), F32, kind="ExternalOutput").ap()
    program(nc, aps)
    result = run_bass_kernel_spmd(nc, [{f"in_{n}": a for n, a in arrays.items()}], core_ids=[0])
    return result.results[0]["out_x"].reshape(B, S, D)
```

```python
from contextlib import ExitStack

import numpy as np

import concourse.bass as bass
from concourse import mybir

F32 = mybir.dt.float32
F32R = mybir.dt.float32r
ALU = mybir.AluOpType
ACT = mybir.ActivationFunctionType
AX = mybir.AxisListType

P = 128
B, S, D = 8, 512, 256
T = B * S
NT = S // P
KC = D // P
H0, DH = 16, 64
NP = H0 // 2
FF = 1024
MC = FF // P
H1, DE = 16, 16
NE = 8
TT = T // P
TILE = 512
TILES = 2 * T // TILE + NE
MAX_TRIPS = T // TILE
ZERO_W = 1024
EPS = 1e-5
SCALE = 1.0 / 8.0
WORKERS = 4
PE, DVE, ACTE, POOL = range(WORKERS)


class Stage:

    def __init__(self, nc, ctx, name):
        self.nc, self.ctx, self.name = nc, ctx, name
        self.cleared = []
        self.arrived = self.lasting("arrived")
        self.go = [self.lasting(f"go{i}") for i in range(WORKERS)]

    def sb(self, name, shape, dt=F32):
        return self.ctx.enter_context(self.nc.sbuf_tensor(f"{self.name}_{name}", shape, dt))

    def bank(self, name, shape=(P, 512)):
        return self.ctx.enter_context(self.nc.psum_tensor(f"{self.name}_{name}", list(shape), F32))

    def lasting(self, name):
        return self.ctx.enter_context(self.nc.semaphore(f"{self.name}_{name}"))

    def sem(self, name):
        s = self.lasting(name)
        self.cleared.append(s)
        return s

    def meet(self, eng, worker):
        eng.sem_inc(self.arrived, 1)
        eng.wait_ge(self.go[worker], 1)
        eng.sem_clear(self.go[worker])

    def lead(self, eng, workers=WORKERS):
        eng.wait_ge(self.arrived, workers)
        for s in self.cleared:
            eng.sem_clear(s)
        eng.sem_clear(self.arrived)
        for go in self.go[:workers]:
            eng.sem_inc(go, 1)


def product(nc, out, l_hi, l_lo, r_hi, r_lo, start, stop, **kw):
    nc.tensor.matmul(out, l_lo, r_hi, start=start, stop=False, **kw)
    nc.tensor.matmul(out, l_hi, r_lo, start=False, stop=False, **kw)
    return nc.tensor.matmul(out, l_hi, r_hi, start=False, stop=stop, **kw)


def layer_norm(nc, dve, x, out, stats, mean_var, var_eps, std, rstd, shift, ready, done, root_done):
    sem, n = done
    tiles = x.shape[1]
    for t in range(tiles):
        nc.vector.bn_stats(stats[:, t, :], x[:, t, :]).then_inc(sem, 1)
    dve.wait_ge(sem, n + tiles)
    for t in range(tiles):
        nc.vector.bn_aggr(mean_var[:, t, :], stats[:, t, :]).then_inc(sem, 1)
    dve.wait_ge(sem, n + 2 * tiles)
    nc.vector.tensor_scalar(var_eps, mean_var[:, :, 1], EPS, None, ALU.add).then_inc(sem, 1)
    dve.wait_ge(*root_done)
    nc.vector.reciprocal(rstd, std).then_inc(sem, 1)
    dve.wait_ge(sem, n + 2 * tiles + 2)
    nc.vector.scalar_tensor_tensor(out=shift, in0=mean_var[:, :, 0], scalar=-1.0, in1=rstd,
                                   op0=ALU.mult, op1=ALU.mult).then_inc(sem, 1)
    dve.wait_ge(sem, n + 2 * tiles + 3)
    for t in range(tiles):
        nc.vector.tensor_scalar(out[:, t, :], x[:, t, :], rstd[:, t:t + 1], shift[:, t:t + 1],
                                ALU.mult, ALU.add).then_inc(sem, 1)
    return n + 3 * tiles + 3


LN_VAR = 2 * NT + 1
LN_ALL = 3 * NT + 3


def tokens(ap, b):
    return ap[bass.ds(b * S, S), :].rearrange("(t p) d -> p t d", p=P)


def latent(ap, b):
    return ap[bass.ds(b * P, P), :].rearrange("p (i s) -> p i s", i=4)


def stage_f(nc, x, w1_rows, w1_t, w2_t, b1, b2, wd_t, ln_sb, ident_d, part, latents, rows, results):
    with ExitStack() as ctx:
        st = Stage(nc, ctx, "f")
        sb, bank, sem = st.sb, st.bank, st.sem
        ident = sb("ident", [P, P])
        ones = sb("ones", [P, P])
        zero = sb("zero", [P, ZERO_W])
        b1_c = sb("b1_c", [P, MC])
        b2_row = sb("b2_row", [P, D])
        alpha1 = sb("alpha1", [P, MC])
        alpha2 = sb("alpha2", [P, 2, D])
        sign1 = sb("sign1", [P, KC, FF], F32R)
        sign2 = sb("sign2", [P, MC, D], F32R)
        w1r = sb("w1r", [P, MC, D])
        w1s = sb("w1s", [P, KC, FF])
        w2s = sb("w2s", [P, MC, D])
        w2abs = sb("w2abs", [P, MC, D])

        x_t = sb("x_t", [P, NT, D])
        xn = sb("xn", [P, NT, D])
        base = sb("base", [P, NT, D])
        y = sb("y", [P, NT, D])
        out = sb("out", [P, NT, D])
        stats = sb("stats", [P, NT, 6])
        mean_var = sb("mean_var", [P, NT, 2])
        small = sb("small", [P, 4, NT])
        xT_hi = sb("xT_hi", [P, KC, S], F32R)
        xT_lo = sb("xT_lo", [P, KC, S], F32R)
        g = sb("g", [P, MC, S])
        g_hi = sb("g_hi", [P, MC, S], F32R)
        g_lo = sb("g_lo", [P, MC, S], F32R)

        ln = sb("ln", [P, 2, KC])
        wd = sb("wd", [P, KC * 2 * P])
        wd_hi = sb("wd_hi", [P, KC * 2 * P], F32R)
        wd_lo = sb("wd_lo", [P, KC * 2 * P], F32R)
        h = sb("h", [P, NT, D])
        hT = sb("hT", [P, KC, S])
        hT_hi = sb("hT_hi", [P, KC, S], F32R)
        hT_lo = sb("hT_lo", [P, KC, S], F32R)
        c_parts = sb("c_parts", [P, 4, S], F32R)

        pX = [bank(f"pX{c}") for c in range(KC)]
        pU = [bank(f"pU{i}") for i in range(3)]
        pY = [bank(f"pY{i}", (P, 2, D)) for i in range(2)]

        loaded = st.lasting("loaded")
        ones_set = st.lasting("ones_set")
        zero_set = st.lasting("zero_set")
        zeroed = st.lasting("zeroed")
        signs_done = st.lasting("signs_done")
        alpha1_done = st.lasting("alpha1_done")
        sums_done = st.lasting("sums_done")
        alpha2_done = st.lasting("alpha2_done")
        wd_split = st.lasting("wd_split")
        spare_done = st.lasting("spare_done")

        x_in = sem("x_in")
        ln_step = sem("ln_step")
        root = sem("root")
        xT_done = sem("xT_done")
        xT_hi_done = sem("xT_hi_done")
        xT_lo_done = sem("xT_lo_done")
        up_done = sem("up_done")
        gelu_done = sem("gelu_done")
        g_lo_done = sem("g_lo_done")
        down_done = sem("down_done")
        base_done = sem("base_done")
        h_done = sem("h_done")
        hT_f_done = sem("hT_f_done")
        hT_split = sem("hT_split")
        c_done = sem("c_done")
        c_hi_done = sem("c_hi_done")
        c_lo_done = sem("c_lo_done")
        y_done = sem("y_done")
        out_done = sem("out_done")
        stored = sem("stored")

        with nc.Block() as block:
            @block.sync
            def _(sp):
                sp.dma_start(ident[:], ident_d).then_inc(loaded, 16)
                sp.dma_start(w1r[:], w1_rows.rearrange("(m p) d -> p m d", p=P)).then_inc(loaded, 16)
                sp.dma_start(w1s[:], w1_t.rearrange("(c p) f -> p c f", p=P)).then_inc(loaded, 16)
                sp.dma_start(w2s[:], w2_t.rearrange("(m p) d -> p m d", p=P)).then_inc(loaded, 16)
                sp.dma_start(b1_c[:], b1).then_inc(loaded, 16)
                sp.dma_start(b2_row[:], b2).then_inc(loaded, 16)
                sp.dma_start(wd[:], wd_t).then_inc(loaded, 16)
                sp.dma_start(ln[:], ln_sb).then_inc(loaded, 16)
                with sp.Fori(0, B) as b:
                    sp.dma_start(x_t[:], tokens(x, b)).then_inc(x_in, 16)
                    sp.wait_ge(out_done, 2)
                    sp.dma_start(tokens(part, b), out[:]).then_inc(stored, 16)
                    sp.wait_ge(c_lo_done, 2)
                    sp.dma_start(latent(latents, b), c_parts[:].bitcast(F32)).then_inc(stored, 16)
                    sp.wait_ge(stored, 32)
                    st.lead(sp)
                sp.dma_start(latent(latents, B), latent(latents, 0)).then_inc(spare_done, 16)
                sp.wait_ge(spare_done, 16)

            @block.gpsimd
            def _(pool):
                nc.gpsimd.memset(ones[:], 1.0).then_inc(ones_set, 1)
                nc.gpsimd.memset(zero[:], 0.0).then_inc(zero_set, 1)
                pool.wait_ge(zero_set, 1)
                chunks = [buf.shape[0] * D // P // ZERO_W for buf in (rows, results)]
                for buf, n in zip((rows, results), chunks):
                    flat = buf.rearrange("(p r) d -> p (r d)", p=P)
                    for i in range(n):
                        pool.dma_start(flat[:, i * ZERO_W:(i + 1) * ZERO_W], zero[:]).then_inc(zeroed, 16)
                pool.wait_ge(loaded, 128)
                nc.gpsimd.tensor_copy(wd_hi[:], wd[:]).then_inc(wd_split, 1)
                pool.wait_ge(wd_split, 1)
                nc.gpsimd.tensor_tensor(wd_lo[:], wd[:], wd_hi[:], ALU.subtract).then_inc(wd_split, 1)
                with pool.Fori(0, B) as b:
                    pool.wait_ge(ln_step, LN_ALL)
                    nc.gpsimd.tensor_tensor(base[:], x_t[:], xn[:], ALU.add).then_inc(base_done, 1)
                    pool.wait_ge(base_done, 1)
                    for t in range(NT):
                        nc.gpsimd.tensor_tensor(base[:, t, :], base[:, t, :], b2_row[:],
                                                ALU.add).then_inc(base_done, 1)
                    for c in range(KC):
                        pool.wait_ge(hT_f_done, c + 1)
                        nc.gpsimd.tensor_copy(hT_hi[:, c, :], hT[:, c, :]).then_inc(hT_split, 1)
                        pool.wait_ge(hT_split, 2 * c + 1)
                        nc.gpsimd.tensor_tensor(hT_lo[:, c, :], hT[:, c, :], hT_hi[:, c, :],
                                                ALU.subtract).then_inc(hT_split, 1)
                    pool.wait_ge(base_done, 1 + NT)
                    pool.wait_ge(hT_split, 2 * KC)
                    st.meet(pool, POOL)
                pool.wait_ge(zeroed, 16 * sum(chunks))

            @block.scalar
            def _(act):
                act.wait_ge(loaded, 128)
                nc.scalar.activation(sign1[:], w1s[:], ACT.Sign).then_inc(signs_done, 1)
                nc.scalar.activation(sign2[:], w2s[:], ACT.Sign).then_inc(signs_done, 1)
                nc.scalar.activation(w2abs[:], w2s[:], ACT.Abs).then_inc(signs_done, 1)
                act.wait_ge(alpha1_done, 3)
                with act.Fori(0, B) as b:
                    act.wait_ge(ln_step, LN_VAR)
                    nc.scalar.activation(small[:, 1, :], small[:, 0, :], ACT.Sqrt).then_inc(root, 1)
                    for c in range(KC):
                        act.wait_ge(xT_done, c + 1)
                        nc.scalar.copy(xT_hi[:, c, :], pX[c][:]).then_inc(xT_hi_done, 1)
                    act.wait_ge(ln_step, LN_ALL + LN_VAR)
                    nc.scalar.activation(small[:, 1, :], small[:, 0, :], ACT.Sqrt).then_inc(root, 1)
                    for m in range(MC):
                        act.wait_ge(up_done, m + 1)
                        for dst in (g, g_hi):
                            nc.scalar.activation(dst[:, m, :], pU[m % 3][:], ACT.Gelu, bias=b1_c[:, m:m + 1],
                                                 scale=alpha1[:, m:m + 1]).then_inc(gelu_done, 1)
                    for i in range(2):
                        act.wait_ge(c_done, i + 1)
                        nc.scalar.copy(c_parts[:, i, :], pX[i][:]).then_inc(c_hi_done, 1)
                    act.wait_ge(gelu_done, 2 * MC)
                    act.wait_ge(c_hi_done, 2)
                    st.meet(act, ACTE)

            @block.vector
            def _(dve):
                dve.wait_ge(loaded, 128)
                nc.vector.tensor_reduce(alpha1[:], w1r[:], AX.X, ALU.add,
                                        apply_absolute_value=True).then_inc(alpha1_done, 1)
                dve.wait_ge(alpha1_done, 1)
                nc.vector.tensor_scalar(alpha1[:], alpha1[:], 1.0 / D, None, ALU.mult).then_inc(alpha1_done, 2)
                dve.wait_ge(sums_done, 1)
                for i in range(2):
                    nc.vector.tensor_scalar(alpha2[:, i, :], pY[0][:, 0, :], 1.0 / FF, None,
                                            ALU.mult).then_inc(alpha2_done, 1)
                dve.wait_ge(alpha2_done, 2)
                with dve.Fori(0, B) as b:
                    dve.wait_ge(x_in, 16)
                    layer_norm(nc, dve, x_t, xn, stats, mean_var, small[:, 0, :], small[:, 1, :],
                               small[:, 2, :], small[:, 3, :], None, (ln_step, 0), (root, 1))
                    for c in range(KC):
                        dve.wait_ge(xT_hi_done, c + 1)
                        nc.vector.tensor_tensor(xT_lo[:, c, :], pX[c][:], xT_hi[:, c, :],
                                                ALU.subtract).then_inc(xT_lo_done, 1)
                    dve.wait_ge(ln_step, LN_ALL)
                    layer_norm(nc, dve, xn, h, stats, mean_var, small[:, 0, :], small[:, 1, :],
                               small[:, 2, :], small[:, 3, :], None, (ln_step, LN_ALL), (root, 2))
                    for m in range(MC):
                        dve.wait_ge(gelu_done, 2 * m + 2)
                        nc.vector.tensor_tensor(g_lo[:, m, :], g[:, m, :], g_hi[:, m, :],
                                                ALU.subtract).then_inc(g_lo_done, 1)
                        if m == MC - 2:
                            for c in range(KC):
                                dve.wait_ge(h_done, c + 1)
                                nc.vector.tensor_scalar(hT[:, c, :], pX[c][:], ln[:, 0, c:c + 1], ln[:, 1, c:c + 1],
                                                        ALU.mult, ALU.add).then_inc(hT_f_done, 1)
                    for i in range(2):
                        dve.wait_ge(c_hi_done, i + 1)
                        nc.vector.tensor_tensor(c_parts[:, 2 + i, :], pX[i][:], c_parts[:, i, :],
                                                ALU.subtract).then_inc(c_lo_done, 1)
                    for i in range(2):
                        dve.wait_ge(down_done, i + 1)
                        nc.vector.tensor_tensor(y[:, 2 * i:2 * i + 2, :], pY[i][:], alpha2[:],
                                                ALU.mult).then_inc(y_done, 1)
                    dve.wait_ge(base_done, 1 + NT)
                    for i in range(2):
                        dve.wait_ge(y_done, i + 1)
                        nc.vector.tensor_tensor(out[:, 2 * i:2 * i + 2, :], y[:, 2 * i:2 * i + 2, :],
                                                base[:, 2 * i:2 * i + 2, :], ALU.add).then_inc(out_done, 1)
                    dve.wait_ge(out_done, 2)
                    dve.wait_ge(c_lo_done, 2)
                    st.meet(dve, DVE)

            @block.tensor
            def _(pe):
                pe.wait_ge(ones_set, 1)
                pe.wait_ge(signs_done, 3)
                for m in range(MC):
                    last = nc.tensor.matmul(pY[0][:, 0, :], ones[:], w2abs[:, m, :],
                                            start=(m == 0), stop=(m == MC - 1))
                last.then_inc(sums_done, 1)
                pe.wait_ge(alpha2_done, 2)
                pe.wait_ge(wd_split, 2)
                with pe.Fori(0, B) as b:
                    pe.wait_ge(ln_step, LN_ALL)
                    for c in range(KC):
                        for t in range(NT):
                            last = nc.tensor.transpose(pX[c][:, t * P:(t + 1) * P],
                                                       xn[:, t, c * P:(c + 1) * P], ident[:])
                        last.then_inc(xT_done, 1)
                    pe.wait_ge(xT_lo_done, KC)
                    for m in range(MC):
                        if m >= 3:
                            pe.wait_ge(gelu_done, 2 * (m - 2))
                        for c in range(KC):
                            w = sign1[:, c, m * P:(m + 1) * P]
                            nc.tensor.matmul(pU[m % 3][:], w, xT_lo[:, c, :], start=(c == 0), stop=False)
                            last = nc.tensor.matmul(pU[m % 3][:], w, xT_hi[:, c, :], start=False,
                                                    stop=(c == KC - 1))
                        last.then_inc(up_done, 1)
                        if m == MC - 3:
                            pe.wait_ge(ln_step, 2 * LN_ALL)
                            for c in range(KC):
                                for t in range(NT):
                                    last = nc.tensor.transpose(pX[c][:, t * P:(t + 1) * P],
                                                               h[:, t, c * P:(c + 1) * P], ident[:])
                                last.then_inc(h_done, 1)
                    for t in range(NT):
                        if t == 1:
                            pe.wait_ge(hT_split, 2 * KC)
                            for i in range(2):
                                for c in range(KC):
                                    cols = slice((2 * c + i) * P, (2 * c + i + 1) * P)
                                    last = product(nc, pX[i][:], wd_hi[:, cols], wd_lo[:, cols],
                                                   hT_hi[:, c, :], hT_lo[:, c, :], c == 0, c == KC - 1)
                                last.then_inc(c_done, 1)
                        for m in range(MC):
                            if t == 0:
                                pe.wait_ge(g_lo_done, m + 1)
                            for part_ in (g_lo, g_hi):
                                last = nc.tensor.matmul(pY[t // 2][:, t % 2, :], part_[:, m, t * P:(t + 1) * P],
                                                        sign2[:, m, :], start=(m == 0 and part_ is g_lo),
                                                        stop=(m == MC - 1 and part_ is g_hi))
                        if t % 2:
                            last.then_inc(down_done, 1)
                    pe.wait_ge(down_done, 2)
                    st.meet(pe, PE)


WQK = 192 * NP


def stage_a(nc, wq_t, wk_t, wv_t, wo_t, rope_c, rope_s, own_d, ident_d, part, latents, x1):
    with ExitStack() as ctx:
        st = Stage(nc, ctx, "a")
        sb, bank, sem = st.sb, st.bank, st.sem
        ident = sb("ident", [P, P])
        ones = sb("ones", [P, P], F32R)
        cos = sb("cos", [P, S])
        sin = sb("sin", [P, S])
        names = {"q": (wq_t, WQK), "k": (wk_t, WQK), "v": (wv_t, H0 * DH),
                 "o": (wo_t, NP * D)}
        w_hi = {n: sb(f"w{n}_hi", [P, f], F32R) for n, (_, f) in names.items()}
        w_lo = {n: sb(f"w{n}_lo", [P, f], F32R) for n, (_, f) in names.items()}
        v_hi = sb("v_hi", [P, NT, NP, 3, DH], F32R)
        v_lo = sb("v_lo", [P, NT, NP, 3, DH], F32R)
        own = sb("own", [P, 2])
        q_hi = sb("q_hi", [P, 2, 2, S], F32R)
        q_lo = sb("q_lo", [P, 2, 2, S], F32R)

        J = H0 * NT
        PR = 3

        loaded = st.lasting("loaded")
        w_split = st.lasting("w_split")
        w_lo_done = st.lasting("w_lo_done")
        first_in = st.lasting("first_in")
        fills = st.lasting("fills")
        c_in = sem("c_in")
        v_done = sem("v_done")
        v_hi_done = sem("v_hi_done")
        v_lo_done = sem("v_lo_done")
        pj_done = sem("pj_done")
        rot_mul = sem("rot_mul")
        rot_add = sem("rot_add")
        qk_hi_done = sem("qk_hi_done")
        qk_lo_done = sem("qk_lo_done")
        s_done = sem("s_done")
        max_done = sem("max_done")
        diag_done = sem("diag_done")
        st_done = sem("st_done")
        exp_done = sem("exp_done")
        p_lo_done = sem("p_lo_done")
        pv_done = sem("pv_done")
        inv_done = sem("inv_done")
        sums_out = sem("sums_out")
        norm_done = sem("norm_done")
        att_split = sem("att_split")
        o_done = sem("o_done")
        part_in = sem("part_in")
        out_done = sem("out_done")
        stored = sem("stored")

        with ExitStack() as ctx2:
            raw = {n: ctx2.enter_context(nc.sbuf_tensor(f"a_raw_{n}", [P, f], F32)) for n, (_, f) in names.items()}
            with nc.Block() as block:
                @block.sync
                def _(sp):
                    for n, (src, _) in names.items():
                        sp.dma_start(raw[n][:], src).then_inc(loaded, 16)
                    for dst, src in ((ident, ident_d), (cos, rope_c), (sin, rope_s), (own, own_d)):
                        sp.dma_start(dst[:], src).then_inc(loaded, 16)

                @block.scalar
                def _(act):
                    act.wait_ge(loaded, 16 * (len(names) + 4))
                    for n in names:
                        nc.scalar.copy(w_hi[n][:], raw[n][:]).then_inc(w_split, 1)

                @block.vector
                def _(dve):
                    for i, n in enumerate(names):
                        dve.wait_ge(w_split, i + 1)
                        nc.vector.tensor_tensor(w_lo[n][:], raw[n][:], w_hi[n][:],
                                                ALU.subtract).then_inc(w_lo_done, 1)
                    dve.wait_ge(w_lo_done, len(names))

                @block.gpsimd
                def _(pool):
                    nc.gpsimd.memset(ones[:].bitcast(F32), 1.0).then_inc(fills, 1)
                    nc.gpsimd.memset(v_hi[:, :, :, 1, :].bitcast(F32), 1.0).then_inc(fills, 1)
                    nc.gpsimd.memset(v_lo[:, :, :, 1, :].bitcast(F32), 0.0).then_inc(fills, 1)
                    pool.wait_ge(fills, 3)

        x_t = sb("x_t", [P, NT, D])
        x_out = sb("x_out", [P, NT, D])
        pr = x_out[:, :, :].rearrange("p (i t) d -> p i (t d)", i=2)
        latent_parts = sb("latent_parts", [P, 4, S], F32R)
        c_hi, c_lo = latent_parts[:, 0:2, :], latent_parts[:, 2:4, :]
        rot = sb("rot", [P, 3, S])
        k_hi = sb("k_hi", [P, 2, S], F32R)
        k_lo = sb("k_lo", [P, 2, S], F32R)
        row_max = sb("row_max", [P, H0, NT])
        diag = sb("diag", [P, 2, NT, P], F32R)
        pr_hi = sb("pr_hi", [P, PR, S], F32R)
        pr_lo = sb("pr_lo", [P, PR, S], F32R)
        den = sb("den", [P, S])
        att = sb("att", [P, 2, S])
        att_hi = sb("att_hi", [P, NP, S], F32R)
        att_lo = sb("att_lo", [P, NP, S], F32R)

        pG = [bank(f"pG{i}") for i in range(2)]
        pM = [bank(f"pM{i}") for i in range(2)]
        pT = [bank(f"pT{i}") for i in range(2)]
        pA = [bank(f"pA{i}") for i in range(2)]

        def head_cols(w, p, swapped):
            return w[:, 192 * p + 64 * swapped:192 * p + 64 * swapped + P]

        def v_cols(v, t, h):
            return v[:, t, h // 2, :, :].rearrange("p b d -> p (b d)")[:, 64 * (h % 2):64 * (h % 2) + P]

        with nc.Block() as block:
            @block.sync
            def _(sp):
                sp.dma_start(latent_parts[:].bitcast(F32), latent(latents, 0)).then_inc(first_in, 16)
                st.lead(sp)
                with sp.Fori(0, B) as b:
                    sp.dma_start(x_t[:], tokens(part, b)).then_inc(part_in, 16)
                    sp.wait_ge(pj_done, 4 * (NP - 1))
                    sp.dma_start(latent_parts[:].bitcast(F32), latent(latents, b + 1)).then_inc(c_in, 16)
                    sp.wait_ge(out_done, 2)
                    sp.dma_start(tokens(x1, b), x_out[:]).then_inc(stored, 16)
                    sp.wait_ge(stored, 16)
                    st.lead(sp)

            @block.tensor
            def _(pe):
                def project(u, p, i):
                    n = 4 * u + i
                    if n >= 2:
                        pe.wait_ge(rot_mul, n - 1)
                    w, c = ("q", 0) if i < 2 else ("k", 1)
                    product(nc, pG[i % 2][:], head_cols(w_hi[w], p, i % 2), head_cols(w_lo[w], p, i % 2),
                            c_hi[:, c, :], c_lo[:, c, :], True, True).then_inc(pj_done, 1)

                def scores(v, h, t, u):
                    p, n = h // 2, NT * v + t
                    if t == 0 and u is not None:
                        pe.wait_ge(qk_hi_done, 3 * u + 3)
                    if n >= 2:
                        pe.wait_ge(max_done, n - 1)
                    nc.tensor.matmul(pM[n % 2][:], q_hi[:, p % 2, h % 2, t * P:(t + 1) * P], k_hi[:, p % 2, :],
                                     start=True, stop=True).then_inc(s_done, 1)

                def values():
                    for i in range(2 * NT):
                        t, half = i // 2, i % 2
                        if i >= 2:
                            pe.wait_ge(v_lo_done, i - 1)
                        cols = slice(half * 512, half * 512 + 512)
                        ts = slice(t * P, (t + 1) * P)
                        product(nc, pG[half][:], c_hi[:, 1, ts], c_lo[:, 1, ts], w_hi["v"][:, cols],
                                w_lo["v"][:, cols], True, True).then_inc(v_done, 1)

                def shifted(j):
                    h, t = j // NT, j % NT
                    p = h // 2
                    ks = slice(t * P, (t + 1) * P)
                    if t == 0 and p >= 1:
                        pe.wait_ge(qk_lo_done, 3 * p)
                    if j >= 2:
                        pe.wait_ge(exp_done, 2 * (j - 1))
                    product(nc, pT[j % 2][:], k_hi[:, p % 2, ks], k_lo[:, p % 2, ks],
                            q_hi[:, p % 2, h % 2, :], q_lo[:, p % 2, h % 2, :], True, False)
                    if t == 0 and h >= 1:
                        pe.wait_ge(diag_done, NT * h)
                    nc.tensor.matmul(pT[j % 2][:], ones[:], diag[:, h % 2, :, :], start=False,
                                     stop=True).then_inc(st_done, 1)

                def weigh(j):
                    h, t = j // NT, j % NT
                    if t == 0 and h >= 2:
                        pe.wait_ge(sums_out, 2 * (h - 1))
                    pe.wait_ge(p_lo_done, j + 1)
                    product(nc, pA[h % 2][:], v_cols(v_hi, t, h), v_cols(v_lo, t, h), pr_hi[:, j % PR, :],
                            pr_lo[:, j % PR, :], t == 0, t == NT - 1).then_inc(pv_done, 1)

                pe.wait_ge(first_in, 16)
                for i in range(4):
                    project(0, 0, i)
                pe.wait_ge(rot_mul, 4)
                values()
                for t in range(NT):
                    scores(0, 0, t, 0)
                pe.wait_ge(s_done, NT)
                st.meet(pe, PE)
                with pe.Fori(0, B) as b:
                    for j in range(J + 2):
                        h, t = j // NT, j % NT
                        if j < J:
                            shifted(j)
                            if h % 2 == 0 and t < 2 and h // 2 + 1 < NP:
                                project(h // 2, h // 2 + 1, 2 * t)
                                project(h // 2, h // 2 + 1, 2 * t + 1)
                            if h + 1 < H0 and t < 3:
                                u = (h + 1) // 2 - 1 if h >= 1 else None
                                for i in ((0, 1), (2,), (3,))[t]:
                                    scores(h, h + 1, i, u)
                        if j == J - 1:
                            pe.wait_ge(c_in, 16)
                            for i in range(4):
                                project(NP - 1, 0, i)
                        if j >= 2:
                            weigh(j - 2)
                    pe.wait_ge(rot_mul, 4 * NP)
                    values()
                    for t in range(NT):
                        scores(H0 - 1, 0, t, NP - 1)
                    pe.wait_ge(exp_done, 2 * J)
                    pe.wait_ge(att_split, 2 * NP)
                    for t in range(NT):
                        ts = slice(t * P, (t + 1) * P)
                        for p in range(NP):
                            cols = slice(p * D, (p + 1) * D)
                            last = product(nc, pT[t // 2][:, (t % 2) * D:(t % 2 + 1) * D], att_hi[:, p, ts],
                                           att_lo[:, p, ts], w_hi["o"][:, cols], w_lo["o"][:, cols],
                                           p == 0, p == NP - 1)
                        if t % 2:
                            last.then_inc(o_done, 1)
                    pe.wait_ge(o_done, 2)
                    st.meet(pe, PE)

            @block.vector
            def _(dve):
                def rotate(u, i):
                    n = 4 * u + i
                    dve.wait_ge(pj_done, n + 1)
                    if n >= 2:
                        dve.wait_ge(rot_add, n // 2)
                    nc.vector.tensor_tensor(rot[:, i % 2, :], pG[i % 2][:], (cos, sin)[i % 2][:],
                                            ALU.mult).then_inc(rot_mul, 1)

                def q_low(u, p):
                    for i in range(2):
                        dve.wait_ge(qk_hi_done, 3 * u + i + 1)
                        nc.vector.scalar_tensor_tensor(out=q_lo[:, p % 2, i, :], in0=rot[:, 2, :],
                                                       scalar=own[:, i:i + 1], in1=q_hi[:, p % 2, i, :],
                                                       op0=ALU.mult, op1=ALU.subtract).then_inc(qk_lo_done, 1)

                def k_low(u, p):
                    dve.wait_ge(qk_hi_done, 3 * u + 3)
                    nc.vector.tensor_tensor(k_lo[:, p % 2, :], rot[:, 2, :], k_hi[:, p % 2, :],
                                            ALU.subtract).then_inc(qk_lo_done, 1)

                def maximum(v, h, t):
                    n = NT * v + t
                    dve.wait_ge(s_done, n + 1)
                    nc.vector.reduce_max(row_max[:, h, t:t + 1], pM[n % 2][:], AX.X).then_inc(max_done, 1)
                    if t == 0 and v >= 1:
                        dve.wait_ge(st_done, NT * v)
                    dve.wait_ge(max_done, n + 1)
                    nc.vector.tensor_scalar(diag[:, h % 2, t, :], ident[:], row_max[:, h, t:t + 1], -1.0,
                                            ALU.mult, ALU.mult).then_inc(diag_done, 1)

                def values_low():
                    for i in range(2 * NT):
                        t, half = i // 2, i % 2
                        ps = slice(half * NP // 2, (half + 1) * NP // 2)
                        dve.wait_ge(v_hi_done, i + 1)
                        nc.vector.tensor_tensor(v_lo[:, t, ps, 0:3:2, :],
                                                pG[half][:].rearrange("p (h o d) -> p h o d", o=2, d=DH),
                                                v_hi[:, t, ps, 0:3:2, :], ALU.subtract).then_inc(v_lo_done, 1)

                def normalise(p):
                    dve.wait_ge(sums_out, 4 * p + 4)
                    nc.vector.reciprocal(den[:], den[:]).then_inc(inv_done, 1)
                    dve.wait_ge(inv_done, p + 1)
                    nc.vector.tensor_tensor(att[:, p % 2, :], att[:, p % 2, :], den[:],
                                            ALU.mult).then_inc(norm_done, 1)

                for i in range(4):
                    rotate(0, i)
                q_low(0, 0)
                k_low(0, 0)
                values_low()
                for t in range(NT):
                    maximum(0, 0, t)
                dve.wait_ge(diag_done, NT)
                dve.wait_ge(v_lo_done, 2 * NT)
                dve.wait_ge(qk_lo_done, 3)
                st.meet(dve, DVE)
                with dve.Fori(0, B) as b:
                    for j in range(J):
                        h, t = j // NT, j % NT
                        nxt = h // 2 + 1
                        more = h % 2 == 0 and nxt < NP
                        if more and t < 2:
                            rotate(h // 2, 2 * t)
                            rotate(h // 2, 2 * t + 1)
                        if h + 1 < H0 and t < 3:
                            for i in ((0, 1), (2,), (3,))[t]:
                                maximum(h, h + 1, i)
                        if more and t == 1:
                            q_low(h // 2, nxt)
                        if more and t == 2:
                            k_low(h // 2, nxt)
                        if h % 2 and h >= 3 and t == 1:
                            normalise(h // 2 - 1)
                    for i in range(4):
                        rotate(NP - 1, i)
                    q_low(NP - 1, 0)
                    normalise(NP - 1)
                    k_low(NP - 1, 0)
                    values_low()
                    for t in range(NT):
                        maximum(H0 - 1, 0, t)
                    dve.wait_ge(part_in, 16)
                    for i in range(2):
                        dve.wait_ge(o_done, i + 1)
                        nc.vector.tensor_tensor(x_out[:, 2 * i:2 * i + 2, :],
                                                pT[i][:].rearrange("p (t d) -> p t d", d=D),
                                                x_t[:, 2 * i:2 * i + 2, :], ALU.add).then_inc(out_done, 1)
                    dve.wait_ge(out_done, 2)
                    dve.wait_ge(diag_done, NT * H0)
                    dve.wait_ge(v_lo_done, 2 * NT)
                    dve.wait_ge(qk_lo_done, 3 * NP)
                    st.meet(dve, DVE)

            @block.scalar
            def _(act):
                def q_high(u, p):
                    for i in range(2):
                        act.wait_ge(rot_add, 2 * u + 1)
                        if u >= 1:
                            act.wait_ge(st_done, 2 * NT * u)
                        nc.scalar.activation(q_hi[:, p % 2, i, :], rot[:, 2, :], ACT.Copy,
                                             scale=own[:, i:i + 1]).then_inc(qk_hi_done, 1)

                def k_high(u, p):
                    act.wait_ge(rot_add, 2 * u + 2)
                    nc.scalar.copy(k_hi[:, p % 2, :], rot[:, 2, :]).then_inc(qk_hi_done, 1)

                def values_high():
                    for i in range(2 * NT):
                        t, half = i // 2, i % 2
                        act.wait_ge(v_done, i + 1)
                        nc.scalar.copy(v_hi[:, t, half * NP // 2:(half + 1) * NP // 2, 0:3:2, :],
                                       pG[half][:].rearrange("p (h o d) -> p h o d", o=2, d=DH)).then_inc(v_hi_done, 1)

                def take_sums(h):
                    mine, other = slice(64 * (h % 2), 64 * (h % 2) + 64), slice(64 - 64 * (h % 2), 128 - 64 * (h % 2))
                    act.wait_ge(pv_done, NT * (h + 1))
                    if h >= 4:
                        act.wait_ge(att_split, 2 * (h // 2) - 2)
                    if h >= 2:
                        act.wait_ge(norm_done, h // 2)
                    nc.scalar.copy(att[mine, h // 2 % 2, :], pA[h % 2][mine, :]).then_inc(sums_out, 1)
                    nc.scalar.copy(den[mine, :], pA[h % 2][other, :]).then_inc(sums_out, 1)

                q_high(0, 0)
                k_high(0, 0)
                values_high()
                act.wait_ge(v_hi_done, 2 * NT)
                st.meet(act, ACTE)
                with act.Fori(0, B) as b:
                    for j in range(J):
                        h, t = j // NT, j % NT
                        nxt = h // 2 + 1
                        more = h % 2 == 0 and nxt < NP
                        act.wait_ge(st_done, j + 1)
                        if j >= 2:
                            act.wait_ge(p_lo_done, j - 1)
                        nc.scalar.activation(pr[:, j % 2, :], pT[j % 2][:], ACT.Exp, scale=SCALE).then_inc(exp_done, 1)
                        if j >= PR:
                            act.wait_ge(pv_done, j - PR + 1)
                        nc.scalar.activation(pr_hi[:, j % PR, :], pT[j % 2][:], ACT.Exp,
                                             scale=SCALE).then_inc(exp_done, 1)
                        if more and t == 1:
                            q_high(h // 2, nxt)
                        if more and t == 2:
                            k_high(h // 2, nxt)
                        if h % 2 == 0 and h >= 2:
                            if t == 0:
                                take_sums(h - 2)
                            if t == 3:
                                take_sums(h - 1)
                    take_sums(H0 - 2)
                    q_high(NP - 1, 0)
                    take_sums(H0 - 1)
                    k_high(NP - 1, 0)
                    values_high()
                    act.wait_ge(v_hi_done, 2 * NT)
                    act.wait_ge(qk_hi_done, 3 * NP)
                    act.wait_ge(sums_out, 2 * H0)
                    st.meet(act, ACTE)

            @block.gpsimd
            def _(pool):
                def add(n):
                    pool.wait_ge(rot_mul, 2 * n + 2)
                    if n >= 1:
                        pool.wait_ge(qk_lo_done, 3 * (n // 2) + (2 if n % 2 else 0))
                    nc.gpsimd.tensor_tensor(rot[:, 2, :], rot[:, 0, :], rot[:, 1, :], ALU.add).then_inc(rot_add, 1)

                def split_att(p):
                    pool.wait_ge(norm_done, p + 1)
                    nc.gpsimd.tensor_copy(att_hi[:, p, :], att[:, p % 2, :]).then_inc(att_split, 1)
                    pool.wait_ge(att_split, 2 * p + 1)
                    nc.gpsimd.tensor_tensor(att_lo[:, p, :], att[:, p % 2, :], att_hi[:, p, :],
                                            ALU.subtract).then_inc(att_split, 1)

                add(0)
                add(1)
                pool.wait_ge(rot_add, 2)
                st.meet(pool, POOL)
                with pool.Fori(0, B) as b:
                    for j in range(J):
                        h, t = j // NT, j % NT
                        more = h % 2 == 0 and h // 2 + 1 < NP
                        if more and t == 0:
                            add(h)
                        pool.wait_ge(exp_done, 2 * j + 2)
                        if j >= PR:
                            pool.wait_ge(pv_done, j - PR + 1)
                        nc.gpsimd.tensor_tensor(pr_lo[:, j % PR, :], pr[:, j % 2, :], pr_hi[:, j % PR, :],
                                                ALU.subtract).then_inc(p_lo_done, 1)
                        if more and t == 1:
                            add(h + 1)
                        if h % 2 and h >= 3 and t == 3:
                            split_att(h // 2 - 1)
                    add(2 * NP - 2)
                    add(2 * NP - 1)
                    split_att(NP - 1)
                    pool.wait_ge(rot_add, 2 * NP)
                    pool.wait_ge(att_split, 2 * NP)
                    st.meet(pool, POOL)


NC1 = KC
GW = 4 * (P + DE)


def stage_b(nc, wq_t, wk_t, wv_t, wo_t, wg, bg, own8_d, mask_d, before_d, ident_d, x1, xm_d, x2, sel_d):
    with ExitStack() as ctx:
        st = Stage(nc, ctx, "b")
        sb, bank, sem = st.sb, st.bank, st.sem
        ident = sb("ident", [P, P])
        own8 = sb("own8", [P, 8])
        mask = sb("mask", [P, P + P + 3 * P])
        before = sb("before", [P, NE, NE])
        bg_row = sb("bg_row", [P, NE])
        names = {"q": (wq_t, KC * D), "k": (wk_t, KC * D), "v": (wv_t, KC * D), "o": (wo_t, KC * D),
                 "g": (wg, KC * NE)}
        w_hi = {n: sb(f"w{n}_hi", [P, f], F32R) for n, (_, f) in names.items()}
        w_lo = {n: sb(f"w{n}_lo", [P, f], F32R) for n, (_, f) in names.items()}
        raw = {n: sb(f"raw_{n}", [P, f]) for n, (_, f) in names.items()}
        v_hi = sb("v_hi", [P, NT, 4, GW], F32R)
        v_lo = sb("v_lo", [P, NT, 4, GW], F32R)

        x_t = sb("x_t", [P, NT, D])
        xm = sb("xm", [P, NT, D])
        x_out = sb("x_out", [P, NT, D])
        stats = sb("stats", [P, NT, 6])
        mean_var = sb("mean_var", [P, NT, 2])
        small = sb("small", [P, 4, NT])
        xT_hi = sb("xT_hi", [P, KC, S], F32R)
        xT_lo = sb("xT_lo", [P, KC, S], F32R)
        neg = sb("neg", [P, 2, S])
        ex = sb("ex", [P, 2, S])
        feat = sb("feat", [P, 2 * NC1, S])
        q_hi = sb("q_hi", [P, NC1, S], F32R)
        q_lo = sb("q_lo", [P, NC1, S], F32R)
        kz_hi = sb("kz_hi", [P, 3, S], F32R)
        kz_lo = sb("kz_lo", [P, 3, S], F32R)
        RA = 4
        a_hi = sb("a_hi", [P, RA, S], F32R)
        a_lo = sb("a_lo", [P, RA, S], F32R)
        den = sb("den", [P, S])
        inv = sb("inv", [P, S])
        o = sb("o", [P, NC1, S])
        o_hi = sb("o_hi", [P, NC1, S], F32R)
        o_lo = sb("o_lo", [P, NC1, S], F32R)
        lg = sb("lg", [P, NT, NE])
        top = sb("top", [P, NT])
        tot = sb("tot", [P, NT])
        gate = sb("gate", [P, NT, NE])
        more = sb("more", [P, NT * NE, NE])
        same = sb("same", [P, NT * NE, NE])
        rank = sb("rank", [P, NT, NE])
        sel = sb("sel", [P, NT, NE])

        pG = [bank(f"pG{i}") for i in range(2)]
        pS = [bank(f"pS{i}") for i in range(4)]
        pO = [bank(f"pO{i}") for i in range(2)]

        loaded = st.lasting("loaded")
        w_split = st.lasting("w_split")
        w_lo_done = st.lasting("w_lo_done")
        zeros = st.lasting("zeros")
        fills = st.lasting("fills")
        x_in = sem("x_in")
        ln_step = sem("ln_step")
        root = sem("root")
        xm_out = sem("xm_out")
        xT_done = sem("xT_done")
        xT_hi_done = sem("xT_hi_done")
        xT_lo_done = sem("xT_lo_done")
        lg_done = sem("lg_done")
        gate_step = sem("gate_step")
        gate_exp = sem("gate_exp")
        v_done = sem("v_done")
        v_hi_done = sem("v_hi_done")
        v_lo_done = sem("v_lo_done")
        pj_done = sem("pj_done")
        neg_done = sem("neg_done")
        ex_done = sem("ex_done")
        feat_done = sem("feat_done")
        q_hi_done = sem("q_hi_done")
        q_lo_done = sem("q_lo_done")
        kz_hi_done = sem("kz_hi_done")
        kz_lo_done = sem("kz_lo_done")
        a_done = sem("a_done")
        a_hi_done = sem("a_hi_done")
        a_lo_done = sem("a_lo_done")
        mask_done = sem("mask_done")
        pv_done = sem("pv_done")
        den_done = sem("den_done")
        inv_done = sem("inv_done")
        o_done = sem("o_done")
        o_split = sem("o_split")
        y_done = sem("y_done")
        out_done = sem("out_done")
        stored = sem("stored")

        NJ = H1 * NT
        START = [0, P, 2 * P, 2 * P]
        def width(t):
            return S - START[t]

        with nc.Block() as block:
            @block.sync
            def _(sp):
                for n, (src, _) in names.items():
                    sp.dma_start(raw[n][:], src).then_inc(loaded, 16)
                for dst, src in ((ident, ident_d), (own8, own8_d), (mask, mask_d), (bg_row, bg)):
                    sp.dma_start(dst[:], src).then_inc(loaded, 16)
                sp.dma_start(before[:], before_d).then_inc(loaded, 16)
                with sp.Fori(0, B) as b:
                    sp.dma_start(x_t[:], tokens(x1, b)).then_inc(x_in, 16)
                    sp.wait_ge(ln_step, LN_ALL)
                    sp.dma_start(tokens(xm_d, b), xm[:]).then_inc(xm_out, 16)
                    sp.wait_ge(gate_step, 11)
                    sp.dma_start(tokens(sel_d, b), sel[:]).then_inc(xm_out, 16)
                    sp.wait_ge(out_done, 2)
                    sp.dma_start(tokens(x2, b), x_out[:]).then_inc(stored, 16)
                    sp.wait_ge(xm_out, 32)
                    sp.wait_ge(stored, 16)
                    st.lead(sp)

            @block.tensor
            def _(pe):
                def products(j):
                    h, t = j // NT, j % NT
                    c, w = h // 8, width(t)
                    ks, qs = slice(t * P, (t + 1) * P), slice(START[t], S)
                    if t == 0:
                        pe.wait_ge(q_lo_done, c + 1)
                        pe.wait_ge(kz_lo_done, h + 1)
                    if j >= 4:
                        pe.wait_ge(a_lo_done, j - 3)
                    product(nc, pS[j % 4][:, 0:w], kz_hi[:, h % 3, ks], kz_lo[:, h % 3, ks], q_hi[:, c, qs],
                            q_lo[:, c, qs], True, True).then_inc(a_done, 1)

                def weigh(j):
                    h, t = j // NT, j % NT
                    g, i, w = h // 4, h % 4, width(t)
                    if h % 4 == 0 and t == 0 and g >= 2:
                        pe.wait_ge(o_done, g - 1)
                    pe.wait_ge(mask_done, 2 * j + 2)
                    first, final = i == 0 and t == 0, i == 3 and t == NT - 1
                    cols = slice(i * P, (i + 1) * P)
                    product(nc, pO[g % 2][:, START[t]:S], v_hi[:, t, g, cols], v_lo[:, t, g, cols],
                            a_hi[:, j % RA, 0:w], a_lo[:, j % RA, 0:w], first, final).then_inc(pv_done, 1)

                pe.wait_ge(fills, NT)
                pe.wait_ge(w_lo_done, len(names))
                with pe.Fori(0, B) as b:
                    pe.wait_ge(ln_step, LN_ALL)
                    for c in range(KC):
                        for t in range(NT):
                            last = nc.tensor.transpose(pS[c][:, t * P:(t + 1) * P],
                                                       xm[:, t, c * P:(c + 1) * P], ident[:])
                        last.then_inc(xT_done, 1)
                    pe.wait_ge(xT_lo_done, KC)
                    for i in range(2 * NC1):
                        w = "q" if i < NC1 else "k"
                        if i >= 2:
                            pe.wait_ge(feat_done, i - 1)
                        for c in range(KC):
                            cols = slice(c * D + (i % NC1) * P, c * D + (i % NC1 + 1) * P)
                            last = product(nc, pG[i % 2][:], w_hi[w][:, cols], w_lo[w][:, cols],
                                           xT_hi[:, c, :], xT_lo[:, c, :], c == 0, c == KC - 1)
                        last.then_inc(pj_done, 1)
                    for t in range(NT):
                        ts = slice(t * P, (t + 1) * P)
                        for c in range(KC):
                            last = product(nc, pS[2][:, 8 * t:8 * t + 8], xT_hi[:, c, ts], xT_lo[:, c, ts],
                                           w_hi["g"][:, c * NE:(c + 1) * NE], w_lo["g"][:, c * NE:(c + 1) * NE],
                                           c == 0, c == KC - 1)
                    last.then_inc(lg_done, 1)
                    for t in range(NT):
                        ts = slice(t * P, (t + 1) * P)
                        pe.wait_ge(feat_done, 3 + t % 2)
                        if t >= 2:
                            pe.wait_ge(v_lo_done, t - 1)
                        for c in range(KC):
                            last = product(nc, pG[t % 2][:, 0:D], xT_hi[:, c, ts], xT_lo[:, c, ts],
                                           w_hi["v"][:, c * D:(c + 1) * D], w_lo["v"][:, c * D:(c + 1) * D],
                                           c == 0, c == KC - 1)
                        last.then_inc(v_done, 1)
                    pe.wait_ge(gate_step, 1)
                    pe.wait_ge(v_lo_done, NT)
                    for j in range(NJ + 3):
                        if j < NJ:
                            products(j)
                        if j >= 3:
                            weigh(j - 3)
                    for t in range(NT):
                        ts = slice(t * P, (t + 1) * P)
                        for c in range(NC1):
                            if t == 0:
                                pe.wait_ge(o_split, 2 * c + 2)
                            last = product(nc, pG[t // 2][:, (t % 2) * D:(t % 2 + 1) * D], o_hi[:, c, ts],
                                           o_lo[:, c, ts], w_hi["o"][:, c * D:(c + 1) * D],
                                           w_lo["o"][:, c * D:(c + 1) * D], c == 0, c == NC1 - 1)
                        if t % 2:
                            last.then_inc(y_done, 1)
                    pe.wait_ge(y_done, 2)
                    st.meet(pe, PE)

            @block.vector
            def _(dve):
                for i, n in enumerate(names):
                    dve.wait_ge(w_split, i + 1)
                    nc.vector.tensor_tensor(w_lo[n][:], raw[n][:], w_hi[n][:],
                                            ALU.subtract).then_inc(w_lo_done, 1)

                def features(i):
                    dve.wait_ge(pj_done, i + 1)
                    nc.vector.tensor_scalar(neg[:, i % 2, :], pG[i % 2][:], 0.0, None, ALU.min).then_inc(neg_done, 1)
                    dve.wait_ge(ex_done, i + 1)
                    nc.vector.scalar_tensor_tensor(out=feat[:, i, :], in0=pG[i % 2][:], scalar=0.0,
                                                   in1=ex[:, i % 2, :], op0=ALU.max,
                                                   op1=ALU.add).then_inc(feat_done, 1)

                def k_low(h):
                    dve.wait_ge(kz_hi_done, h + 1)
                    nc.vector.scalar_tensor_tensor(out=kz_lo[:, h % 3, :], in0=feat[:, NC1 + h // 8, :],
                                                   scalar=own8[:, h % 8:h % 8 + 1], in1=kz_hi[:, h % 3, :],
                                                   op0=ALU.mult, op1=ALU.subtract).then_inc(kz_lo_done, 1)

                def low(j):
                    w = width(j % NT)
                    dve.wait_ge(a_hi_done, j + 1)
                    nc.vector.tensor_tensor(a_lo[:, j % RA, 0:w], pS[j % 4][:, 0:w], a_hi[:, j % RA, 0:w],
                                            ALU.subtract).then_inc(a_lo_done, 1)

                def denominators(g):
                    rows = slice(64 * (g % 2), 64 * (g % 2) + 64)
                    dve.wait_ge(pv_done, 4 * NT * (g + 1))
                    nc.vector.tensor_scalar(den[rows, :], pO[g % 2][64:128, :], 1e-6, None,
                                            ALU.max).then_inc(den_done, 1)

                def quotients(c):
                    dve.wait_ge(den_done, 2 * c + 2)
                    nc.vector.reciprocal(inv[:], den[:]).then_inc(inv_done, 1)
                    dve.wait_ge(inv_done, c + 1)
                    for i in range(2):
                        rows = slice(64 * i, 64 * i + 64)
                        nc.vector.tensor_tensor(o[rows, c, :], pO[i][0:64, :], inv[rows, :],
                                                ALU.mult).then_inc(o_done, 1)

                def step(n, ins):
                    ins.then_inc(gate_step, 1)
                    dve.wait_ge(gate_step, n)

                def over(m, shape):
                    return m[:].unsqueeze(2).to_broadcast(shape)

                def choose():
                    by_e = [P, NT, NE]
                    step(2, nc.vector.tensor_reduce(top[:], lg[:], AX.X, ALU.max))
                    step(3, nc.vector.tensor_tensor(lg[:], lg[:], over(top, by_e), ALU.subtract))
                    dve.wait_ge(gate_exp, 1)
                    step(4, nc.vector.tensor_reduce(tot[:], gate[:], AX.X, ALU.add))
                    step(5, nc.vector.reciprocal(tot[:], tot[:]))
                    step(6, nc.vector.tensor_tensor(gate[:], gate[:], over(tot, by_e), ALU.mult))
                    for t in range(NT):
                        mine = gate[:, t, :].unsqueeze(2).to_broadcast([P, NE, NE])
                        others = gate[:, t, :].unsqueeze(1).to_broadcast([P, NE, NE])
                        es = slice(NE * t, NE * t + NE)
                        nc.vector.tensor_tensor(more[:, es, :], others, mine, ALU.is_gt)
                        last = nc.vector.tensor_tensor(same[:, es, :], others, mine, ALU.is_equal)
                    step(7, last)
                    for t in range(NT):
                        es = slice(NE * t, NE * t + NE)
                        last = nc.vector.tensor_tensor(same[:, es, :], same[:, es, :], before[:], ALU.mult)
                    step(8, last)
                    step(9, nc.vector.tensor_tensor(more[:], more[:], same[:], ALU.add))
                    step(10, nc.vector.tensor_reduce(rank[:].rearrange("p t e -> p (t e)"), more[:], AX.X, ALU.add))
                    step(11, nc.vector.tensor_scalar(sel[:], rank[:], 1.5, None, ALU.is_lt))

                with dve.Fori(0, B) as b:
                    dve.wait_ge(x_in, 16)
                    layer_norm(nc, dve, x_t, xm, stats, mean_var, small[:, 0, :], small[:, 1, :],
                               small[:, 2, :], small[:, 3, :], None, (ln_step, 0), (root, 1))
                    for c in range(KC):
                        dve.wait_ge(xT_hi_done, c + 1)
                        nc.vector.tensor_tensor(xT_lo[:, c, :], pS[c][:], xT_hi[:, c, :],
                                                ALU.subtract).then_inc(xT_lo_done, 1)
                    for i in range(2 * NC1):
                        features(i)
                    dve.wait_ge(lg_done, 1)
                    for t in range(NT):
                        last = nc.vector.tensor_tensor(lg[:, t, :], pS[2][:, 8 * t:8 * t + 8], bg_row[:], ALU.add)
                    step(1, last)
                    for t in range(NT):
                        dve.wait_ge(v_hi_done, t + 1)
                        blocks = lambda v: v[:, t, :, :].rearrange("p g (j c) -> p g j c", c=P + DE)[:, :, :, 0:DE]
                        nc.vector.tensor_tensor(blocks(v_lo), pG[t % 2][:, 0:D].rearrange("p (g j c) -> p g j c", j=4, c=DE),
                                                blocks(v_hi), ALU.subtract).then_inc(v_lo_done, 1)
                    k_low(0)
                    k_low(1)
                    for j in range(NJ + 4):
                        if j < NJ:
                            low(j)
                            if j % NT == 1 and j // NT + 2 < H1:
                                k_low(j // NT + 2)
                        if j == 2:
                            choose()
                        if j >= 4 * NT + 3 and (j - 3) % (4 * NT) == 0:
                            denominators((j - 3) // (4 * NT) - 1)
                        if j >= 8 * NT + 3 and (j - 3) % (8 * NT) == 0:
                            quotients((j - 3) // (8 * NT) - 1)
                    for i in range(2):
                        dve.wait_ge(y_done, i + 1)
                        nc.vector.tensor_tensor(x_out[:, 2 * i:2 * i + 2, :],
                                                pG[i][:].rearrange("p (t d) -> p t d", d=D),
                                                x_t[:, 2 * i:2 * i + 2, :], ALU.add).then_inc(out_done, 1)
                    dve.wait_ge(out_done, 2)
                    dve.wait_ge(kz_lo_done, H1)
                    st.meet(dve, DVE)

            @block.scalar
            def _(act):
                act.wait_ge(loaded, 16 * (len(names) + 5))
                for n in names:
                    nc.scalar.copy(w_hi[n][:], raw[n][:]).then_inc(w_split, 1)

                def k_high(h):
                    if h >= 3:
                        act.wait_ge(a_done, NT * (h - 2))
                    nc.scalar.activation(kz_hi[:, h % 3, :], feat[:, NC1 + h // 8, :], ACT.Copy,
                                         scale=own8[:, h % 8:h % 8 + 1]).then_inc(kz_hi_done, 1)

                with act.Fori(0, B) as b:
                    act.wait_ge(ln_step, LN_VAR)
                    nc.scalar.activation(small[:, 1, :], small[:, 0, :], ACT.Sqrt).then_inc(root, 1)
                    for c in range(KC):
                        act.wait_ge(xT_done, c + 1)
                        nc.scalar.copy(xT_hi[:, c, :], pS[c][:]).then_inc(xT_hi_done, 1)
                    for i in range(2 * NC1):
                        act.wait_ge(neg_done, i + 1)
                        nc.scalar.activation(ex[:, i % 2, :], neg[:, i % 2, :], ACT.Exp).then_inc(ex_done, 1)
                    act.wait_ge(feat_done, 2 * NC1)
                    for c in range(NC1):
                        nc.scalar.copy(q_hi[:, c, :], feat[:, c, :]).then_inc(q_hi_done, 1)
                    k_high(0)
                    k_high(1)
                    for t in range(NT):
                        act.wait_ge(v_done, t + 1)
                        nc.scalar.copy(v_hi[:, t, :, :].rearrange("p g (j c) -> p g j c", c=P + DE)[:, :, :, 0:DE],
                                       pG[t % 2][:, 0:D].rearrange("p (g j c) -> p g j c", j=4, c=DE)).then_inc(v_hi_done, 1)
                    for j in range(NJ):
                        h, t = j // NT, j % NT
                        w = width(t)
                        act.wait_ge(a_done, j + 1)
                        if j >= RA:
                            act.wait_ge(pv_done, j - RA + 1)
                        nc.scalar.copy(a_hi[:, j % RA, 0:w], pS[j % 4][:, 0:w]).then_inc(a_hi_done, 1)
                        if t == 1 and h + 2 < H1:
                            k_high(h + 2)
                        if j == 6:
                            act.wait_ge(gate_step, 3)
                            nc.scalar.activation(gate[:], lg[:], ACT.Exp).then_inc(gate_exp, 1)
                    act.wait_ge(a_hi_done, NJ)
                    act.wait_ge(kz_hi_done, H1)
                    st.meet(act, ACTE)

            @block.gpsimd
            def _(pool):
                for v in (v_hi, v_lo):
                    nc.gpsimd.memset(v[:].bitcast(F32), 0.0).then_inc(zeros, 1)
                pool.wait_ge(zeros, 2)
                for t in range(NT):
                    blocks = v_hi[:, t, :, :].rearrange("p g (j c) -> p g j c", c=P + DE)[:, :, :, 64:64 + DE]
                    nc.gpsimd.memset(blocks.bitcast(F32), 1.0).then_inc(fills, 1)
                pool.wait_ge(fills, NT)

                def split_o(c):
                    pool.wait_ge(o_done, 2 * c + 2)
                    nc.gpsimd.tensor_copy(o_hi[:, c, :], o[:, c, :]).then_inc(o_split, 1)
                    pool.wait_ge(o_split, 2 * c + 1)
                    nc.gpsimd.tensor_tensor(o_lo[:, c, :], o[:, c, :], o_hi[:, c, :],
                                            ALU.subtract).then_inc(o_split, 1)

                with pool.Fori(0, B) as b:
                    for c in range(NC1):
                        pool.wait_ge(q_hi_done, c + 1)
                        nc.gpsimd.tensor_tensor(q_lo[:, c, :], feat[:, c, :], q_hi[:, c, :],
                                                ALU.subtract).then_inc(q_lo_done, 1)
                    for j in range(NJ):
                        h, t = j // NT, j % NT
                        pool.wait_ge(a_lo_done, j + 1)
                        cut = slice(0, 2 * P) if t == 3 else slice(0, P)
                        m = mask[:, 0:2 * P] if t == 3 else mask[:, P:2 * P]
                        for a in (a_hi, a_lo):
                            nc.gpsimd.tensor_tensor(a[:, j % RA, cut], a[:, j % RA, cut], m, ALU.mult).then_inc(mask_done, 1)
                        if j == 8 * NT + 6:
                            split_o(0)
                    split_o(1)
                    pool.wait_ge(o_split, 2 * NC1)
                    pool.wait_ge(mask_done, 2 * NJ)
                    st.meet(pool, POOL)




def stage_c(nc, w1, w2, b1, b2, thresholds_d, lower_d, ident_d, xm_d, x2, sel_d, rows, results, out):
    I32 = mybir.dt.int32
    with ExitStack() as ctx:
        st = Stage(nc, ctx, "c")
        sb, bank, sem = st.sb, st.bank, st.sem
        ident = sb("ident", [P, P])
        slot_a = sb("slot_a", [P, TT], I32)
        slot_b = sb("slot_b", [P, TT], I32)
        trips = sb("trips", [P, NE], I32)
        first = sb("first", [P, NE], I32)
        all_rows = sb("all_rows", [P, TT, D])

        raw1 = sb("raw1", [P, KC, FF])
        raw2 = sb("raw2", [P, MC, D])
        raw_b1 = sb("raw_b1", [P, MC])
        raw_b2 = sb("raw_b2", [P, D])
        w1_hi = [sb(f"w1_hi{i}", [P, KC, FF], F32R) for i in range(2)]
        w1_lo = [sb(f"w1_lo{i}", [P, KC, FF], F32R) for i in range(2)]
        w2_hi = [sb(f"w2_hi{i}", [P, MC, D], F32R) for i in range(2)]
        w2_lo = [sb(f"w2_lo{i}", [P, MC, D], F32R) for i in range(2)]
        b1_c = [sb(f"b1_c{i}", [P, MC]) for i in range(2)]
        b2_row = [sb(f"b2_row{i}", [P, D]) for i in range(2)]

        raw_in = st.lasting("raw_in")
        split_hi = st.lasting("split_hi")
        split_lo = st.lasting("split_lo")

        def load_weights(sp, e):
            sp.dma_start(raw1[:], w1[bass.ds(e, 1), :, :].rearrange("o (c p) f -> p (o c) f", p=P)).then_inc(raw_in, 16)
            sp.dma_start(raw2[:], w2[bass.ds(e, 1), :, :].rearrange("o (m p) d -> p (o m) d", p=P)).then_inc(raw_in, 16)
            sp.dma_start(raw_b1[:], b1[bass.ds(e, 1), :, :].rearrange("o p m -> p (o m)")).then_inc(raw_in, 16)
            sp.dma_start(raw_b2[:], b2[bass.ds(e, 1), :, :].rearrange("o p d -> p (o d)")).then_inc(raw_in, 16)

        loaded = st.lasting("loaded")
        rows_in = st.lasting("rows_in")
        filled = st.lasting("filled")
        counted = st.lasting("counted")
        slot_step = st.lasting("slot_step")
        ones_set = st.lasting("ones_set")
        scattered = st.lasting("scattered")

        with ExitStack() as ctx2:
            def tmp(name, shape, dt=F32):
                return ctx2.enter_context(nc.sbuf_tensor(f"c_{name}", shape, dt))
            lower = tmp("lower", [P, P])
            ones = tmp("ones", [P, P])
            thresholds = tmp("thresholds", [P, NE, MAX_TRIPS - 1])
            sel = tmp("sel", [P, TT, NE])
            tot = tmp("tot", [P, TT, NE])
            upto = tmp("upto", [P, TT, NE])
            unit = tmp("unit", [P, TT])
            slot = tmp("slot", [P, TT, NE])
            pick = tmp("pick", [P, TT, NE])
            near = tmp("near", [P, 2, TT])
            above = tmp("above", [P, NE, MAX_TRIPS - 1])
            n_trips = tmp("n_trips", [P, NE])
            trips_upto = tmp("trips_upto", [P, NE])
            e_base = tmp("e_base", [P, NE])
            p_in = ctx2.enter_context(nc.psum_tensor("c_p_in", [P, TT, NE], F32))
            p_tot = ctx2.enter_context(nc.psum_tensor("c_p_tot", [P, TT, NE], F32))
            FAR = float(1 << 20)
            with nc.Block() as block:
                @block.sync
                def _(sp):
                    for dst, src in ((ident, ident_d), (lower, lower_d), (thresholds, thresholds_d),
                                     (sel, sel_d.rearrange("(t p) e -> p t e", p=P))):
                        sp.dma_start(dst[:], src).then_inc(loaded, 16)
                    sp.dma_start(all_rows[:], xm_d.rearrange("(t p) d -> p t d", p=P)).then_inc(rows_in, 16)
                    load_weights(sp, 0)

                @block.scalar
                def _(act):
                    act.wait_ge(raw_in, 64)
                    for dst, src in ((w1_hi[0], raw1), (w2_hi[0], raw2), (b1_c[0], raw_b1), (b2_row[0], raw_b2)):
                        nc.scalar.copy(dst[:], src[:]).then_inc(split_hi, 1)
                    act.wait_ge(split_hi, 4)
                    act.sem_clear(raw_in)

                @block.tensor
                def _(pe):
                    pe.wait_ge(loaded, 64)
                    pe.wait_ge(ones_set, 1)
                    nc.tensor.matmul(p_in[:], lower[:], sel[:], start=True, stop=True).then_inc(counted, 1)
                    nc.tensor.matmul(p_tot[:], ones[:], sel[:], start=True, stop=True).then_inc(counted, 1)

                @block.vector
                def _(dve):
                    def step(n, ins):
                        ins.then_inc(slot_step, 1)
                        dve.wait_ge(slot_step, n)
                    step(1, nc.vector.memset(unit[:], 1.0))
                    dve.wait_ge(counted, 2)
                    step(2, nc.vector.tensor_copy(tot[:], p_tot[:]))
                    for e in range(NE):
                        last = nc.vector.tensor_tensor_scan(out=upto[:, :, e], data0=unit[:], data1=tot[:, :, e],
                                                            initial=0.0, op0=ALU.mult, op1=ALU.add)
                    step(3, last)
                    step(4, nc.vector.tensor_tensor(
                        above[:], upto[:, TT - 1, :].unsqueeze(2).to_broadcast([P, NE, MAX_TRIPS - 1]),
                        thresholds[:], ALU.is_gt))
                    step(5, nc.vector.tensor_reduce(n_trips[:], above[:], AX.X, ALU.add))
                    step(6, nc.vector.tensor_scalar(n_trips[:], n_trips[:], 1.0, None, ALU.add))
                    step(7, nc.vector.tensor_tensor_scan(out=trips_upto[:], data0=unit[:, 0:NE], data1=n_trips[:],
                                                         initial=0.0, op0=ALU.mult, op1=ALU.add))
                    step(8, nc.vector.tensor_tensor(e_base[:], trips_upto[:], n_trips[:], ALU.subtract))
                    nc.vector.tensor_copy(trips[:], n_trips[:])
                    step(9, nc.vector.tensor_copy(first[:], e_base[:]))
                    step(10, nc.vector.tensor_scalar(e_base[:], e_base[:], float(TILE), None, ALU.mult))
                    step(11, nc.vector.tensor_tensor(slot[:], upto[:], tot[:], ALU.subtract))
                    step(12, nc.vector.tensor_tensor(slot[:], slot[:], p_in[:], ALU.add))
                    step(13, nc.vector.tensor_tensor(slot[:], slot[:], e_base[:].unsqueeze(1).to_broadcast([P, TT, NE]),
                                                     ALU.add))
                    step(14, nc.vector.scalar_tensor_tensor(out=pick[:], in0=slot[:], scalar=-FAR, in1=sel[:],
                                                            op0=ALU.add, op1=ALU.mult))
                    step(15, nc.vector.tensor_reduce(near[:, 0, :], pick[:], AX.X, ALU.min))
                    step(16, nc.vector.tensor_scalar(slot_a[:], near[:, 0, :], FAR, None, ALU.add))
                    step(17, nc.vector.tensor_tensor(pick[:], slot[:], sel[:], ALU.mult))
                    step(18, nc.vector.tensor_reduce(near[:, 1, :], pick[:], AX.X, ALU.max))
                    step(19, nc.vector.tensor_copy(slot_b[:], near[:, 1, :]))
                    for i, (dst, src, hi) in enumerate(((w1_lo[0], raw1, w1_hi[0]), (w2_lo[0], raw2, w2_hi[0]))):
                        dve.wait_ge(split_hi, i + 1)
                        nc.vector.tensor_tensor(dst[:], src[:], hi[:], ALU.subtract).then_inc(split_lo, 1)
                    dve.wait_ge(split_lo, 2)

                @block.gpsimd
                def _(pool):
                    nc.gpsimd.memset(ones[:], 1.0).then_inc(ones_set, 1)
                    pool.wait_ge(slot_step, 19)
                    pool.wait_ge(rows_in, 16)
                    for t in range(TT):
                        for s in (slot_a, slot_b):
                            pool.indirect_dma_start(out=rows, out_offset=bass.IndirectOffsetOnAxis(ap=s[:, t:t + 1], axis=0),
                                                    in_=all_rows[:, t, :], in_offset=None).then_inc(scattered, 16)
                    pool.wait_ge(scattered, 32 * TT)

        x_t = sb("x_t", [P, NT, D])
        xT_hi = sb("xT_hi", [P, KC, S], F32R)
        xT_lo = sb("xT_lo", [P, KC, S], F32R)
        RH = 4
        h = sb("h", [P, RH, S])
        h_hi = sb("h_hi", [P, RH, S], F32R)
        h_lo = sb("h_lo", [P, RH, S], F32R)
        y = sb("y", [P, NT, D])
        pX = bank("pX")
        pU = [bank(f"pU{i}") for i in range(3)]
        pY = [bank(f"pY{i}", (P, D)) for i in range(NT)]

        w_split = st.lasting("w_split")
        w_ready = st.lasting("w_ready")
        pool_go = st.lasting("pool_go")
        stored = st.lasting("stored")
        x_in = sem("x_in")
        xT_done = sem("xT_done")
        xT_hi_done = sem("xT_hi_done")
        xT_lo_done = sem("xT_lo_done")
        up_done = sem("up_done")
        relu_done = sem("relu_done")
        h_lo_done = sem("h_lo_done")
        down_done = sem("down_done")
        y_done = sem("y_done")
        TILE_WORKERS = 3

        def per_expert(eng, run):
            with eng.Fori(0, NE // 2 - 1) as half:
                run(0, half * 2, True)
                run(1, half * 2 + 1, True)
            run(0, NE - 2, True)
            run(1, NE - 1, False)

        def tiles_of(eng, e):
            return eng.value_load(trips[0:1, bass.ds(e, 1)], min_val=1, max_val=MAX_TRIPS)

        with nc.Block() as block:
            @block.sync
            def _(sp):
                def load(at):
                    sp.dma_start(x_t[:], rows[bass.ds(at, TILE), :].rearrange("(t p) d -> p t d", p=P)).then_inc(x_in, 16)

                def run(parity, e, more):
                    if more:
                        load_weights(sp, e + 1)
                    start = sp.value_load(first[0:1, bass.ds(e, 1)], min_val=0, max_val=TILES - 1)
                    with sp.Fori(0, tiles_of(sp, e)) as i:
                        sp.wait_ge(stored, 16)
                        sp.sem_clear(stored)
                        at = nc.s_assert_le(start + i, TILES - 1) * TILE
                        load(at + TILE)
                        sp.wait_ge(y_done, NT)
                        sp.dma_start(results[bass.ds(at, TILE), :].rearrange("(t p) d -> p t d", p=P),
                                     y[:]).then_inc(stored, 16)
                        st.lead(sp, TILE_WORKERS)
                    if more:
                        sp.wait_ge(w_ready, 1)
                        sp.sem_clear(w_ready)
                        st.lead(sp, TILE_WORKERS)
                        sp.sem_inc(pool_go, 1)

                load(0)
                st.lead(sp, TILE_WORKERS)
                sp.sem_inc(stored, 16)
                per_expert(sp, run)
                sp.wait_ge(stored, 16)

            @block.tensor
            def _(pe):
                def transpose(c):
                    if c:
                        pe.wait_ge(xT_lo_done, 1)
                    else:
                        pe.wait_ge(x_in, 16)
                    for t in range(NT):
                        last = nc.tensor.transpose(pX[:, t * P:(t + 1) * P], x_t[:, t, c * P:(c + 1) * P], ident[:])
                    last.then_inc(xT_done, 1)

                def up(w, m):
                    if m >= 3:
                        pe.wait_ge(relu_done, 2 * (m - 2))
                    for c in range(KC):
                        cols = slice(m * P, (m + 1) * P)
                        last = product(nc, pU[m % 3][:], w1_hi[w][:, c, cols], w1_lo[w][:, c, cols], xT_hi[:, c, :],
                                       xT_lo[:, c, :], c == 0, c == KC - 1)
                    last.then_inc(up_done, 1)

                def down(w, m):
                    pe.wait_ge(h_lo_done, m + 1)
                    for t in range(NT):
                        ts = slice(t * P, (t + 1) * P)
                        last = product(nc, pY[t][:], h_hi[:, m % RH, ts], h_lo[:, m % RH, ts], w2_hi[w][:, m, :],
                                       w2_lo[w][:, m, :], m == 0, m == MC - 1)
                    last.then_inc(down_done, 1)

                def run(parity, e, more):
                    with pe.Fori(0, tiles_of(pe, e)):
                        for m in range(MC):
                            up(parity, m)
                            if m >= 2:
                                down(parity, m - 2)
                        transpose(0)
                        down(parity, MC - 2)
                        transpose(1)
                        down(parity, MC - 1)
                        pe.wait_ge(down_done, MC)
                        st.meet(pe, PE)
                    if more:
                        st.meet(pe, PE)

                transpose(0)
                transpose(1)
                st.meet(pe, PE)
                per_expert(pe, run)

            @block.scalar
            def _(act):
                def x_high():
                    for c in range(KC):
                        act.wait_ge(xT_done, c + 1)
                        nc.scalar.copy(xT_hi[:, c, :], pX[:]).then_inc(xT_hi_done, 1)

                def run(parity, e, more):
                    with act.Fori(0, tiles_of(act, e)):
                        for m in range(MC):
                            act.wait_ge(up_done, m + 1)
                            if m >= RH:
                                act.wait_ge(down_done, m - RH + 1)
                            for dst in (h, h_hi):
                                nc.scalar.activation(dst[:, m % RH, :], pU[m % 3][:], ACT.Relu,
                                                     bias=b1_c[parity][:, m:m + 1]).then_inc(relu_done, 1)
                        x_high()
                        act.wait_ge(relu_done, 2 * MC)
                        act.wait_ge(xT_hi_done, KC)
                        st.meet(act, ACTE)
                    if more:
                        st.meet(act, ACTE)

                x_high()
                act.wait_ge(xT_hi_done, KC)
                st.meet(act, ACTE)
                per_expert(act, run)

            @block.vector
            def _(dve):
                def x_low():
                    for c in range(KC):
                        dve.wait_ge(xT_hi_done, c + 1)
                        nc.vector.tensor_tensor(xT_lo[:, c, :], pX[:], xT_hi[:, c, :],
                                                ALU.subtract).then_inc(xT_lo_done, 1)

                def run(parity, e, more):
                    with dve.Fori(0, tiles_of(dve, e)):
                        for m in range(MC):
                            dve.wait_ge(relu_done, 2 * m + 2)
                            if m >= RH:
                                dve.wait_ge(down_done, m - RH + 1)
                            nc.vector.tensor_tensor(h_lo[:, m % RH, :], h[:, m % RH, :], h_hi[:, m % RH, :],
                                                    ALU.subtract).then_inc(h_lo_done, 1)
                        x_low()
                        dve.wait_ge(down_done, MC)
                        for t in range(NT):
                            nc.vector.tensor_tensor(y[:, t, :], pY[t][:], b2_row[parity][:], ALU.add).then_inc(y_done, 1)
                        dve.wait_ge(y_done, NT)
                        dve.wait_ge(xT_lo_done, KC)
                        st.meet(dve, DVE)
                    if more:
                        st.meet(dve, DVE)

                x_low()
                dve.wait_ge(xT_lo_done, KC)
                st.meet(dve, DVE)
                per_expert(dve, run)

            @block.gpsimd
            def _(pool):
                def run(parity, e, more):
                    if not more:
                        return
                    w = 1 - parity
                    pool.wait_ge(raw_in, 64)
                    pool.sem_clear(raw_in)
                    for dst, src in ((w1_hi[w], raw1), (w2_hi[w], raw2), (b1_c[w], raw_b1), (b2_row[w], raw_b2)):
                        nc.gpsimd.tensor_copy(dst[:], src[:]).then_inc(w_split, 1)
                    for i, (dst, src, hi) in enumerate(((w1_lo[w], raw1, w1_hi[w]), (w2_lo[w], raw2, w2_hi[w]))):
                        pool.wait_ge(w_split, 4)
                        nc.gpsimd.tensor_tensor(dst[:], src[:], hi[:], ALU.subtract).then_inc(w_split, 1)
                    pool.wait_ge(w_split, 6)
                    pool.sem_clear(w_split)
                    pool.sem_inc(w_ready, 1)
                    pool.wait_ge(pool_go, 1)
                    pool.sem_clear(pool_go)

                per_expert(pool, run)

        with ExitStack() as ctx2:
            RG = 4
            ya = ctx2.enter_context(nc.sbuf_tensor("c_ya", [P, RG, D], F32))
            yb = ctx2.enter_context(nc.sbuf_tensor("c_yb", [P, RG, D], F32))
            x2_in = st.lasting("x2_in")
            ya_in = [st.lasting(f"ya_in{i}") for i in range(RG)]
            yb_in = [st.lasting(f"yb_in{i}") for i in range(RG)]
            added = st.lasting("added")
            out_stored = st.lasting("out_stored")
            with nc.Block() as block:
                @block.sync
                def _(sp):
                    sp.dma_start(all_rows[:], x2.rearrange("(t p) d -> p t d", p=P)).then_inc(x2_in, 16)
                    for i in range(TT // NT):
                        sp.wait_ge(added, 2 * NT * (i + 1))
                        sp.dma_start(tokens(out, i), all_rows[:, NT * i:NT * i + NT, :]).then_inc(out_stored, 16)
                    sp.wait_ge(out_stored, 16 * (TT // NT))

                @block.gpsimd
                def _(pool):
                    for t in range(TT):
                        if t >= RG:
                            pool.wait_ge(added, 2 * (t - RG + 1))
                        for dst, s, done in ((ya, slot_a, ya_in), (yb, slot_b, yb_in)):
                            pool.indirect_dma_start(out=dst[:, t % RG, :], out_offset=None, in_=results,
                                                    in_offset=bass.IndirectOffsetOnAxis(ap=s[:, t:t + 1], axis=0)
                                                    ).then_inc(done[t % RG], 16)

                @block.vector
                def _(dve):
                    dve.wait_ge(x2_in, 16)
                    for t in range(TT):
                        for k, (src, done) in enumerate(((ya, ya_in), (yb, yb_in))):
                            dve.wait_ge(done[t % RG], 16 * (t // RG + 1))
                            if k:
                                dve.wait_ge(added, 2 * t + 1)
                            nc.vector.tensor_tensor(all_rows[:, t, :], all_rows[:, t, :], src[:, t % RG, :],
                                                    ALU.add).then_inc(added, 1)


def rope_tables():
    inv_freq = 1.0 / 10000.0 ** (np.arange(0, DH, 2, dtype=np.float32) / DH)
    freqs = np.outer(np.arange(S, dtype=np.float32), inv_freq)[:, (2 * np.arange(32)) % 32].T
    c, s = np.cos(freqs), np.sin(freqs)
    return (np.ascontiguousarray(np.concatenate([c, c, c, c])).astype(np.float32),
            np.ascontiguousarray(np.concatenate([-s, -s, s, s])).astype(np.float32))


def lay_out(a):
    even, odd = np.arange(0, DH, 2), np.arange(1, DH, 2)
    of_pair = lambda f: np.concatenate([f, DH + f])
    rows = (2 * DH * np.arange(NP)[:, None] + np.concatenate([of_pair(even), of_pair(odd), of_pair(even)])[None]).ravel()
    by_chunk = lambda m: m.reshape(-1, P, m.shape[-1]).transpose(1, 0, 2).reshape(P, -1)
    down = np.stack([a["L0_attn_w_down_q"], a["L0_attn_w_down_kv"]])
    cos, sin = rope_tables()
    return {
        "x": a["L0_attn_x"].reshape(T, D),
        "w1_rows": a["L0_ffn_w1"],
        "w1_t": a["L0_ffn_w1"].T,
        "w2_t": a["L0_ffn_w2"].T,
        "b1": a["L0_ffn_b1"].reshape(MC, P).T,
        "b2": np.broadcast_to(a["L0_ffn_b2"], (P, D)),
        "ident_d": np.eye(P, dtype=np.float32),
        "wd_t": down.reshape(2, P, KC, P).transpose(3, 2, 0, 1).reshape(P, -1),
        "wq_t": a["L0_attn_w_up_q"][rows].T,
        "wk_t": a["L0_attn_w_up_k"][rows].T,
        "wv_t": a["L0_attn_w_up_v"].T,
        "wo_t": by_chunk(a["L0_attn_w_out"].T),
        "ln_sb": np.stack([a["L0_attn_ln_scale"].reshape(KC, P), a["L0_attn_ln_bias"].reshape(KC, P)]).transpose(2, 0, 1),
        "rope_c": cos,
        "rope_s": sin,
        "own_d": np.ascontiguousarray(np.tile(np.repeat(np.eye(2, dtype=np.float32), 32, axis=0), (2, 1))),
        "l1_wq": by_chunk(a["L1_attn_Wq"].T),
        "l1_wk": by_chunk(a["L1_attn_Wk"].T),
        "l1_wv": by_chunk(a["L1_attn_Wv"].T),
        "l1_wo": by_chunk(a["L1_attn_Wo"].T),
        "wg": by_chunk(a["L1_ffn_Wg"]),
        "bg": np.broadcast_to(a["L1_ffn_bg"], (P, NE)),
        "own8_d": np.repeat(np.eye(8, dtype=np.float32), DE, axis=0),
        "mask_d": np.concatenate([np.zeros((P, P)), np.triu(np.ones((P, P))), np.ones((P, 3 * P))], 1).astype(np.float32),
        "e_w1": a["L1_ffn_W1"],
        "e_w2": a["L1_ffn_W2"],
        "e_b1": a["L1_ffn_b1"].reshape(NE, MC, P).transpose(0, 2, 1),
        "e_b2": np.broadcast_to(a["L1_ffn_b2"][:, None, :], (NE, P, D)),
        "thresholds": np.broadcast_to(TILE * np.arange(1, MAX_TRIPS, dtype=np.float32), (P, NE, MAX_TRIPS - 1)),
        "lower_d": np.triu(np.ones((P, P), np.float32), 1),
        "before_d": np.broadcast_to(np.tril(np.ones((NE, NE)), -1).astype(np.float32), (P, NE, NE)),
    }


STAGES = (
    (stage_f, ("x", "w1_rows", "w1_t", "w2_t", "b1", "b2", "wd_t", "ln_sb", "ident_d"),
     ("part", "latents", "rows", "results")),
    (stage_a, ("wq_t", "wk_t", "wv_t", "wo_t", "rope_c", "rope_s", "own_d", "ident_d"),
     ("part", "latents", "x1")),
    (stage_b, ("l1_wq", "l1_wk", "l1_wv", "l1_wo", "wg", "bg", "own8_d", "mask_d", "before_d", "ident_d"),
     ("x1", "xm", "x2", "sel")),
    (stage_c, ("e_w1", "e_w2", "e_b1", "e_b2", "thresholds", "lower_d", "ident_d"),
     ("xm", "x2", "sel", "rows", "results", "out")),
)
SCRATCH = {"part": (T, D), "x1": (T, D), "xm": (T, D), "x2": (T, D), "sel": (T, NE),
           "latents": ((B + 1) * P, 4 * S), "rows": ((TILES + 1) * TILE, D), "results": (TILES * TILE, D)}


def program(nc, aps):
    for stage, inputs, between in STAGES:
        stage(nc, *(aps[n] for n in inputs + between))


def kernel(**inputs):
    import concourse.bacc as bacc
    from concourse.bass_utils import run_bass_kernel_spmd

    arrays = {n: np.ascontiguousarray(v) for n, v in lay_out({k: np.asarray(v) for k, v in inputs.items()}).items()}
    nc = bacc.Bacc("TRN2", target_bir_lowering=False, num_devices=1)
    aps = {n: nc.dram_tensor(f"in_{n}", a.shape, F32, kind="ExternalInput").ap() for n, a in arrays.items()}
    for n, shape in SCRATCH.items():
        aps[n] = nc.dram_tensor(f"mid_{n}", shape, F32, kind="Internal").ap()
    aps["out"] = nc.dram_tensor("out_x", (T, D), F32, kind="ExternalOutput").ap()
    program(nc, aps)
    result = run_bass_kernel_spmd(nc, [{f"in_{n}": a for n, a in arrays.items()}], core_ids=[0])
    return result.results[0]["out_x"].reshape(B, S, D)
```

```python
from contextlib import ExitStack

import numpy as np

import concourse.bass as bass
from concourse import mybir

F32 = mybir.dt.float32
F32R = mybir.dt.float32r
ALU = mybir.AluOpType
ACT = mybir.ActivationFunctionType
AX = mybir.AxisListType

P = 128
B, S, D = 8, 512, 256
T = B * S
NT = S // P
KC = D // P
H0, DH = 16, 64
NP = H0 // 2
FF = 1024
MC = FF // P
H1, DE = 16, 16
NE = 8
TT = T // P
TILE = 512
TILES = 2 * T // TILE + NE
MAX_TRIPS = T // TILE
ZERO_W = (TILES + 1) * TILE * D // P // B
EPS = 1e-5
SCALE = 1.0 / 8.0
WORKERS = 4
PE, DVE, ACTE, POOL = range(WORKERS)


class Stage:

    def __init__(self, nc, ctx, name):
        self.nc, self.ctx, self.name = nc, ctx, name
        self.cleared = []
        self.arrived = self.lasting("arrived")
        self.go = [self.lasting(f"go{i}") for i in range(WORKERS)]

    def sb(self, name, shape, dt=F32):
        return self.ctx.enter_context(self.nc.sbuf_tensor(f"{self.name}_{name}", shape, dt))

    def bank(self, name, shape=(P, 512)):
        return self.ctx.enter_context(self.nc.psum_tensor(f"{self.name}_{name}", list(shape), F32))

    def lasting(self, name):
        return self.ctx.enter_context(self.nc.semaphore(f"{self.name}_{name}"))

    def sem(self, name):
        s = self.lasting(name)
        self.cleared.append(s)
        return s

    def meet(self, eng, worker):
        eng.sem_inc(self.arrived, 1)
        eng.wait_ge(self.go[worker], 1)
        eng.sem_clear(self.go[worker])

    def lead(self, eng, workers=WORKERS):
        eng.wait_ge(self.arrived, workers)
        for s in self.cleared:
            eng.sem_clear(s)
        eng.sem_clear(self.arrived)
        for go in self.go[:workers]:
            eng.sem_inc(go, 1)


def product(nc, out, l_hi, l_lo, r_hi, r_lo, start, stop, **kw):
    nc.tensor.matmul(out, l_lo, r_hi, start=start, stop=False, **kw)
    nc.tensor.matmul(out, l_hi, r_lo, start=False, stop=False, **kw)
    return nc.tensor.matmul(out, l_hi, r_hi, start=False, stop=stop, **kw)


def layer_norm(nc, dve, x, out, stats, mean_var, var_eps, std, rstd, shift, ready, done, root_done):
    sem, n = done
    tiles = x.shape[1]
    for t in range(tiles):
        nc.vector.bn_stats(stats[:, t, :], x[:, t, :]).then_inc(sem, 1)
    dve.wait_ge(sem, n + tiles)
    for t in range(tiles):
        nc.vector.bn_aggr(mean_var[:, t, :], stats[:, t, :]).then_inc(sem, 1)
    dve.wait_ge(sem, n + 2 * tiles)
    nc.vector.tensor_scalar(var_eps, mean_var[:, :, 1], EPS, None, ALU.add).then_inc(sem, 1)
    dve.wait_ge(*root_done)
    nc.vector.reciprocal(rstd, std).then_inc(sem, 1)
    dve.wait_ge(sem, n + 2 * tiles + 2)
    nc.vector.scalar_tensor_tensor(out=shift, in0=mean_var[:, :, 0], scalar=-1.0, in1=rstd,
                                   op0=ALU.mult, op1=ALU.mult).then_inc(sem, 1)
    dve.wait_ge(sem, n + 2 * tiles + 3)
    for t in range(tiles):
        nc.vector.tensor_scalar(out[:, t, :], x[:, t, :], rstd[:, t:t + 1], shift[:, t:t + 1],
                                ALU.mult, ALU.add).then_inc(sem, 1)
    return n + 3 * tiles + 3


LN_VAR = 2 * NT + 1
LN_ALL = 3 * NT + 3


def tokens(ap, b):
    return ap[bass.ds(b * S, S), :].rearrange("(t p) d -> p t d", p=P)


def latent(ap, b):
    return ap[bass.ds(b * P, P), :].rearrange("p (i s) -> p i s", i=4)


def stage_f(nc, x, w1_rows, w1_t, w2_t, b1, b2, wd_t, ln_sb, ident_d, part, latents, rows, results):
    with ExitStack() as ctx:
        st = Stage(nc, ctx, "f")
        sb, bank, sem = st.sb, st.bank, st.sem
        ident = sb("ident", [P, P])
        ones = sb("ones", [P, P])
        zero = sb("zero", [P, ZERO_W])
        b1_c = sb("b1_c", [P, MC])
        b2_row = sb("b2_row", [P, D])
        alpha1 = sb("alpha1", [P, MC])
        alpha2 = sb("alpha2", [P, 2, D])
        sign1 = sb("sign1", [P, KC, FF], F32R)
        sign2 = sb("sign2", [P, MC, D], F32R)
        w1r = sb("w1r", [P, MC, D])
        w1s = sb("w1s", [P, KC, FF])
        w2s = sb("w2s", [P, MC, D])
        w2abs = sb("w2abs", [P, MC, D])

        x_t = sb("x_t", [P, NT, D])
        xn = sb("xn", [P, NT, D])
        base = sb("base", [P, NT, D])
        y = sb("y", [P, NT, D])
        out = sb("out", [P, NT, D])
        stats = sb("stats", [P, NT, 6])
        mean_var = sb("mean_var", [P, NT, 2])
        small = sb("small", [P, 4, NT])
        xT_hi = sb("xT_hi", [P, KC, S], F32R)
        xT_lo = sb("xT_lo", [P, KC, S], F32R)
        g = sb("g", [P, MC, S])
        g_hi = sb("g_hi", [P, MC, S], F32R)
        g_lo = sb("g_lo", [P, MC, S], F32R)

        ln = sb("ln", [P, 2, KC])
        wd = sb("wd", [P, KC * 2 * P])
        wd_hi = sb("wd_hi", [P, KC * 2 * P], F32R)
        wd_lo = sb("wd_lo", [P, KC * 2 * P], F32R)
        h = sb("h", [P, NT, D])
        hT = sb("hT", [P, KC, S])
        hT_hi = sb("hT_hi", [P, KC, S], F32R)
        hT_lo = sb("hT_lo", [P, KC, S], F32R)
        c_parts = sb("c_parts", [P, 4, S], F32R)

        pX = [bank(f"pX{c}") for c in range(KC)]
        pU = [bank(f"pU{i}") for i in range(3)]
        pY = [bank(f"pY{i}", (P, 2, D)) for i in range(2)]

        loaded = st.lasting("loaded")
        ident_in = st.lasting("ident_in")
        ones_set = st.lasting("ones_set")
        zero_set = st.lasting("zero_set")
        signs_done = st.lasting("signs_done")
        alpha1_done = st.lasting("alpha1_done")
        sums_done = st.lasting("sums_done")
        alpha2_done = st.lasting("alpha2_done")
        wd_split = st.lasting("wd_split")
        spare_done = st.lasting("spare_done")
        stored = st.lasting("stored")

        x_in = sem("x_in")
        ln_step = sem("ln_step")
        root = sem("root")
        xT_done = sem("xT_done")
        xT_hi_done = sem("xT_hi_done")
        xT_lo_done = sem("xT_lo_done")
        up_done = sem("up_done")
        gelu_done = sem("gelu_done")
        g_lo_done = sem("g_lo_done")
        down_done = sem("down_done")
        base_done = sem("base_done")
        h_done = sem("h_done")
        hT_f_done = sem("hT_f_done")
        hT_split = sem("hT_split")
        c_done = sem("c_done")
        c_hi_done = sem("c_hi_done")
        c_lo_done = sem("c_lo_done")
        y_done = sem("y_done")
        out_done = sem("out_done")
        latents_out = sem("latents_out")
        zeroed = sem("zeroed")
        out_free = sem("out_free")

        with nc.Block() as block:
            @block.sync
            def _(sp):
                def one(sp, b, more):
                    sp.wait_ge(stored, 16)
                    sp.sem_clear(stored)
                    sp.sem_inc(out_free, 1)
                    if more:
                        sp.wait_ge(base_done, 1)
                        sp.dma_start(x_t[:], tokens(x, b + 1)).then_inc(x_in, 16)
                    for buf in (rows, results):
                        flat = buf.rearrange("(p r) d -> p (r d)", p=P)
                        share = flat.shape[1] // B
                        sp.dma_start(flat[:, bass.ds(b * share, share)], zero[:, 0:share]).then_inc(zeroed, 16)
                    sp.wait_ge(c_lo_done, 2)
                    sp.dma_start(latent(latents, b), c_parts[:].bitcast(F32)).then_inc(latents_out, 16)
                    sp.wait_ge(out_done, 2)
                    sp.dma_start(tokens(part, b), out[:]).then_inc(stored, 16)
                    sp.wait_ge(latents_out, 16)
                    sp.wait_ge(zeroed, 32)
                    st.lead(sp)

                sp.dma_start(x_t[:], tokens(x, 0)).then_inc(x_in, 16)
                sp.dma_start(ident[:], ident_d).then_inc(ident_in, 16)
                sp.dma_start(w1r[:], w1_rows.rearrange("(m p) d -> p m d", p=P)).then_inc(loaded, 16)
                sp.dma_start(w1s[:], w1_t.rearrange("(c p) f -> p c f", p=P)).then_inc(loaded, 16)
                sp.dma_start(w2s[:], w2_t.rearrange("(m p) d -> p m d", p=P)).then_inc(loaded, 16)
                sp.dma_start(b1_c[:], b1).then_inc(loaded, 16)
                sp.dma_start(b2_row[:], b2).then_inc(loaded, 16)
                sp.dma_start(wd[:], wd_t).then_inc(loaded, 16)
                sp.dma_start(ln[:], ln_sb).then_inc(loaded, 16)
                st.lead(sp)
                sp.wait_ge(zero_set, 1)
                sp.sem_inc(stored, 16)
                with sp.Fori(0, B - 1) as b:
                    one(sp, b, True)
                one(sp, B - 1, False)
                sp.wait_ge(stored, 16)
                sp.dma_start(latent(latents, B), latent(latents, 0)).then_inc(spare_done, 16)
                sp.wait_ge(spare_done, 16)

            @block.gpsimd
            def _(pool):
                nc.gpsimd.memset(ones[:], 1.0).then_inc(ones_set, 1)
                nc.gpsimd.memset(zero[:], 0.0).then_inc(zero_set, 1)
                pool.wait_ge(loaded, 112)
                nc.gpsimd.tensor_copy(wd_hi[:], wd[:]).then_inc(wd_split, 1)
                pool.wait_ge(wd_split, 1)
                nc.gpsimd.tensor_tensor(wd_lo[:], wd[:], wd_hi[:], ALU.subtract).then_inc(wd_split, 1)
                st.meet(pool, POOL)
                with pool.Fori(0, B) as b:
                    nc.gpsimd.tensor_tensor(base[:], x_t[:], xn[:], ALU.add).then_inc(base_done, 1)
                    for c in range(KC):
                        pool.wait_ge(hT_f_done, c + 1)
                        nc.gpsimd.tensor_copy(hT_hi[:, c, :], hT[:, c, :]).then_inc(hT_split, 1)
                        pool.wait_ge(hT_split, 2 * c + 1)
                        nc.gpsimd.tensor_tensor(hT_lo[:, c, :], hT[:, c, :], hT_hi[:, c, :],
                                                ALU.subtract).then_inc(hT_split, 1)
                    pool.wait_ge(base_done, 1)
                    for t in range(NT):
                        nc.gpsimd.tensor_tensor(base[:, t, :], base[:, t, :], b2_row[:],
                                                ALU.add).then_inc(base_done, 1)
                    pool.wait_ge(base_done, 1 + NT)
                    pool.wait_ge(hT_split, 2 * KC)
                    st.meet(pool, POOL)

            @block.scalar
            def _(act):
                def norm_roots():
                    for i in range(2):
                        act.wait_ge(ln_step, i * LN_ALL + LN_VAR)
                        nc.scalar.activation(small[:, 1, :], small[:, 0, :], ACT.Sqrt).then_inc(root, 1)

                def x_high():
                    for c in range(KC):
                        act.wait_ge(xT_done, c + 1)
                        nc.scalar.copy(xT_hi[:, c, :], pX[c][:]).then_inc(xT_hi_done, 1)

                def one(more):
                    for m in range(MC):
                        act.wait_ge(up_done, m + 1)
                        for dst in (g, g_hi):
                            nc.scalar.activation(dst[:, m, :], pU[m % 3][:], ACT.Gelu, bias=b1_c[:, m:m + 1],
                                                 scale=alpha1[:, m:m + 1]).then_inc(gelu_done, 1)
                    for i in range(2):
                        act.wait_ge(c_done, i + 1)
                        nc.scalar.copy(c_parts[:, i, :], pX[i][:]).then_inc(c_hi_done, 1)
                    if more:
                        norm_roots()
                        x_high()
                        act.wait_ge(xT_hi_done, KC)
                    act.wait_ge(gelu_done, 2 * MC)
                    act.wait_ge(c_hi_done, 2)
                    st.meet(act, ACTE)

                norm_roots()
                x_high()
                act.wait_ge(xT_hi_done, KC)
                act.wait_ge(loaded, 112)
                nc.scalar.activation(sign1[:], w1s[:], ACT.Sign).then_inc(signs_done, 1)
                nc.scalar.activation(sign2[:], w2s[:], ACT.Sign).then_inc(signs_done, 1)
                nc.scalar.activation(w2abs[:], w2s[:], ACT.Abs).then_inc(signs_done, 1)
                act.wait_ge(alpha1_done, 3)
                st.meet(act, ACTE)
                with act.Fori(0, B - 1):
                    one(True)
                one(False)

            @block.vector
            def _(dve):
                def norms():
                    dve.wait_ge(x_in, 16)
                    layer_norm(nc, dve, x_t, xn, stats, mean_var, small[:, 0, :], small[:, 1, :],
                               small[:, 2, :], small[:, 3, :], None, (ln_step, 0), (root, 1))
                    dve.wait_ge(ln_step, LN_ALL)
                    layer_norm(nc, dve, xn, h, stats, mean_var, small[:, 0, :], small[:, 1, :],
                               small[:, 2, :], small[:, 3, :], None, (ln_step, LN_ALL), (root, 2))

                def x_low():
                    for c in range(KC):
                        dve.wait_ge(xT_hi_done, c + 1)
                        nc.vector.tensor_tensor(xT_lo[:, c, :], pX[c][:], xT_hi[:, c, :],
                                                ALU.subtract).then_inc(xT_lo_done, 1)
                    dve.wait_ge(xT_lo_done, KC)
                    dve.wait_ge(ln_step, 2 * LN_ALL)

                def one(more):
                    for c in range(KC):
                        dve.wait_ge(h_done, c + 1)
                        nc.vector.tensor_scalar(hT[:, c, :], pX[c][:], ln[:, 0, c:c + 1], ln[:, 1, c:c + 1],
                                                ALU.mult, ALU.add).then_inc(hT_f_done, 1)
                    for m in range(MC):
                        dve.wait_ge(gelu_done, 2 * m + 2)
                        nc.vector.tensor_tensor(g_lo[:, m, :], g[:, m, :], g_hi[:, m, :],
                                                ALU.subtract).then_inc(g_lo_done, 1)
                    for i in range(2):
                        dve.wait_ge(c_hi_done, i + 1)
                        nc.vector.tensor_tensor(c_parts[:, 2 + i, :], pX[i][:], c_parts[:, i, :],
                                                ALU.subtract).then_inc(c_lo_done, 1)
                    if more:
                        norms()
                        x_low()
                    for i in range(2):
                        dve.wait_ge(down_done, i + 1)
                        nc.vector.tensor_tensor(y[:, 2 * i:2 * i + 2, :], pY[i][:], alpha2[:],
                                                ALU.mult).then_inc(y_done, 1)
                    dve.wait_ge(base_done, 1 + NT)
                    dve.wait_ge(out_free, 1)
                    for i in range(2):
                        dve.wait_ge(y_done, i + 1)
                        nc.vector.tensor_tensor(out[:, 2 * i:2 * i + 2, :], y[:, 2 * i:2 * i + 2, :],
                                                base[:, 2 * i:2 * i + 2, :], ALU.add).then_inc(out_done, 1)
                    dve.wait_ge(out_done, 2)
                    dve.wait_ge(c_lo_done, 2)
                    st.meet(dve, DVE)

                norms()
                x_low()
                dve.wait_ge(loaded, 112)
                nc.vector.tensor_reduce(alpha1[:], w1r[:], AX.X, ALU.add,
                                        apply_absolute_value=True).then_inc(alpha1_done, 1)
                dve.wait_ge(alpha1_done, 1)
                nc.vector.tensor_scalar(alpha1[:], alpha1[:], 1.0 / D, None, ALU.mult).then_inc(alpha1_done, 2)
                dve.wait_ge(sums_done, 1)
                for i in range(2):
                    nc.vector.tensor_scalar(alpha2[:, i, :], pY[0][:, 0, :], 1.0 / FF, None,
                                            ALU.mult).then_inc(alpha2_done, 1)
                dve.wait_ge(alpha2_done, 2)
                st.meet(dve, DVE)
                with dve.Fori(0, B - 1):
                    one(True)
                one(False)

            @block.tensor
            def _(pe):
                def transposes(src, done):
                    for c in range(KC):
                        for t in range(NT):
                            last = nc.tensor.transpose(pX[c][:, t * P:(t + 1) * P],
                                                       src[:, t, c * P:(c + 1) * P], ident[:])
                        last.then_inc(done, 1)

                def one(more):
                    transposes(h, h_done)
                    for m in range(MC):
                        if m >= 3:
                            pe.wait_ge(gelu_done, 2 * (m - 2))
                        for c in range(KC):
                            w = sign1[:, c, m * P:(m + 1) * P]
                            nc.tensor.matmul(pU[m % 3][:], w, xT_lo[:, c, :], start=(c == 0), stop=False)
                            last = nc.tensor.matmul(pU[m % 3][:], w, xT_hi[:, c, :], start=False,
                                                    stop=(c == KC - 1))
                        last.then_inc(up_done, 1)
                    pe.wait_ge(hT_split, 2 * KC)
                    for i in range(2):
                        for c in range(KC):
                            cols = slice((2 * c + i) * P, (2 * c + i + 1) * P)
                            last = product(nc, pX[i][:], wd_hi[:, cols], wd_lo[:, cols],
                                           hT_hi[:, c, :], hT_lo[:, c, :], c == 0, c == KC - 1)
                        last.then_inc(c_done, 1)
                    for t in range(NT):
                        if t == 2 and more:
                            pe.wait_ge(c_lo_done, 2)
                            pe.wait_ge(ln_step, LN_ALL)
                            transposes(xn, xT_done)
                        for m in range(MC):
                            if t == 0:
                                pe.wait_ge(g_lo_done, m + 1)
                            for part_ in (g_lo, g_hi):
                                last = nc.tensor.matmul(pY[t // 2][:, t % 2, :], part_[:, m, t * P:(t + 1) * P],
                                                        sign2[:, m, :], start=(m == 0 and part_ is g_lo),
                                                        stop=(m == MC - 1 and part_ is g_hi))
                        if t % 2:
                            last.then_inc(down_done, 1)
                    pe.wait_ge(down_done, 2)
                    st.meet(pe, PE)

                pe.wait_ge(ident_in, 16)
                pe.wait_ge(ln_step, LN_ALL)
                transposes(xn, xT_done)
                pe.wait_ge(xT_done, KC)
                pe.wait_ge(ones_set, 1)
                pe.wait_ge(signs_done, 3)
                for m in range(MC):
                    last = nc.tensor.matmul(pY[0][:, 0, :], ones[:], w2abs[:, m, :],
                                            start=(m == 0), stop=(m == MC - 1))
                last.then_inc(sums_done, 1)
                pe.wait_ge(alpha2_done, 2)
                pe.wait_ge(wd_split, 2)
                st.meet(pe, PE)
                with pe.Fori(0, B - 1):
                    one(True)
                one(False)


WQK = 192 * NP


def stage_a(nc, wq_t, wk_t, wv_t, wo_t, rope_c, rope_s, own_d, ident_d, part, latents, x1):
    with ExitStack() as ctx:
        st = Stage(nc, ctx, "a")
        sb, bank, sem = st.sb, st.bank, st.sem
        ident = sb("ident", [P, P])
        ones = sb("ones", [P, P], F32R)
        cos = sb("cos", [P, S])
        sin = sb("sin", [P, S])
        names = {"q": (wq_t, WQK), "k": (wk_t, WQK), "v": (wv_t, H0 * DH),
                 "o": (wo_t, NP * D)}
        w_hi = {n: sb(f"w{n}_hi", [P, f], F32R) for n, (_, f) in names.items()}
        w_lo = {n: sb(f"w{n}_lo", [P, f], F32R) for n, (_, f) in names.items()}
        v_hi = sb("v_hi", [P, NT, NP, 3, DH], F32R)
        v_lo = sb("v_lo", [P, NT, NP, 3, DH], F32R)
        own = sb("own", [P, 2])
        q_hi = sb("q_hi", [P, 2, 2, S], F32R)
        q_lo = sb("q_lo", [P, 2, 2, S], F32R)

        J = H0 * NT
        PR = 4

        loaded = st.lasting("loaded")
        w_split = st.lasting("w_split")
        w_lo_done = st.lasting("w_lo_done")
        first_in = st.lasting("first_in")
        spare_done = st.lasting("spare_done")
        fills = st.lasting("fills")
        c_in = sem("c_in")
        v_done = sem("v_done")
        v_hi_done = sem("v_hi_done")
        v_lo_done = sem("v_lo_done")
        pj_done = sem("pj_done")
        rot_mul = sem("rot_mul")
        rot_add = sem("rot_add")
        qk_hi_done = sem("qk_hi_done")
        qk_lo_done = sem("qk_lo_done")
        s_done = sem("s_done")
        max_done = sem("max_done")
        diag_done = sem("diag_done")
        st_done = sem("st_done")
        exp_done = sem("exp_done")
        p_lo_done = sem("p_lo_done")
        pv_done = sem("pv_done")
        inv_done = sem("inv_done")
        sums_out = sem("sums_out")
        norm_done = sem("norm_done")
        att_split = sem("att_split")
        o_done = sem("o_done")
        part_in = sem("part_in")
        out_done = sem("out_done")
        stored = st.lasting("stored")

        with ExitStack() as ctx2:
            raw = {n: ctx2.enter_context(nc.sbuf_tensor(f"a_raw_{n}", [P, f], F32)) for n, (_, f) in names.items()}
            with nc.Block() as block:
                @block.sync
                def _(sp):
                    for n, (src, _) in names.items():
                        sp.dma_start(raw[n][:], src).then_inc(loaded, 16)
                    for dst, src in ((ident, ident_d), (cos, rope_c), (sin, rope_s), (own, own_d)):
                        sp.dma_start(dst[:], src).then_inc(loaded, 16)

                @block.scalar
                def _(act):
                    act.wait_ge(loaded, 16 * (len(names) + 4))
                    for n in names:
                        nc.scalar.copy(w_hi[n][:], raw[n][:]).then_inc(w_split, 1)

                @block.vector
                def _(dve):
                    for i, n in enumerate(names):
                        dve.wait_ge(w_split, i + 1)
                        nc.vector.tensor_tensor(w_lo[n][:], raw[n][:], w_hi[n][:],
                                                ALU.subtract).then_inc(w_lo_done, 1)
                    dve.wait_ge(w_lo_done, len(names))

                @block.gpsimd
                def _(pool):
                    nc.gpsimd.memset(ones[:].bitcast(F32), 1.0).then_inc(fills, 1)
                    nc.gpsimd.memset(v_hi[:, :, :, 1, :].bitcast(F32), 1.0).then_inc(fills, 1)
                    nc.gpsimd.memset(v_lo[:, :, :, 1, :].bitcast(F32), 0.0).then_inc(fills, 1)
                    pool.wait_ge(fills, 3)

        x_t = sb("x_t", [P, NT, D])
        pr = sb("pr", [P, 2, S])
        latent_parts = sb("latent_parts", [P, 4, S], F32R)
        c_hi, c_lo = latent_parts[:, 0:2, :], latent_parts[:, 2:4, :]
        rot = sb("rot", [P, 3, S])
        k_hi = sb("k_hi", [P, 2, S], F32R)
        k_lo = sb("k_lo", [P, 2, S], F32R)
        row_max = sb("row_max", [P, H0, NT])
        diag = sb("diag", [P, 2, NT, P], F32R)
        pr_hi = sb("pr_hi", [P, PR, S], F32R)
        pr_lo = sb("pr_lo", [P, PR, S], F32R)
        den = sb("den", [P, S])
        att = sb("att", [P, 2, S])
        att_hi = sb("att_hi", [P, NP, S], F32R)
        att_lo = sb("att_lo", [P, NP, S], F32R)

        pG = [bank(f"pG{i}") for i in range(2)]
        pM = [bank(f"pM{i}") for i in range(2)]
        pT = [bank(f"pT{i}") for i in range(2)]
        pA = [bank(f"pA{i}") for i in range(2)]

        def head_cols(w, p, swapped):
            return w[:, 192 * p + 64 * swapped:192 * p + 64 * swapped + P]

        def v_cols(v, t, h):
            return v[:, t, h // 2, :, :].rearrange("p b d -> p (b d)")[:, 64 * (h % 2):64 * (h % 2) + P]

        with nc.Block() as block:
            @block.sync
            def _(sp):
                sp.dma_start(latent_parts[:].bitcast(F32), latent(latents, 0)).then_inc(first_in, 16)
                st.lead(sp)
                sp.sem_inc(stored, 16)
                with sp.Fori(0, B) as b:
                    sp.wait_ge(stored, 16)
                    sp.sem_clear(stored)
                    sp.dma_start(x_t[:], tokens(part, b)).then_inc(part_in, 16)
                    sp.wait_ge(pj_done, 4 * (NP - 1))
                    sp.dma_start(latent_parts[:].bitcast(F32), latent(latents, b + 1)).then_inc(c_in, 16)
                    sp.wait_ge(out_done, 2)
                    sp.dma_start(tokens(x1, b), x_t[:]).then_inc(stored, 16)
                    st.lead(sp)
                sp.wait_ge(stored, 16)
                sp.dma_start(tokens(x1, B), tokens(x1, 0)).then_inc(spare_done, 16)
                sp.wait_ge(spare_done, 16)

            @block.tensor
            def _(pe):
                def project(u, p, i):
                    n = 4 * u + i
                    if n >= 2:
                        pe.wait_ge(rot_mul, n - 1)
                    w, c = ("q", 0) if i < 2 else ("k", 1)
                    product(nc, pG[i % 2][:], head_cols(w_hi[w], p, i % 2), head_cols(w_lo[w], p, i % 2),
                            c_hi[:, c, :], c_lo[:, c, :], True, True).then_inc(pj_done, 1)

                def scores(v, h, t, u):
                    p, n = h // 2, NT * v + t
                    if t == 0 and u is not None:
                        pe.wait_ge(qk_hi_done, 3 * u + 3)
                    if n >= 2:
                        pe.wait_ge(max_done, n - 1)
                    nc.tensor.matmul(pM[n % 2][:], q_hi[:, p % 2, h % 2, t * P:(t + 1) * P], k_hi[:, p % 2, :],
                                     start=True, stop=True).then_inc(s_done, 1)

                def values():
                    for i in range(2 * NT):
                        t, half = i // 2, i % 2
                        if i >= 2:
                            pe.wait_ge(v_lo_done, i - 1)
                        cols = slice(half * 512, half * 512 + 512)
                        ts = slice(t * P, (t + 1) * P)
                        product(nc, pG[half][:], c_hi[:, 1, ts], c_lo[:, 1, ts], w_hi["v"][:, cols],
                                w_lo["v"][:, cols], True, True).then_inc(v_done, 1)

                def shifted(j):
                    h, t = j // NT, j % NT
                    p = h // 2
                    ks = slice(t * P, (t + 1) * P)
                    if t == 0 and p >= 1:
                        pe.wait_ge(qk_lo_done, 3 * p)
                    if j >= 2:
                        pe.wait_ge(exp_done, 2 * (j - 1))
                    product(nc, pT[j % 2][:], k_hi[:, p % 2, ks], k_lo[:, p % 2, ks],
                            q_hi[:, p % 2, h % 2, :], q_lo[:, p % 2, h % 2, :], True, False)
                    if t == 0 and h >= 1:
                        pe.wait_ge(diag_done, NT * h)
                    nc.tensor.matmul(pT[j % 2][:], ones[:], diag[:, h % 2, :, :], start=False,
                                     stop=True).then_inc(st_done, 1)

                def weigh(j):
                    h, t = j // NT, j % NT
                    if t == 0 and h >= 2:
                        pe.wait_ge(sums_out, 2 * (h - 1))
                    pe.wait_ge(p_lo_done, j + 1)
                    product(nc, pA[h % 2][:], v_cols(v_hi, t, h), v_cols(v_lo, t, h), pr_hi[:, j % PR, :],
                            pr_lo[:, j % PR, :], t == 0, t == NT - 1).then_inc(pv_done, 1)

                pe.wait_ge(first_in, 16)
                for i in range(4):
                    project(0, 0, i)
                pe.wait_ge(rot_mul, 4)
                values()
                for t in range(NT):
                    scores(0, 0, t, 0)
                pe.wait_ge(s_done, NT)
                st.meet(pe, PE)
                with pe.Fori(0, B) as b:
                    for j in range(J + 3):
                        h, t = j // NT, j % NT
                        if j < J:
                            shifted(j)
                            if h % 2 == 0 and t < 2 and h // 2 + 1 < NP:
                                project(h // 2, h // 2 + 1, 2 * t)
                                project(h // 2, h // 2 + 1, 2 * t + 1)
                            if h + 1 < H0 and t < 3:
                                u = (h + 1) // 2 - 1 if h >= 1 else None
                                for i in ((0, 1), (2,), (3,))[t]:
                                    scores(h, h + 1, i, u)
                        if j == J - 1:
                            pe.wait_ge(c_in, 16)
                            for i in range(4):
                                project(NP - 1, 0, i)
                        if j >= 3:
                            weigh(j - 3)
                    pe.wait_ge(rot_mul, 4 * NP)
                    values()
                    for t in range(NT):
                        scores(H0 - 1, 0, t, NP - 1)
                    pe.wait_ge(exp_done, 2 * J)
                    pe.wait_ge(att_split, 2 * NP)
                    for t in range(NT):
                        ts = slice(t * P, (t + 1) * P)
                        for p in range(NP):
                            cols = slice(p * D, (p + 1) * D)
                            last = product(nc, pT[t // 2][:, (t % 2) * D:(t % 2 + 1) * D], att_hi[:, p, ts],
                                           att_lo[:, p, ts], w_hi["o"][:, cols], w_lo["o"][:, cols],
                                           p == 0, p == NP - 1)
                        if t % 2:
                            last.then_inc(o_done, 1)
                    pe.wait_ge(o_done, 2)
                    st.meet(pe, PE)

            @block.vector
            def _(dve):
                def rotate(u, i):
                    n = 4 * u + i
                    dve.wait_ge(pj_done, n + 1)
                    if n >= 2:
                        dve.wait_ge(rot_add, n // 2)
                    nc.vector.tensor_tensor(rot[:, i % 2, :], pG[i % 2][:], (cos, sin)[i % 2][:],
                                            ALU.mult).then_inc(rot_mul, 1)

                def q_low(u, p):
                    for i in range(2):
                        dve.wait_ge(qk_hi_done, 3 * u + i + 1)
                        nc.vector.scalar_tensor_tensor(out=q_lo[:, p % 2, i, :], in0=rot[:, 2, :],
                                                       scalar=own[:, i:i + 1], in1=q_hi[:, p % 2, i, :],
                                                       op0=ALU.mult, op1=ALU.subtract).then_inc(qk_lo_done, 1)

                def k_low(u, p):
                    dve.wait_ge(qk_hi_done, 3 * u + 3)
                    nc.vector.tensor_tensor(k_lo[:, p % 2, :], rot[:, 2, :], k_hi[:, p % 2, :],
                                            ALU.subtract).then_inc(qk_lo_done, 1)

                def maximum(v, h, t):
                    n = NT * v + t
                    dve.wait_ge(s_done, n + 1)
                    nc.vector.reduce_max(row_max[:, h, t:t + 1], pM[n % 2][:], AX.X).then_inc(max_done, 1)
                    if t == 0 and v >= 1:
                        dve.wait_ge(st_done, NT * v)
                    dve.wait_ge(max_done, n + 1)
                    nc.vector.tensor_scalar(diag[:, h % 2, t, :], ident[:], row_max[:, h, t:t + 1], -1.0,
                                            ALU.mult, ALU.mult).then_inc(diag_done, 1)

                def values_low():
                    for i in range(2 * NT):
                        t, half = i // 2, i % 2
                        ps = slice(half * NP // 2, (half + 1) * NP // 2)
                        dve.wait_ge(v_hi_done, i + 1)
                        nc.vector.tensor_tensor(v_lo[:, t, ps, 0:3:2, :],
                                                pG[half][:].rearrange("p (h o d) -> p h o d", o=2, d=DH),
                                                v_hi[:, t, ps, 0:3:2, :], ALU.subtract).then_inc(v_lo_done, 1)

                def normalise(p):
                    dve.wait_ge(sums_out, 4 * p + 4)
                    nc.vector.reciprocal(den[:], den[:]).then_inc(inv_done, 1)
                    dve.wait_ge(inv_done, p + 1)
                    nc.vector.tensor_tensor(att[:, p % 2, :], att[:, p % 2, :], den[:],
                                            ALU.mult).then_inc(norm_done, 1)

                for i in range(4):
                    rotate(0, i)
                q_low(0, 0)
                k_low(0, 0)
                values_low()
                for t in range(NT):
                    maximum(0, 0, t)
                dve.wait_ge(diag_done, NT)
                dve.wait_ge(v_lo_done, 2 * NT)
                dve.wait_ge(qk_lo_done, 3)
                st.meet(dve, DVE)
                with dve.Fori(0, B) as b:
                    for j in range(J):
                        h, t = j // NT, j % NT
                        nxt = h // 2 + 1
                        more = h % 2 == 0 and nxt < NP
                        if more and t < 2:
                            rotate(h // 2, 2 * t)
                            rotate(h // 2, 2 * t + 1)
                        if h + 1 < H0 and t < 3:
                            for i in ((0, 1), (2,), (3,))[t]:
                                maximum(h, h + 1, i)
                        if more and t == 1:
                            q_low(h // 2, nxt)
                        if more and t == 2:
                            k_low(h // 2, nxt)
                        if h % 2 and h >= 3 and t == 1:
                            normalise(h // 2 - 1)
                    for i in range(4):
                        rotate(NP - 1, i)
                    q_low(NP - 1, 0)
                    normalise(NP - 1)
                    k_low(NP - 1, 0)
                    values_low()
                    for t in range(NT):
                        maximum(H0 - 1, 0, t)
                    dve.wait_ge(part_in, 16)
                    for i in range(2):
                        dve.wait_ge(o_done, i + 1)
                        nc.vector.tensor_tensor(x_t[:, 2 * i:2 * i + 2, :],
                                                pT[i][:].rearrange("p (t d) -> p t d", d=D),
                                                x_t[:, 2 * i:2 * i + 2, :], ALU.add).then_inc(out_done, 1)
                    dve.wait_ge(out_done, 2)
                    dve.wait_ge(diag_done, NT * H0)
                    dve.wait_ge(v_lo_done, 2 * NT)
                    dve.wait_ge(qk_lo_done, 3 * NP)
                    st.meet(dve, DVE)

            @block.scalar
            def _(act):
                def q_high(u, p):
                    for i in range(2):
                        act.wait_ge(rot_add, 2 * u + 1)
                        if u >= 1:
                            act.wait_ge(st_done, 2 * NT * u)
                        nc.scalar.activation(q_hi[:, p % 2, i, :], rot[:, 2, :], ACT.Copy,
                                             scale=own[:, i:i + 1]).then_inc(qk_hi_done, 1)

                def k_high(u, p):
                    act.wait_ge(rot_add, 2 * u + 2)
                    nc.scalar.copy(k_hi[:, p % 2, :], rot[:, 2, :]).then_inc(qk_hi_done, 1)

                def values_high():
                    for i in range(2 * NT):
                        t, half = i // 2, i % 2
                        act.wait_ge(v_done, i + 1)
                        nc.scalar.copy(v_hi[:, t, half * NP // 2:(half + 1) * NP // 2, 0:3:2, :],
                                       pG[half][:].rearrange("p (h o d) -> p h o d", o=2, d=DH)).then_inc(v_hi_done, 1)

                def take_sums(h):
                    mine, other = slice(64 * (h % 2), 64 * (h % 2) + 64), slice(64 - 64 * (h % 2), 128 - 64 * (h % 2))
                    act.wait_ge(pv_done, NT * (h + 1))
                    if h >= 4:
                        act.wait_ge(att_split, 2 * (h // 2) - 2)
                    if h >= 2:
                        act.wait_ge(norm_done, h // 2)
                    nc.scalar.copy(att[mine, h // 2 % 2, :], pA[h % 2][mine, :]).then_inc(sums_out, 1)
                    nc.scalar.copy(den[mine, :], pA[h % 2][other, :]).then_inc(sums_out, 1)

                q_high(0, 0)
                k_high(0, 0)
                values_high()
                act.wait_ge(v_hi_done, 2 * NT)
                st.meet(act, ACTE)
                with act.Fori(0, B) as b:
                    for j in range(J):
                        h, t = j // NT, j % NT
                        nxt = h // 2 + 1
                        more = h % 2 == 0 and nxt < NP
                        act.wait_ge(st_done, j + 1)
                        if j >= 2:
                            act.wait_ge(p_lo_done, j - 1)
                        nc.scalar.activation(pr[:, j % 2, :], pT[j % 2][:], ACT.Exp, scale=SCALE).then_inc(exp_done, 1)
                        if j >= PR:
                            act.wait_ge(pv_done, j - PR + 1)
                        nc.scalar.activation(pr_hi[:, j % PR, :], pT[j % 2][:], ACT.Exp,
                                             scale=SCALE).then_inc(exp_done, 1)
                        if more and t == 1:
                            q_high(h // 2, nxt)
                        if more and t == 2:
                            k_high(h // 2, nxt)
                        if h % 2 == 0 and h >= 2:
                            if t == 0:
                                take_sums(h - 2)
                            if t == 3:
                                take_sums(h - 1)
                    take_sums(H0 - 2)
                    q_high(NP - 1, 0)
                    take_sums(H0 - 1)
                    k_high(NP - 1, 0)
                    values_high()
                    act.wait_ge(v_hi_done, 2 * NT)
                    act.wait_ge(qk_hi_done, 3 * NP)
                    act.wait_ge(sums_out, 2 * H0)
                    st.meet(act, ACTE)

            @block.gpsimd
            def _(pool):
                def add(n):
                    pool.wait_ge(rot_mul, 2 * n + 2)
                    if n >= 1:
                        pool.wait_ge(qk_lo_done, 3 * (n // 2) + (2 if n % 2 else 0))
                    nc.gpsimd.tensor_tensor(rot[:, 2, :], rot[:, 0, :], rot[:, 1, :], ALU.add).then_inc(rot_add, 1)

                def split_att(p):
                    pool.wait_ge(norm_done, p + 1)
                    nc.gpsimd.tensor_copy(att_hi[:, p, :], att[:, p % 2, :]).then_inc(att_split, 1)
                    pool.wait_ge(att_split, 2 * p + 1)
                    nc.gpsimd.tensor_tensor(att_lo[:, p, :], att[:, p % 2, :], att_hi[:, p, :],
                                            ALU.subtract).then_inc(att_split, 1)

                add(0)
                add(1)
                pool.wait_ge(rot_add, 2)
                st.meet(pool, POOL)
                with pool.Fori(0, B) as b:
                    for j in range(J):
                        h, t = j // NT, j % NT
                        more = h % 2 == 0 and h // 2 + 1 < NP
                        if more and t == 0:
                            add(h)
                        pool.wait_ge(exp_done, 2 * j + 2)
                        if j >= PR:
                            pool.wait_ge(pv_done, j - PR + 1)
                        nc.gpsimd.tensor_tensor(pr_lo[:, j % PR, :], pr[:, j % 2, :], pr_hi[:, j % PR, :],
                                                ALU.subtract).then_inc(p_lo_done, 1)
                        if more and t == 1:
                            add(h + 1)
                        if h % 2 and h >= 3 and t == 3:
                            split_att(h // 2 - 1)
                    add(2 * NP - 2)
                    add(2 * NP - 1)
                    split_att(NP - 1)
                    pool.wait_ge(rot_add, 2 * NP)
                    pool.wait_ge(att_split, 2 * NP)
                    st.meet(pool, POOL)


NC1 = KC
GW = 4 * (P + DE)


def stage_b(nc, wq_t, wk_t, wv_t, wo_t, wg, bg, own8_d, mask_d, before_d, ident_d, x1, xm_d, x2, sel_d):
    with ExitStack() as ctx:
        st = Stage(nc, ctx, "b")
        sb, bank, sem = st.sb, st.bank, st.sem
        ident = sb("ident", [P, P])
        own8 = sb("own8", [P, 8])
        mask = sb("mask", [P, P + P + 3 * P])
        before = sb("before", [P, NE, NE])
        bg_row = sb("bg_row", [P, NE])
        names = {"q": (wq_t, KC * D), "k": (wk_t, KC * D), "v": (wv_t, KC * D), "o": (wo_t, KC * D),
                 "g": (wg, KC * NE)}
        w_hi = {n: sb(f"w{n}_hi", [P, f], F32R) for n, (_, f) in names.items()}
        w_lo = {n: sb(f"w{n}_lo", [P, f], F32R) for n, (_, f) in names.items()}
        raw = {n: sb(f"raw_{n}", [P, f]) for n, (_, f) in names.items()}
        v_hi = sb("v_hi", [P, NT, 4, GW], F32R)
        v_lo = sb("v_lo", [P, NT, 4, GW], F32R)

        x_new = sb("x_new", [P, NT, D])
        x_t = sb("x_t", [P, NT, D])
        xm = sb("xm", [P, NT, D])
        x_out = sb("x_out", [P, NT, D])
        stats = sb("stats", [P, NT, 6])
        mean_var = sb("mean_var", [P, NT, 2])
        small = sb("small", [P, 4, NT])
        xT_hi = sb("xT_hi", [P, KC, S], F32R)
        xT_lo = sb("xT_lo", [P, KC, S], F32R)
        neg = sb("neg", [P, 2, S])
        ex = sb("ex", [P, 2, S])
        feat = sb("feat", [P, 2 * NC1, S])
        q_hi = sb("q_hi", [P, NC1, S], F32R)
        q_lo = sb("q_lo", [P, NC1, S], F32R)
        kz_hi = sb("kz_hi", [P, 3, S], F32R)
        kz_lo = sb("kz_lo", [P, 3, S], F32R)
        RA = 4
        a_hi = sb("a_hi", [P, RA, S], F32R)
        a_lo = sb("a_lo", [P, RA, S], F32R)
        den = sb("den", [P, S])
        inv = sb("inv", [P, S])
        o = sb("o", [P, NC1, S])
        o_hi = sb("o_hi", [P, NC1, S], F32R)
        o_lo = sb("o_lo", [P, NC1, S], F32R)
        lg = sb("lg", [P, NT, NE])
        top = sb("top", [P, NT])
        tot = sb("tot", [P, NT])
        gate = sb("gate", [P, NT, NE])
        more = sb("more", [P, NT * NE, NE])
        same = sb("same", [P, NT * NE, NE])
        rank = sb("rank", [P, NT, NE])
        sel = sb("sel", [P, NT, NE])

        pG = [bank(f"pG{i}") for i in range(2)]
        pS = [bank(f"pS{i}") for i in range(4)]
        pO = [bank(f"pO{i}") for i in range(2)]

        loaded = st.lasting("loaded")
        w_split = st.lasting("w_split")
        w_lo_done = st.lasting("w_lo_done")
        zeros = st.lasting("zeros")
        fills = st.lasting("fills")
        x_in = sem("x_in")
        x_t_in = sem("x_t_in")
        ln_step = sem("ln_step")
        root = sem("root")
        xm_out = sem("xm_out")
        xT_done = sem("xT_done")
        xT_hi_done = sem("xT_hi_done")
        xT_lo_done = sem("xT_lo_done")
        lg_done = sem("lg_done")
        gate_step = sem("gate_step")
        gate_exp = sem("gate_exp")
        v_done = sem("v_done")
        v_hi_done = sem("v_hi_done")
        v_lo_done = sem("v_lo_done")
        pj_done = sem("pj_done")
        neg_done = sem("neg_done")
        ex_done = sem("ex_done")
        feat_done = sem("feat_done")
        q_hi_done = sem("q_hi_done")
        q_lo_done = sem("q_lo_done")
        kz_hi_done = sem("kz_hi_done")
        kz_lo_done = sem("kz_lo_done")
        a_done = sem("a_done")
        a_hi_done = sem("a_hi_done")
        a_lo_done = sem("a_lo_done")
        mask_hi_done = sem("mask_hi_done")
        mask_lo_done = sem("mask_lo_done")
        nums_out = sem("nums_out")
        lg_ready = sem("lg_ready")
        pv_done = sem("pv_done")
        den_done = sem("den_done")
        inv_done = sem("inv_done")
        o_done = sem("o_done")
        o_split = sem("o_split")
        y_done = sem("y_done")
        out_done = sem("out_done")
        stored = st.lasting("stored")

        NJ = H1 * NT
        START = [0, P, 2 * P, 2 * P]
        def width(t):
            return S - START[t]

        def masked(j):
            if j % NT == NT - 1:
                return slice(0, 2 * P), mask[:, 0:2 * P]
            return slice(0, P), mask[:, P:2 * P]

        AT_NORM = 20
        AT_TRANSPOSE = 30
        AT_PROJECT = (40, 44, 48, 56)

        with nc.Block() as block:
            @block.sync
            def _(sp):
                for n, (src, _) in names.items():
                    sp.dma_start(raw[n][:], src).then_inc(loaded, 16)
                for dst, src in ((ident, ident_d), (own8, own8_d), (mask, mask_d), (bg_row, bg)):
                    sp.dma_start(dst[:], src).then_inc(loaded, 16)
                sp.dma_start(before[:], before_d).then_inc(loaded, 16)
                sp.dma_start(x_new[:], tokens(x1, 0)).then_inc(x_in, 16)
                sp.wait_ge(ln_step, LN_ALL)
                sp.dma_start(tokens(xm_d, 0), xm[:]).then_inc(xm_out, 16)
                sp.wait_ge(xm_out, 16)
                st.lead(sp)
                sp.sem_inc(stored, 16)
                with sp.Fori(0, B) as b:
                    sp.wait_ge(stored, 16)
                    sp.sem_clear(stored)
                    sp.dma_start(x_new[:], tokens(x1, b + 1)).then_inc(x_in, 16)
                    sp.dma_start(x_t[:], tokens(x1, b)).then_inc(x_t_in, 16)
                    sp.wait_ge(gate_step, 10)
                    sp.dma_start(tokens(sel_d, b), sel[:]).then_inc(xm_out, 16)
                    sp.wait_ge(ln_step, LN_ALL)
                    sp.dma_start(tokens(xm_d, b + 1), xm[:]).then_inc(xm_out, 16)
                    sp.wait_ge(out_done, 2)
                    sp.dma_start(tokens(x2, b), x_out[:]).then_inc(stored, 16)
                    sp.wait_ge(xm_out, 32)
                    st.lead(sp)
                sp.wait_ge(stored, 16)

            @block.tensor
            def _(pe):
                def transposes():
                    pe.wait_ge(ln_step, LN_ALL)
                    for c in range(KC):
                        for t in range(NT):
                            last = nc.tensor.transpose(pG[c][:, t * P:(t + 1) * P],
                                                       xm[:, t, c * P:(c + 1) * P], ident[:])
                        last.then_inc(xT_done, 1)

                def project(i):
                    w = "q" if i < NC1 else "k"
                    pe.wait_ge(xT_lo_done, KC)
                    if i >= 2:
                        pe.wait_ge(feat_done, i - 1)
                    for c in range(KC):
                        cols = slice(c * D + (i % NC1) * P, c * D + (i % NC1 + 1) * P)
                        last = product(nc, pG[i % 2][:], w_hi[w][:, cols], w_lo[w][:, cols],
                                       xT_hi[:, c, :], xT_lo[:, c, :], c == 0, c == KC - 1)
                    last.then_inc(pj_done, 1)

                def logits_and_values():
                    pe.wait_ge(feat_done, 2 * NC1)
                    for t in range(NT):
                        ts = slice(t * P, (t + 1) * P)
                        for c in range(KC):
                            last = product(nc, pG[0][:, 8 * t:8 * t + 8], xT_hi[:, c, ts], xT_lo[:, c, ts],
                                           w_hi["g"][:, c * NE:(c + 1) * NE], w_lo["g"][:, c * NE:(c + 1) * NE],
                                           c == 0, c == KC - 1)
                    last.then_inc(lg_done, 1)
                    for t in range(NT):
                        ts = slice(t * P, (t + 1) * P)
                        if t == 1:
                            pe.wait_ge(lg_ready, 1)
                        if t >= 2:
                            pe.wait_ge(v_lo_done, t - 1)
                        for c in range(KC):
                            last = product(nc, pG[(t + 1) % 2][:, 0:D], xT_hi[:, c, ts], xT_lo[:, c, ts],
                                           w_hi["v"][:, c * D:(c + 1) * D], w_lo["v"][:, c * D:(c + 1) * D],
                                           c == 0, c == KC - 1)
                        last.then_inc(v_done, 1)

                def products(j):
                    h, t = j // NT, j % NT
                    c, w = h // 8, width(t)
                    ks, qs = slice(t * P, (t + 1) * P), slice(START[t], S)
                    if t == 0 and h >= 2:
                        pe.wait_ge(kz_lo_done, h - 1)
                    if j >= 4:
                        pe.wait_ge(a_lo_done, j - 3)
                    product(nc, pS[j % 4][:, 0:w], kz_hi[:, h % 3, ks], kz_lo[:, h % 3, ks], q_hi[:, c, qs],
                            q_lo[:, c, qs], True, True).then_inc(a_done, 1)

                def weigh(j):
                    h, t = j // NT, j % NT
                    g, i, w = h // 4, h % 4, width(t)
                    if h % 4 == 0 and t == 0 and g >= 2:
                        pe.wait_ge(den_done, g - 1)
                        pe.wait_ge(nums_out, g - 1)
                    pe.wait_ge(mask_hi_done, j + 1)
                    pe.wait_ge(mask_lo_done, j + 1)
                    first, final = i == 0 and t == 0, i == 3 and t == NT - 1
                    cols = slice(i * P, (i + 1) * P)
                    product(nc, pO[g % 2][:, START[t]:S], v_hi[:, t, g, cols], v_lo[:, t, g, cols],
                            a_hi[:, j % RA, 0:w], a_lo[:, j % RA, 0:w], first, final).then_inc(pv_done, 1)

                pe.wait_ge(fills, NT)
                pe.wait_ge(w_lo_done, len(names))
                transposes()
                for i in range(2 * NC1):
                    project(i)
                logits_and_values()
                pe.wait_ge(v_done, NT)
                st.meet(pe, PE)
                with pe.Fori(0, B) as b:
                    for j in range(NJ + 3):
                        if j < NJ:
                            products(j)
                        if j >= 3:
                            weigh(j - 3)
                        if j == AT_TRANSPOSE:
                            transposes()
                        if j in AT_PROJECT:
                            project(AT_PROJECT.index(j))
                    logits_and_values()
                    pe.wait_ge(a_lo_done, NJ)
                    for t in range(NT):
                        ts = slice(t * P, (t + 1) * P)
                        for c in range(NC1):
                            if t == 0:
                                pe.wait_ge(o_split, 2 * c + 2)
                            last = product(nc, pS[t // 2][:, (t % 2) * D:(t % 2 + 1) * D], o_hi[:, c, ts],
                                           o_lo[:, c, ts], w_hi["o"][:, c * D:(c + 1) * D],
                                           w_lo["o"][:, c * D:(c + 1) * D], c == 0, c == NC1 - 1)
                        if t % 2:
                            last.then_inc(y_done, 1)
                    pe.wait_ge(y_done, 2)
                    st.meet(pe, PE)

            @block.vector
            def _(dve):
                for i, n in enumerate(names):
                    dve.wait_ge(w_split, i + 1)
                    nc.vector.tensor_tensor(w_lo[n][:], raw[n][:], w_hi[n][:],
                                            ALU.subtract).then_inc(w_lo_done, 1)

                def norm():
                    dve.wait_ge(x_in, 16)
                    layer_norm(nc, dve, x_new, xm, stats, mean_var, small[:, 0, :], small[:, 1, :],
                               small[:, 2, :], small[:, 3, :], None, (ln_step, 0), (root, 1))

                def x_low():
                    for c in range(KC):
                        dve.wait_ge(xT_hi_done, c + 1)
                        nc.vector.tensor_tensor(xT_lo[:, c, :], pG[c][:], xT_hi[:, c, :],
                                                ALU.subtract).then_inc(xT_lo_done, 1)

                def features(i):
                    dve.wait_ge(pj_done, i + 1)
                    nc.vector.tensor_scalar(neg[:, i % 2, :], pG[i % 2][:], 0.0, None, ALU.min).then_inc(neg_done, 1)
                    dve.wait_ge(ex_done, i + 1)
                    nc.vector.scalar_tensor_tensor(out=feat[:, i, :], in0=pG[i % 2][:], scalar=0.0,
                                                   in1=ex[:, i % 2, :], op0=ALU.max,
                                                   op1=ALU.add).then_inc(feat_done, 1)

                def logits_and_values_low():
                    dve.wait_ge(lg_done, 1)
                    for t in range(NT):
                        last = nc.vector.tensor_tensor(lg[:, t, :], pG[0][:, 8 * t:8 * t + 8], bg_row[:], ALU.add)
                    last.then_inc(lg_ready, 1)
                    for t in range(NT):
                        dve.wait_ge(v_hi_done, t + 1)
                        blocks = lambda v: v[:, t, :, :].rearrange("p g (j c) -> p g j c", c=P + DE)[:, :, :, 0:DE]
                        nc.vector.tensor_tensor(blocks(v_lo),
                                                pG[(t + 1) % 2][:, 0:D].rearrange("p (g j c) -> p g j c", j=4, c=DE),
                                                blocks(v_hi), ALU.subtract).then_inc(v_lo_done, 1)

                def k_low(h, n):
                    dve.wait_ge(kz_hi_done, n + 1)
                    nc.vector.scalar_tensor_tensor(out=kz_lo[:, h % 3, :], in0=feat[:, NC1 + h // 8, :],
                                                   scalar=own8[:, h % 8:h % 8 + 1], in1=kz_hi[:, h % 3, :],
                                                   op0=ALU.mult, op1=ALU.subtract).then_inc(kz_lo_done, 1)

                def low(j):
                    w = width(j % NT)
                    dve.wait_ge(a_hi_done, j + 1)
                    nc.vector.tensor_tensor(a_lo[:, j % RA, 0:w], pS[j % 4][:, 0:w], a_hi[:, j % RA, 0:w],
                                            ALU.subtract).then_inc(a_lo_done, 1)
                    cut, m = masked(j)
                    dve.wait_ge(a_lo_done, j + 1)
                    nc.vector.tensor_tensor(a_lo[:, j % RA, cut], a_lo[:, j % RA, cut], m,
                                            ALU.mult).then_inc(mask_lo_done, 1)

                def denominators(g):
                    rows = slice(64 * (g % 2), 64 * (g % 2) + 64)
                    dve.wait_ge(pv_done, 4 * NT * (g + 1))
                    nc.vector.tensor_scalar(den[rows, :], pO[g % 2][64:128, :], 1e-6, None,
                                            ALU.max).then_inc(den_done, 1)

                def quotients(c):
                    dve.wait_ge(den_done, 2 * c + 2)
                    nc.vector.reciprocal(inv[:], den[:]).then_inc(inv_done, 1)
                    dve.wait_ge(inv_done, c + 1)
                    dve.wait_ge(nums_out, 2 * c + 2)
                    nc.vector.tensor_tensor(o[:, c, :], o[:, c, :], inv[:], ALU.mult).then_inc(o_done, 1)

                def step(n, ins):
                    ins.then_inc(gate_step, 1)
                    dve.wait_ge(gate_step, n)

                def over(m, shape):
                    return m[:].unsqueeze(2).to_broadcast(shape)

                def choose():
                    by_e = [P, NT, NE]
                    step(1, nc.vector.tensor_reduce(top[:], lg[:], AX.X, ALU.max))
                    step(2, nc.vector.tensor_tensor(lg[:], lg[:], over(top, by_e), ALU.subtract))
                    dve.wait_ge(gate_exp, 1)
                    step(3, nc.vector.tensor_reduce(tot[:], gate[:], AX.X, ALU.add))
                    step(4, nc.vector.reciprocal(tot[:], tot[:]))
                    step(5, nc.vector.tensor_tensor(gate[:], gate[:], over(tot, by_e), ALU.mult))
                    for t in range(NT):
                        mine = gate[:, t, :].unsqueeze(2).to_broadcast([P, NE, NE])
                        others = gate[:, t, :].unsqueeze(1).to_broadcast([P, NE, NE])
                        es = slice(NE * t, NE * t + NE)
                        nc.vector.tensor_tensor(more[:, es, :], others, mine, ALU.is_gt)
                        last = nc.vector.tensor_tensor(same[:, es, :], others, mine, ALU.is_equal)
                    step(6, last)
                    for t in range(NT):
                        es = slice(NE * t, NE * t + NE)
                        last = nc.vector.tensor_tensor(same[:, es, :], same[:, es, :], before[:], ALU.mult)
                    step(7, last)
                    step(8, nc.vector.tensor_tensor(more[:], more[:], same[:], ALU.add))
                    step(9, nc.vector.tensor_reduce(rank[:].rearrange("p t e -> p (t e)"), more[:], AX.X, ALU.add))
                    step(10, nc.vector.tensor_scalar(sel[:], rank[:], 1.5, None, ALU.is_lt))

                norm()
                x_low()
                for i in range(2 * NC1):
                    features(i)
                logits_and_values_low()
                k_low(0, 0)
                k_low(1, 1)
                dve.wait_ge(v_lo_done, NT)
                dve.wait_ge(lg_ready, 1)
                dve.wait_ge(kz_lo_done, 2)
                st.meet(dve, DVE)
                with dve.Fori(0, B) as b:
                    for j in range(NJ):
                        low(j)
                        if j % NT == 1 and j // NT + 2 < H1:
                            k_low(j // NT + 2, j // NT)
                        if j == 4:
                            choose()
                        if j == AT_NORM:
                            norm()
                        if j == AT_TRANSPOSE + 1:
                            x_low()
                        if j - 1 in AT_PROJECT:
                            features(AT_PROJECT.index(j - 1))
                        if j >= 4 * NT + 4 and (j - 4) % (4 * NT) == 0:
                            denominators((j - 4) // (4 * NT) - 1)
                        if j == 8 * NT + 5:
                            quotients(0)
                    denominators(3)
                    quotients(1)
                    logits_and_values_low()
                    k_low(0, H1 - 2)
                    k_low(1, H1 - 1)
                    dve.wait_ge(x_t_in, 16)
                    for i in range(2):
                        dve.wait_ge(y_done, i + 1)
                        nc.vector.tensor_tensor(x_out[:, 2 * i:2 * i + 2, :],
                                                pS[i][:].rearrange("p (t d) -> p t d", d=D),
                                                x_t[:, 2 * i:2 * i + 2, :], ALU.add).then_inc(out_done, 1)
                    dve.wait_ge(out_done, 2)
                    dve.wait_ge(kz_lo_done, H1)
                    dve.wait_ge(v_lo_done, NT)
                    dve.wait_ge(mask_lo_done, NJ)
                    st.meet(dve, DVE)

            @block.scalar
            def _(act):
                act.wait_ge(loaded, 16 * (len(names) + 5))
                for n in names:
                    nc.scalar.copy(w_hi[n][:], raw[n][:]).then_inc(w_split, 1)

                def norm_root():
                    act.wait_ge(ln_step, LN_VAR)
                    nc.scalar.activation(small[:, 1, :], small[:, 0, :], ACT.Sqrt).then_inc(root, 1)

                def x_high():
                    for c in range(KC):
                        act.wait_ge(xT_done, c + 1)
                        nc.scalar.copy(xT_hi[:, c, :], pG[c][:]).then_inc(xT_hi_done, 1)

                def exponential(i):
                    act.wait_ge(neg_done, i + 1)
                    nc.scalar.activation(ex[:, i % 2, :], neg[:, i % 2, :], ACT.Exp).then_inc(ex_done, 1)

                def q_high(a):
                    act.wait_ge(feat_done, NC1)
                    if a:
                        act.wait_ge(a_done, a)
                    for c in range(NC1):
                        nc.scalar.copy(q_hi[:, c, :], feat[:, c, :]).then_inc(q_hi_done, 1)

                def k_high(h, n, a=0):
                    if a:
                        act.wait_ge(a_done, a)
                    nc.scalar.activation(kz_hi[:, h % 3, :], feat[:, NC1 + h // 8, :], ACT.Copy,
                                         scale=own8[:, h % 8:h % 8 + 1]).then_inc(kz_hi_done, 1)

                def values_high(a):
                    if a:
                        act.wait_ge(pv_done, a)
                    for t in range(NT):
                        act.wait_ge(v_done, t + 1)
                        nc.scalar.copy(v_hi[:, t, :, :].rearrange("p g (j c) -> p g j c", c=P + DE)[:, :, :, 0:DE],
                                       pG[(t + 1) % 2][:, 0:D].rearrange("p (g j c) -> p g j c", j=4, c=DE)).then_inc(v_hi_done, 1)

                def numerators(g):
                    rows = slice(64 * (g % 2), 64 * (g % 2) + 64)
                    act.wait_ge(pv_done, 4 * NT * (g + 1))
                    nc.scalar.copy(o[rows, g // 2, :], pO[g % 2][0:64, :]).then_inc(nums_out, 1)

                norm_root()
                x_high()
                for i in range(2 * NC1):
                    exponential(i)
                q_high(0)
                act.wait_ge(feat_done, 2 * NC1)
                values_high(0)
                k_high(0, 0)
                k_high(1, 1)
                act.wait_ge(kz_hi_done, 2)
                act.wait_ge(v_hi_done, NT)
                act.wait_ge(q_hi_done, NC1)
                st.meet(act, ACTE)
                with act.Fori(0, B) as b:
                    for j in range(NJ):
                        h, t = j // NT, j % NT
                        w = width(t)
                        act.wait_ge(a_done, j + 1)
                        if j >= RA:
                            act.wait_ge(pv_done, j - RA + 1)
                        nc.scalar.copy(a_hi[:, j % RA, 0:w], pS[j % 4][:, 0:w]).then_inc(a_hi_done, 1)
                        if t == 1 and h + 2 < H1:
                            k_high(h + 2, h, NT * h if h >= 1 else 0)
                        if j == 4:
                            act.wait_ge(gate_step, 2)
                            nc.scalar.activation(gate[:], lg[:], ACT.Exp).then_inc(gate_exp, 1)
                        if j == AT_NORM:
                            norm_root()
                        if j == AT_TRANSPOSE + 1:
                            x_high()
                        if j - 1 in AT_PROJECT:
                            exponential(AT_PROJECT.index(j - 1))
                        if j >= 4 * NT + 4 and (j - 4) % (4 * NT) == 0:
                            numerators((j - 4) // (4 * NT) - 1)
                    q_high(NJ)
                    numerators(3)
                    act.wait_ge(feat_done, 2 * NC1)
                    values_high(NJ)
                    k_high(0, H1 - 2, NJ)
                    k_high(1, H1 - 1)
                    act.wait_ge(a_hi_done, NJ)
                    act.wait_ge(kz_hi_done, H1)
                    act.wait_ge(v_hi_done, NT)
                    st.meet(act, ACTE)

            @block.gpsimd
            def _(pool):
                for v in (v_hi, v_lo):
                    nc.gpsimd.memset(v[:].bitcast(F32), 0.0).then_inc(zeros, 1)
                pool.wait_ge(zeros, 2)
                for t in range(NT):
                    blocks = v_hi[:, t, :, :].rearrange("p g (j c) -> p g j c", c=P + DE)[:, :, :, 64:64 + DE]
                    nc.gpsimd.memset(blocks.bitcast(F32), 1.0).then_inc(fills, 1)
                pool.wait_ge(fills, NT)

                def q_low():
                    for c in range(NC1):
                        pool.wait_ge(q_hi_done, c + 1)
                        nc.gpsimd.tensor_tensor(q_lo[:, c, :], feat[:, c, :], q_hi[:, c, :],
                                                ALU.subtract).then_inc(q_lo_done, 1)

                def split_o(c):
                    pool.wait_ge(o_done, c + 1)
                    nc.gpsimd.tensor_copy(o_hi[:, c, :], o[:, c, :]).then_inc(o_split, 1)
                    pool.wait_ge(o_split, 2 * c + 1)
                    nc.gpsimd.tensor_tensor(o_lo[:, c, :], o[:, c, :], o_hi[:, c, :],
                                            ALU.subtract).then_inc(o_split, 1)

                q_low()
                pool.wait_ge(q_lo_done, NC1)
                st.meet(pool, POOL)
                with pool.Fori(0, B) as b:
                    for j in range(NJ):
                        pool.wait_ge(a_lo_done, j + 1)
                        cut, m = masked(j)
                        nc.gpsimd.tensor_tensor(a_hi[:, j % RA, cut], a_hi[:, j % RA, cut], m,
                                                ALU.mult).then_inc(mask_hi_done, 1)
                        if j == 8 * NT + 10:
                            split_o(0)
                    q_low()
                    split_o(1)
                    pool.wait_ge(o_split, 2 * NC1)
                    pool.wait_ge(q_lo_done, NC1)
                    pool.wait_ge(mask_hi_done, NJ)
                    st.meet(pool, POOL)




def stage_c(nc, w1, w2, b1, b2, thresholds_d, lower_d, ident_d, xm_d, x2, sel_d, rows, results, out):
    I32 = mybir.dt.int32
    with ExitStack() as ctx:
        st = Stage(nc, ctx, "c")
        sb, bank, sem = st.sb, st.bank, st.sem
        ident = sb("ident", [P, P])
        slot_a = sb("slot_a", [P, TT], I32)
        slot_b = sb("slot_b", [P, TT], I32)
        trips = sb("trips", [P, NE], I32)
        first = sb("first", [P, NE], I32)
        all_rows = sb("all_rows", [P, TT, D])

        raw1 = sb("raw1", [P, KC, FF])
        raw2 = sb("raw2", [P, MC, D])
        raw_b1 = sb("raw_b1", [P, MC])
        raw_b2 = sb("raw_b2", [P, D])
        w1_hi = [sb(f"w1_hi{i}", [P, KC, FF], F32R) for i in range(2)]
        w1_lo = [sb(f"w1_lo{i}", [P, KC, FF], F32R) for i in range(2)]
        w2_hi = [sb(f"w2_hi{i}", [P, MC, D], F32R) for i in range(2)]
        w2_lo = [sb(f"w2_lo{i}", [P, MC, D], F32R) for i in range(2)]
        b1_c = [sb(f"b1_c{i}", [P, MC]) for i in range(2)]
        b2_row = [sb(f"b2_row{i}", [P, D]) for i in range(2)]

        raw_in = st.lasting("raw_in")
        split_hi = st.lasting("split_hi")
        split_lo = st.lasting("split_lo")

        def load_weights(sp, e):
            sp.dma_start(raw1[:], w1[bass.ds(e, 1), :, :].rearrange("o (c p) f -> p (o c) f", p=P)).then_inc(raw_in, 16)
            sp.dma_start(raw2[:], w2[bass.ds(e, 1), :, :].rearrange("o (m p) d -> p (o m) d", p=P)).then_inc(raw_in, 16)
            sp.dma_start(raw_b1[:], b1[bass.ds(e, 1), :, :].rearrange("o p m -> p (o m)")).then_inc(raw_in, 16)
            sp.dma_start(raw_b2[:], b2[bass.ds(e, 1), :, :].rearrange("o p d -> p (o d)")).then_inc(raw_in, 16)

        loaded = st.lasting("loaded")
        rows_in = st.lasting("rows_in")
        filled = st.lasting("filled")
        counted = st.lasting("counted")
        slot_step = st.lasting("slot_step")
        ones_set = st.lasting("ones_set")
        scattered = st.lasting("scattered")

        with ExitStack() as ctx2:
            def tmp(name, shape, dt=F32):
                return ctx2.enter_context(nc.sbuf_tensor(f"c_{name}", shape, dt))
            lower = tmp("lower", [P, P])
            ones = tmp("ones", [P, P])
            thresholds = tmp("thresholds", [P, NE, MAX_TRIPS - 1])
            sel = tmp("sel", [P, TT, NE])
            tot = tmp("tot", [P, TT, NE])
            upto = tmp("upto", [P, TT, NE])
            unit = tmp("unit", [P, TT])
            slot = tmp("slot", [P, TT, NE])
            pick = tmp("pick", [P, TT, NE])
            near = tmp("near", [P, 2, TT])
            above = tmp("above", [P, NE, MAX_TRIPS - 1])
            n_trips = tmp("n_trips", [P, NE])
            trips_upto = tmp("trips_upto", [P, NE])
            e_base = tmp("e_base", [P, NE])
            p_in = ctx2.enter_context(nc.psum_tensor("c_p_in", [P, TT, NE], F32))
            p_tot = ctx2.enter_context(nc.psum_tensor("c_p_tot", [P, TT, NE], F32))
            FAR = float(1 << 20)
            with nc.Block() as block:
                @block.sync
                def _(sp):
                    for dst, src in ((ident, ident_d), (lower, lower_d), (thresholds, thresholds_d),
                                     (sel, sel_d.rearrange("(t p) e -> p t e", p=P))):
                        sp.dma_start(dst[:], src).then_inc(loaded, 16)
                    sp.dma_start(all_rows[:], xm_d[0:T, :].rearrange("(t p) d -> p t d", p=P)).then_inc(rows_in, 16)
                    load_weights(sp, 0)

                @block.scalar
                def _(act):
                    act.wait_ge(raw_in, 64)
                    for dst, src in ((w1_hi[0], raw1), (w2_hi[0], raw2), (b1_c[0], raw_b1), (b2_row[0], raw_b2)):
                        nc.scalar.copy(dst[:], src[:]).then_inc(split_hi, 1)
                    act.wait_ge(split_hi, 4)
                    act.sem_clear(raw_in)

                @block.tensor
                def _(pe):
                    pe.wait_ge(loaded, 64)
                    pe.wait_ge(ones_set, 1)
                    nc.tensor.matmul(p_in[:], lower[:], sel[:], start=True, stop=True).then_inc(counted, 1)
                    nc.tensor.matmul(p_tot[:], ones[:], sel[:], start=True, stop=True).then_inc(counted, 1)

                @block.vector
                def _(dve):
                    def step(n, ins):
                        ins.then_inc(slot_step, 1)
                        dve.wait_ge(slot_step, n)
                    step(1, nc.vector.memset(unit[:], 1.0))
                    dve.wait_ge(counted, 2)
                    step(2, nc.vector.tensor_copy(tot[:], p_tot[:]))
                    for e in range(NE):
                        last = nc.vector.tensor_tensor_scan(out=upto[:, :, e], data0=unit[:], data1=tot[:, :, e],
                                                            initial=0.0, op0=ALU.mult, op1=ALU.add)
                    step(3, last)
                    step(4, nc.vector.tensor_tensor(
                        above[:], upto[:, TT - 1, :].unsqueeze(2).to_broadcast([P, NE, MAX_TRIPS - 1]),
                        thresholds[:], ALU.is_gt))
                    step(5, nc.vector.tensor_reduce(n_trips[:], above[:], AX.X, ALU.add))
                    step(6, nc.vector.tensor_scalar(n_trips[:], n_trips[:], 1.0, None, ALU.add))
                    step(7, nc.vector.tensor_tensor_scan(out=trips_upto[:], data0=unit[:, 0:NE], data1=n_trips[:],
                                                         initial=0.0, op0=ALU.mult, op1=ALU.add))
                    step(8, nc.vector.tensor_tensor(e_base[:], trips_upto[:], n_trips[:], ALU.subtract))
                    nc.vector.tensor_copy(trips[:], n_trips[:])
                    step(9, nc.vector.tensor_copy(first[:], e_base[:]))
                    step(10, nc.vector.tensor_scalar(e_base[:], e_base[:], float(TILE), None, ALU.mult))
                    step(11, nc.vector.tensor_tensor(slot[:], upto[:], tot[:], ALU.subtract))
                    step(12, nc.vector.tensor_tensor(slot[:], slot[:], p_in[:], ALU.add))
                    step(13, nc.vector.tensor_tensor(slot[:], slot[:], e_base[:].unsqueeze(1).to_broadcast([P, TT, NE]),
                                                     ALU.add))
                    step(14, nc.vector.scalar_tensor_tensor(out=pick[:], in0=slot[:], scalar=-FAR, in1=sel[:],
                                                            op0=ALU.add, op1=ALU.mult))
                    step(15, nc.vector.tensor_reduce(near[:, 0, :], pick[:], AX.X, ALU.min))
                    step(16, nc.vector.tensor_scalar(slot_a[:], near[:, 0, :], FAR, None, ALU.add))
                    step(17, nc.vector.tensor_tensor(pick[:], slot[:], sel[:], ALU.mult))
                    step(18, nc.vector.tensor_reduce(near[:, 1, :], pick[:], AX.X, ALU.max))
                    step(19, nc.vector.tensor_copy(slot_b[:], near[:, 1, :]))
                    for i, (dst, src, hi) in enumerate(((w1_lo[0], raw1, w1_hi[0]), (w2_lo[0], raw2, w2_hi[0]))):
                        dve.wait_ge(split_hi, i + 1)
                        nc.vector.tensor_tensor(dst[:], src[:], hi[:], ALU.subtract).then_inc(split_lo, 1)
                    dve.wait_ge(split_lo, 2)

                @block.gpsimd
                def _(pool):
                    nc.gpsimd.memset(ones[:], 1.0).then_inc(ones_set, 1)
                    pool.wait_ge(slot_step, 19)
                    pool.wait_ge(rows_in, 16)
                    for t in range(TT):
                        for s in (slot_a, slot_b):
                            pool.indirect_dma_start(out=rows, out_offset=bass.IndirectOffsetOnAxis(ap=s[:, t:t + 1], axis=0),
                                                    in_=all_rows[:, t, :], in_offset=None).then_inc(scattered, 16)
                    pool.wait_ge(scattered, 32 * TT)

        x_t = sb("x_t", [P, NT, D])
        xT_hi = sb("xT_hi", [P, KC, S], F32R)
        xT_lo = sb("xT_lo", [P, KC, S], F32R)
        RH = 4
        h = sb("h", [P, RH, S])
        h_hi = sb("h_hi", [P, RH, S], F32R)
        h_lo = sb("h_lo", [P, RH, S], F32R)
        y = sb("y", [P, NT, D])
        pX = bank("pX")
        pU = [bank(f"pU{i}") for i in range(3)]
        pY = [bank(f"pY{i}", (P, D)) for i in range(NT)]

        w_split = st.lasting("w_split")
        w_ready = st.lasting("w_ready")
        pool_go = st.lasting("pool_go")
        stored = st.lasting("stored")
        x_in = sem("x_in")
        xT_done = sem("xT_done")
        xT_hi_done = sem("xT_hi_done")
        xT_lo_done = sem("xT_lo_done")
        up_done = sem("up_done")
        relu_done = sem("relu_done")
        h_lo_done = sem("h_lo_done")
        down_done = sem("down_done")
        y_done = sem("y_done")
        TILE_WORKERS = 3

        def per_expert(eng, run):
            with eng.Fori(0, NE // 2 - 1) as half:
                run(0, half * 2, True)
                run(1, half * 2 + 1, True)
            run(0, NE - 2, True)
            run(1, NE - 1, False)

        def tiles_of(eng, e):
            return eng.value_load(trips[0:1, bass.ds(e, 1)], min_val=1, max_val=MAX_TRIPS)

        with nc.Block() as block:
            @block.sync
            def _(sp):
                def load(at):
                    sp.dma_start(x_t[:], rows[bass.ds(at, TILE), :].rearrange("(t p) d -> p t d", p=P)).then_inc(x_in, 16)

                def run(parity, e, more):
                    if more:
                        load_weights(sp, e + 1)
                    start = sp.value_load(first[0:1, bass.ds(e, 1)], min_val=0, max_val=TILES - 1)
                    with sp.Fori(0, tiles_of(sp, e)) as i:
                        sp.wait_ge(stored, 16)
                        sp.sem_clear(stored)
                        at = nc.s_assert_le(start + i, TILES - 1) * TILE
                        load(at + TILE)
                        sp.wait_ge(y_done, NT)
                        sp.dma_start(results[bass.ds(at, TILE), :].rearrange("(t p) d -> p t d", p=P),
                                     y[:]).then_inc(stored, 16)
                        st.lead(sp, TILE_WORKERS)
                    if more:
                        sp.wait_ge(w_ready, 1)
                        sp.sem_clear(w_ready)
                        st.lead(sp, TILE_WORKERS)
                        sp.sem_inc(pool_go, 1)

                load(0)
                st.lead(sp, TILE_WORKERS)
                sp.sem_inc(stored, 16)
                per_expert(sp, run)
                sp.wait_ge(stored, 16)

            @block.tensor
            def _(pe):
                def transpose(c):
                    if c:
                        pe.wait_ge(xT_lo_done, 1)
                    else:
                        pe.wait_ge(x_in, 16)
                    for t in range(NT):
                        last = nc.tensor.transpose(pX[:, t * P:(t + 1) * P], x_t[:, t, c * P:(c + 1) * P], ident[:])
                    last.then_inc(xT_done, 1)

                def up(w, m):
                    if m >= 3:
                        pe.wait_ge(relu_done, 2 * (m - 2))
                    for c in range(KC):
                        cols = slice(m * P, (m + 1) * P)
                        last = product(nc, pU[m % 3][:], w1_hi[w][:, c, cols], w1_lo[w][:, c, cols], xT_hi[:, c, :],
                                       xT_lo[:, c, :], c == 0, c == KC - 1)
                    last.then_inc(up_done, 1)

                def down(w, m):
                    pe.wait_ge(h_lo_done, m + 1)
                    for t in range(NT):
                        ts = slice(t * P, (t + 1) * P)
                        last = product(nc, pY[t][:], h_hi[:, m % RH, ts], h_lo[:, m % RH, ts], w2_hi[w][:, m, :],
                                       w2_lo[w][:, m, :], m == 0, m == MC - 1)
                    last.then_inc(down_done, 1)

                def run(parity, e, more):
                    with pe.Fori(0, tiles_of(pe, e)):
                        for m in range(MC):
                            up(parity, m)
                            if m >= 2:
                                down(parity, m - 2)
                        transpose(0)
                        down(parity, MC - 2)
                        transpose(1)
                        down(parity, MC - 1)
                        pe.wait_ge(down_done, MC)
                        st.meet(pe, PE)
                    if more:
                        st.meet(pe, PE)

                transpose(0)
                transpose(1)
                st.meet(pe, PE)
                per_expert(pe, run)

            @block.scalar
            def _(act):
                def x_high():
                    for c in range(KC):
                        act.wait_ge(xT_done, c + 1)
                        nc.scalar.copy(xT_hi[:, c, :], pX[:]).then_inc(xT_hi_done, 1)

                def run(parity, e, more):
                    with act.Fori(0, tiles_of(act, e)):
                        for m in range(MC):
                            act.wait_ge(up_done, m + 1)
                            if m >= RH:
                                act.wait_ge(down_done, m - RH + 1)
                            for dst in (h, h_hi):
                                nc.scalar.activation(dst[:, m % RH, :], pU[m % 3][:], ACT.Relu,
                                                     bias=b1_c[parity][:, m:m + 1]).then_inc(relu_done, 1)
                        x_high()
                        act.wait_ge(relu_done, 2 * MC)
                        act.wait_ge(xT_hi_done, KC)
                        st.meet(act, ACTE)
                    if more:
                        st.meet(act, ACTE)

                x_high()
                act.wait_ge(xT_hi_done, KC)
                st.meet(act, ACTE)
                per_expert(act, run)

            @block.vector
            def _(dve):
                def x_low():
                    for c in range(KC):
                        dve.wait_ge(xT_hi_done, c + 1)
                        nc.vector.tensor_tensor(xT_lo[:, c, :], pX[:], xT_hi[:, c, :],
                                                ALU.subtract).then_inc(xT_lo_done, 1)

                def run(parity, e, more):
                    with dve.Fori(0, tiles_of(dve, e)):
                        for m in range(MC):
                            dve.wait_ge(relu_done, 2 * m + 2)
                            if m >= RH:
                                dve.wait_ge(down_done, m - RH + 1)
                            nc.vector.tensor_tensor(h_lo[:, m % RH, :], h[:, m % RH, :], h_hi[:, m % RH, :],
                                                    ALU.subtract).then_inc(h_lo_done, 1)
                        x_low()
                        dve.wait_ge(down_done, MC)
                        for t in range(NT):
                            nc.vector.tensor_tensor(y[:, t, :], pY[t][:], b2_row[parity][:], ALU.add).then_inc(y_done, 1)
                        dve.wait_ge(y_done, NT)
                        dve.wait_ge(xT_lo_done, KC)
                        st.meet(dve, DVE)
                    if more:
                        st.meet(dve, DVE)

                x_low()
                dve.wait_ge(xT_lo_done, KC)
                st.meet(dve, DVE)
                per_expert(dve, run)

            @block.gpsimd
            def _(pool):
                def run(parity, e, more):
                    if not more:
                        return
                    w = 1 - parity
                    pool.wait_ge(raw_in, 64)
                    pool.sem_clear(raw_in)
                    for dst, src in ((w1_hi[w], raw1), (w2_hi[w], raw2), (b1_c[w], raw_b1), (b2_row[w], raw_b2)):
                        nc.gpsimd.tensor_copy(dst[:], src[:]).then_inc(w_split, 1)
                    for i, (dst, src, hi) in enumerate(((w1_lo[w], raw1, w1_hi[w]), (w2_lo[w], raw2, w2_hi[w]))):
                        pool.wait_ge(w_split, 4)
                        nc.gpsimd.tensor_tensor(dst[:], src[:], hi[:], ALU.subtract).then_inc(w_split, 1)
                    pool.wait_ge(w_split, 6)
                    pool.sem_clear(w_split)
                    pool.sem_inc(w_ready, 1)
                    pool.wait_ge(pool_go, 1)
                    pool.sem_clear(pool_go)

                per_expert(pool, run)

        with ExitStack() as ctx2:
            RG = 4
            ya = ctx2.enter_context(nc.sbuf_tensor("c_ya", [P, RG, D], F32))
            yb = ctx2.enter_context(nc.sbuf_tensor("c_yb", [P, RG, D], F32))
            x2_in = st.lasting("x2_in")
            ya_in = [st.lasting(f"ya_in{i}") for i in range(RG)]
            yb_in = [st.lasting(f"yb_in{i}") for i in range(RG)]
            added = st.lasting("added")
            out_stored = st.lasting("out_stored")
            with nc.Block() as block:
                @block.sync
                def _(sp):
                    sp.dma_start(all_rows[:], x2.rearrange("(t p) d -> p t d", p=P)).then_inc(x2_in, 16)
                    for i in range(TT // NT):
                        sp.wait_ge(added, 2 * NT * (i + 1))
                        sp.dma_start(tokens(out, i), all_rows[:, NT * i:NT * i + NT, :]).then_inc(out_stored, 16)
                    sp.wait_ge(out_stored, 16 * (TT // NT))

                @block.gpsimd
                def _(pool):
                    for t in range(TT):
                        if t >= RG:
                            pool.wait_ge(added, 2 * (t - RG + 1))
                        for dst, s, done in ((ya, slot_a, ya_in), (yb, slot_b, yb_in)):
                            pool.indirect_dma_start(out=dst[:, t % RG, :], out_offset=None, in_=results,
                                                    in_offset=bass.IndirectOffsetOnAxis(ap=s[:, t:t + 1], axis=0)
                                                    ).then_inc(done[t % RG], 16)

                @block.vector
                def _(dve):
                    dve.wait_ge(x2_in, 16)
                    for t in range(TT):
                        for k, (src, done) in enumerate(((ya, ya_in), (yb, yb_in))):
                            dve.wait_ge(done[t % RG], 16 * (t // RG + 1))
                            if k:
                                dve.wait_ge(added, 2 * t + 1)
                            nc.vector.tensor_tensor(all_rows[:, t, :], all_rows[:, t, :], src[:, t % RG, :],
                                                    ALU.add).then_inc(added, 1)


def rope_tables():
    inv_freq = 1.0 / 10000.0 ** (np.arange(0, DH, 2, dtype=np.float32) / DH)
    freqs = np.outer(np.arange(S, dtype=np.float32), inv_freq)[:, (2 * np.arange(32)) % 32].T
    c, s = np.cos(freqs), np.sin(freqs)
    return (np.ascontiguousarray(np.concatenate([c, c, c, c])).astype(np.float32),
            np.ascontiguousarray(np.concatenate([-s, -s, s, s])).astype(np.float32))


def lay_out(a):
    even, odd = np.arange(0, DH, 2), np.arange(1, DH, 2)
    of_pair = lambda f: np.concatenate([f, DH + f])
    rows = (2 * DH * np.arange(NP)[:, None] + np.concatenate([of_pair(even), of_pair(odd), of_pair(even)])[None]).ravel()
    by_chunk = lambda m: m.reshape(-1, P, m.shape[-1]).transpose(1, 0, 2).reshape(P, -1)
    down = np.stack([a["L0_attn_w_down_q"], a["L0_attn_w_down_kv"]])
    cos, sin = rope_tables()
    return {
        "x": a["L0_attn_x"].reshape(T, D),
        "w1_rows": a["L0_ffn_w1"],
        "w1_t": a["L0_ffn_w1"].T,
        "w2_t": a["L0_ffn_w2"].T,
        "b1": a["L0_ffn_b1"].reshape(MC, P).T,
        "b2": np.broadcast_to(a["L0_ffn_b2"], (P, D)),
        "ident_d": np.eye(P, dtype=np.float32),
        "wd_t": down.reshape(2, P, KC, P).transpose(3, 2, 0, 1).reshape(P, -1),
        "wq_t": a["L0_attn_w_up_q"][rows].T,
        "wk_t": a["L0_attn_w_up_k"][rows].T,
        "wv_t": a["L0_attn_w_up_v"].T,
        "wo_t": by_chunk(a["L0_attn_w_out"].T),
        "ln_sb": np.stack([a["L0_attn_ln_scale"].reshape(KC, P), a["L0_attn_ln_bias"].reshape(KC, P)]).transpose(2, 0, 1),
        "rope_c": cos,
        "rope_s": sin,
        "own_d": np.ascontiguousarray(np.tile(np.repeat(np.eye(2, dtype=np.float32), 32, axis=0), (2, 1))),
        "l1_wq": by_chunk(a["L1_attn_Wq"].T),
        "l1_wk": by_chunk(a["L1_attn_Wk"].T),
        "l1_wv": by_chunk(a["L1_attn_Wv"].T),
        "l1_wo": by_chunk(a["L1_attn_Wo"].T),
        "wg": by_chunk(a["L1_ffn_Wg"]),
        "bg": np.broadcast_to(a["L1_ffn_bg"], (P, NE)),
        "own8_d": np.repeat(np.eye(8, dtype=np.float32), DE, axis=0),
        "mask_d": np.concatenate([np.zeros((P, P)), np.triu(np.ones((P, P))), np.ones((P, 3 * P))], 1).astype(np.float32),
        "e_w1": a["L1_ffn_W1"],
        "e_w2": a["L1_ffn_W2"],
        "e_b1": a["L1_ffn_b1"].reshape(NE, MC, P).transpose(0, 2, 1),
        "e_b2": np.broadcast_to(a["L1_ffn_b2"][:, None, :], (NE, P, D)),
        "thresholds": np.broadcast_to(TILE * np.arange(1, MAX_TRIPS, dtype=np.float32), (P, NE, MAX_TRIPS - 1)),
        "lower_d": np.triu(np.ones((P, P), np.float32), 1),
        "before_d": np.broadcast_to(np.tril(np.ones((NE, NE)), -1).astype(np.float32), (P, NE, NE)),
    }


STAGES = (
    (stage_f, ("x", "w1_rows", "w1_t", "w2_t", "b1", "b2", "wd_t", "ln_sb", "ident_d"),
     ("part", "latents", "rows", "results")),
    (stage_a, ("wq_t", "wk_t", "wv_t", "wo_t", "rope_c", "rope_s", "own_d", "ident_d"),
     ("part", "latents", "x1")),
    (stage_b, ("l1_wq", "l1_wk", "l1_wv", "l1_wo", "wg", "bg", "own8_d", "mask_d", "before_d", "ident_d"),
     ("x1", "xm", "x2", "sel")),
    (stage_c, ("e_w1", "e_w2", "e_b1", "e_b2", "thresholds", "lower_d", "ident_d"),
     ("xm", "x2", "sel", "rows", "results", "out")),
)
SCRATCH = {"part": (T, D), "x1": (T + S, D), "xm": (T + S, D), "x2": (T, D), "sel": (T, NE),
           "latents": ((B + 1) * P, 4 * S), "rows": ((TILES + 1) * TILE, D), "results": (TILES * TILE, D)}


def program(nc, aps):
    for stage, inputs, between in STAGES:
        stage(nc, *(aps[n] for n in inputs + between))


def kernel(**inputs):
    import concourse.bacc as bacc
    from concourse.bass_utils import run_bass_kernel_spmd

    arrays = {n: np.ascontiguousarray(v) for n, v in lay_out({k: np.asarray(v) for k, v in inputs.items()}).items()}
    nc = bacc.Bacc("TRN2", target_bir_lowering=False, num_devices=1)
    aps = {n: nc.dram_tensor(f"in_{n}", a.shape, F32, kind="ExternalInput").ap() for n, a in arrays.items()}
    for n, shape in SCRATCH.items():
        aps[n] = nc.dram_tensor(f"mid_{n}", shape, F32, kind="Internal").ap()
    aps["out"] = nc.dram_tensor("out_x", (T, D), F32, kind="ExternalOutput").ap()
    program(nc, aps)
    result = run_bass_kernel_spmd(nc, [{f"in_{n}": a for n, a in arrays.items()}], core_ids=[0])
    return result.results[0]["out_x"].reshape(B, S, D)
```
